# Optimizing a Trainium2 kernel written in Bass

```python
import numpy as np
import jax
import jax.numpy as jnp

def _softmax(x, axis=-1):
    return jax.nn.softmax(x, axis=axis)

def _gelu(x):
    return jax.nn.gelu(x, approximate=True)

def _silu(x):
    return jax.nn.silu(x)

def _sigmoid(x):
    return jax.nn.sigmoid(x)

def _layernorm(x, axis=-1, eps=1e-05):
    m = jnp.mean(x, axis=axis, keepdims=True)
    v = jnp.var(x, axis=axis, keepdims=True)
    return (x - m) / jnp.sqrt(v + eps)

def _scatter_add(tgt, idx, src, axis=0):
    return tgt.at[idx].add(src)

def _segment_sum(src, seg, n):
    return jax.ops.segment_sum(src, seg, n)
kernel_name = 'mk_adaln_attn_ffn_d1_seqx_r4_317c47'

def setup_inputs(seed: int=0):
    np.random.seed(seed)
    _w = jnp.asarray

    def _rec_inputs():
        import jax
        import jax.numpy as jnp
        _rk = jax.random.key(seed)
        x = -5.13e-06 + 0.01765 * jax.random.normal(jax.random.fold_in(_rk, 1), (16, 256, 256), jnp.float32)
        _lenS = 256 - jax.random.randint(jax.random.fold_in(_rk, 7), (16,), 0, max(1, 256 // 4) + 1, jnp.int32)
        _lenS2 = 256 - jax.random.randint(jax.random.fold_in(_rk, 8), (16,), 0, max(1, 256 // 4) + 1, jnp.int32)
        cond_1024 = 0.0061147 + 1.02565 * jax.random.normal(jax.random.fold_in(_rk, 11), (16, 256), jnp.float32)
        return (x, cond_1024)
    x, cond_1024 = _rec_inputs()

    def _L0_cond_setup():
        import math
        import jax, jax.numpy as jnp
        import numpy as np
        EPS = 1e-07
        MAX_TANH_ARG = 1.0 - 1e-05

        def _norm(x):
            return jnp.sqrt(jnp.sum(x * x, axis=-1, keepdims=True)).clip(EPS)

        def logmap0(x):
            n = _norm(x)
            return jnp.arctanh(jnp.clip(n, EPS, MAX_TANH_ARG)) * x / n

        def expmap0(v):
            n = _norm(v)
            return jnp.tanh(n) * v / n

        def mobius_add(x, y):
            x2 = jnp.sum(x * x, -1, keepdims=True)
            y2 = jnp.sum(y * y, -1, keepdims=True)
            xy = jnp.sum(x * y, -1, keepdims=True)
            num = (1 + 2 * xy + y2) * x + (1 - x2) * y
            den = (1 + 2 * xy + x2 * y2).clip(EPS)
            return num / den

        def plin(x, w, b):
            return expmap0(logmap0(x) @ w + b)

        def layer_norm(x, eps=1e-06):
            m = x.mean(-1, keepdims=True)
            v = ((x - m) ** 2).mean(-1, keepdims=True)
            return (x - m) / jnp.sqrt(v + eps)

        def _beta(a, b):
            return math.exp(math.lgamma(a) + math.lgamma(b) - math.lgamma(a + b))
        D, H, FF = (256, 16, 1024)
        HD = D // H
        BETA_N = _beta(D / 2, 0.5)
        BETA_H = _beta(HD / 2, 0.5)

        def _to_heads(p):
            B, S, _ = p.shape
            t = logmap0(p).reshape(B, S, H, HD) * (BETA_H / BETA_N)
            return expmap0(jnp.transpose(t, (0, 2, 1, 3)))

        def _from_heads(ph):
            B, _, S, _ = ph.shape
            t = logmap0(ph) * (BETA_N / BETA_H)
            t = jnp.transpose(t, (0, 2, 1, 3)).reshape(B, S, D)
            return expmap0(t)
        key = jax.random.key(seed)
        ks = jax.random.split(key, 20)
        B, S = (4, 256)
        x = expmap0(0.02 * jax.random.normal(ks[0], (B, S, D), jnp.float32))
        t_emb = jax.random.normal(ks[1], (B, 1, D), jnp.float32)
        g = lambda k, sh: 0.02 * jax.random.normal(k, sh, jnp.float32)
        return {'x': x, 't_emb': t_emb, 'w_q': g(ks[2], (D, D)), 'b_q': jnp.zeros((D,), jnp.float32), 'w_k': g(ks[3], (D, D)), 'b_k': jnp.zeros((D,), jnp.float32), 'w_v': g(ks[4], (D, D)), 'b_v': jnp.zeros((D,), jnp.float32), 'w_o': g(ks[5], (D, D)), 'b_o': jnp.zeros((D,), jnp.float32), 'w_f1': g(ks[6], (D, FF)), 'b_f1': jnp.zeros((FF,), jnp.float32), 'w_f2': g(ks[7], (FF, D)), 'b_f2': jnp.zeros((D,), jnp.float32), 'w_ada': g(ks[8], (D, 6 * D)), 'b_ada': jnp.zeros((6 * D,), jnp.float32)}
    _L0_cond_all = _L0_cond_setup()
    _L0_cond_in = {k: v for k, v in _L0_cond_all.items() if k in ('w_q', 'b_q', 'w_k', 'b_k', 'w_v', 'b_v', 'w_o', 'b_o', 'w_f1', 'b_f1', 'w_f2', 'b_f2', 'w_ada', 'b_ada')}
    del _L0_cond_all

    def _L0_attn_setup():
        import jax, jax.numpy as jnp
        import numpy as np
        D_MODEL = 256
        N_HEADS = 16
        LATENT_HEADS = 8
        LATENT_DIM = 128
        N_LATENTS = 64
        WINDOW = 64
        HEAD_DIM = D_MODEL // N_HEADS
        LAT_HD = LATENT_DIM // LATENT_HEADS
        B, S = (2, 1024)

        def _pool_to_latents(x):
            Bx, Sx, C = x.shape
            chunk = max(1, Sx // N_LATENTS)
            return x.reshape(Bx, N_LATENTS, chunk, C).mean(axis=2)

        def _local_window_attn(Q, K, V):
            Bx, H, Sx, D = Q.shape
            W = WINDOW
            nb = Sx // W
            Qb = Q.reshape(Bx, H, nb, W, D)
            Kp = jnp.pad(K, ((0, 0), (0, 0), (W, 0), (0, 0))).reshape(Bx, H, nb + 1, W, D)
            Vp = jnp.pad(V, ((0, 0), (0, 0), (W, 0), (0, 0))).reshape(Bx, H, nb + 1, W, D)
            Kw = jnp.concatenate([Kp[:, :, :-1], Kp[:, :, 1:]], axis=3)
            Vw = jnp.concatenate([Vp[:, :, :-1], Vp[:, :, 1:]], axis=3)
            i = jnp.arange(W)[:, None]
            j = jnp.arange(2 * W)[None, :]
            base = (j > i) & (j <= i + W)
            blk0 = (jnp.arange(nb) > 0)[:, None, None] | (j >= W)[None, :, :]
            mask = base[None, :, :] & blk0
            sc = jnp.einsum('bhnid,bhnjd->bhnij', Qb, Kw) / np.sqrt(D).astype(np.float32)
            sc = jnp.where(mask[None, None], sc, -jnp.inf)
            p = jax.nn.softmax(sc, axis=-1)
            out = jnp.einsum('bhnij,bhnjd->bhnid', p, Vw)
            return out.reshape(Bx, H, Sx, D)
        key = jax.random.key(seed)
        ks = jax.random.split(key, 11)
        std = 0.02
        w = lambda k, shp: jax.random.normal(k, shp, jnp.float32) * std
        return {'x': jax.random.normal(ks[0], (B, S, D_MODEL), jnp.float32), 'wq': w(ks[1], (D_MODEL, D_MODEL)), 'wk': w(ks[2], (D_MODEL, D_MODEL)), 'wv': w(ks[3], (D_MODEL, D_MODEL)), 'wgq': w(ks[4], (D_MODEL, LATENT_DIM)), 'wgk': w(ks[5], (D_MODEL, LATENT_DIM)), 'wgv': w(ks[6], (D_MODEL, LATENT_DIM)), 'r_out_w': w(ks[7], (LATENT_DIM, D_MODEL)), 'gate_local_w': w(ks[8], (N_HEADS, HEAD_DIM)), 'gate_remote_w': w(ks[9], (N_HEADS, HEAD_DIM)), 'w_out': w(ks[10], (D_MODEL, D_MODEL))}
    _L0_attn_all = _L0_attn_setup()
    _L0_attn_in = {k: v for k, v in _L0_attn_all.items() if k in ('wq', 'wk', 'wv', 'wgq', 'wgk', 'wgv', 'r_out_w', 'gate_local_w', 'gate_remote_w', 'w_out')}
    del _L0_attn_all

    def _L0_cond2_setup():
        import jax, jax.numpy as jnp
        import numpy as np
        IN_FEATURES = 256
        OUT_FEATURES = 256
        BATCH = 32
        SEQ = 256
        EPS = 1e-08
        key = jax.random.key(seed)
        k1, k2, k3 = jax.random.split(key, 3)
        Efou = jax.random.normal(k1, (BATCH, SEQ, IN_FEATURES), dtype=jnp.float32)
        y = jax.random.normal(k2, (BATCH, IN_FEATURES), dtype=jnp.float32)
        weight = jax.random.normal(k3, (IN_FEATURES, OUT_FEATURES), dtype=jnp.float32)
        return {'Efou': Efou, 'y': y, 'weight': weight}
    _L0_cond2_all = _L0_cond2_setup()
    _L0_cond2_in = {k: v for k, v in _L0_cond2_all.items() if k in ('weight',)}
    del _L0_cond2_all

    def _L0_ffn_setup():
        import jax, jax.numpy as jnp
        import numpy as np
        TOP_K = 2
        key = jax.random.key(seed)
        ks = jax.random.split(key, 7)
        B_, S, D, F, E, R = (2, 512, 256, 1024, 4, 4)
        x = jax.random.normal(ks[0], (B_, S, D), dtype=jnp.float32)
        Wg = jax.random.normal(ks[1], (E, D), dtype=jnp.float32) * (1.0 / np.sqrt(D))
        bg = jnp.zeros((E,), dtype=jnp.float32)
        Wi = jax.random.normal(ks[2], (F, D), dtype=jnp.float32) * (1.0 / np.sqrt(D))
        Wo = jax.random.normal(ks[3], (D, F), dtype=jnp.float32) * (1.0 / np.sqrt(F))
        A = jax.random.normal(ks[4], (E, R, D), dtype=jnp.float32) * (1.0 / np.sqrt(D))
        Bm = jax.random.normal(ks[5], (E, F, R), dtype=jnp.float32) * 0.01
        return {'x': x, 'Wg': Wg, 'bg': bg, 'Wi': Wi, 'Wo': Wo, 'A': A, 'B': Bm}
    _L0_ffn_all = _L0_ffn_setup()
    _L0_ffn_in = {k: v for k, v in _L0_ffn_all.items() if k in ('Wg', 'bg', 'Wi', 'Wo', 'A', 'B')}
    del _L0_ffn_all
    return {'x': x, 'cond_1024': cond_1024, 'L0_cond_w_q': _L0_cond_in['w_q'], 'L0_cond_b_q': _L0_cond_in['b_q'], 'L0_cond_w_k': _L0_cond_in['w_k'], 'L0_cond_b_k': _L0_cond_in['b_k'], 'L0_cond_w_v': _L0_cond_in['w_v'], 'L0_cond_b_v': _L0_cond_in['b_v'], 'L0_cond_w_o': _L0_cond_in['w_o'], 'L0_cond_b_o': _L0_cond_in['b_o'], 'L0_cond_w_f1': _L0_cond_in['w_f1'], 'L0_cond_b_f1': _L0_cond_in['b_f1'], 'L0_cond_w_f2': _L0_cond_in['w_f2'], 'L0_cond_b_f2': _L0_cond_in['b_f2'], 'L0_cond_w_ada': _L0_cond_in['w_ada'], 'L0_cond_b_ada': _L0_cond_in['b_ada'], 'L0_attn_wq': _L0_attn_in['wq'], 'L0_attn_wk': _L0_attn_in['wk'], 'L0_attn_wv': _L0_attn_in['wv'], 'L0_attn_wgq': _L0_attn_in['wgq'], 'L0_attn_wgk': _L0_attn_in['wgk'], 'L0_attn_wgv': _L0_attn_in['wgv'], 'L0_attn_r_out_w': _L0_attn_in['r_out_w'], 'L0_attn_gate_local_w': _L0_attn_in['gate_local_w'], 'L0_attn_gate_remote_w': _L0_attn_in['gate_remote_w'], 'L0_attn_w_out': _L0_attn_in['w_out'], 'L0_cond2_weight': _L0_cond2_in['weight'], 'L0_ffn_Wg': _L0_ffn_in['Wg'], 'L0_ffn_bg': _L0_ffn_in['bg'], 'L0_ffn_Wi': _L0_ffn_in['Wi'], 'L0_ffn_Wo': _L0_ffn_in['Wo'], 'L0_ffn_A': _L0_ffn_in['A'], 'L0_ffn_B': _L0_ffn_in['B']}

def reference(x, cond_1024, L0_cond_w_q, L0_cond_b_q, L0_cond_w_k, L0_cond_b_k, L0_cond_w_v, L0_cond_b_v, L0_cond_w_o, L0_cond_b_o, L0_cond_w_f1, L0_cond_b_f1, L0_cond_w_f2, L0_cond_b_f2, L0_cond_w_ada, L0_cond_b_ada, L0_attn_wq, L0_attn_wk, L0_attn_wv, L0_attn_wgq, L0_attn_wgk, L0_attn_wgv, L0_attn_r_out_w, L0_attn_gate_local_w, L0_attn_gate_remote_w, L0_attn_w_out, L0_cond2_weight, L0_ffn_Wg, L0_ffn_bg, L0_ffn_Wi, L0_ffn_Wo, L0_ffn_A, L0_ffn_B):
    import jax
    import jax.numpy as jnp

    def _L0_cond_ref(x, t_emb, w_q, b_q, w_k, b_k, w_v, b_v, w_o, b_o, w_f1, b_f1, w_f2, b_f2, w_ada, b_ada):
        import math
        import jax, jax.numpy as jnp
        import numpy as np
        EPS = 1e-07
        MAX_TANH_ARG = 1.0 - 1e-05

        def _norm(x):
            return jnp.sqrt(jnp.sum(x * x, axis=-1, keepdims=True)).clip(EPS)

        def logmap0(x):
            n = _norm(x)
            return jnp.arctanh(jnp.clip(n, EPS, MAX_TANH_ARG)) * x / n

        def expmap0(v):
            n = _norm(v)
            return jnp.tanh(n) * v / n

        def mobius_add(x, y):
            x2 = jnp.sum(x * x, -1, keepdims=True)
            y2 = jnp.sum(y * y, -1, keepdims=True)
            xy = jnp.sum(x * y, -1, keepdims=True)
            num = (1 + 2 * xy + y2) * x + (1 - x2) * y
            den = (1 + 2 * xy + x2 * y2).clip(EPS)
            return num / den

        def plin(x, w, b):
            return expmap0(logmap0(x) @ w + b)

        def layer_norm(x, eps=1e-06):
            m = x.mean(-1, keepdims=True)
            v = ((x - m) ** 2).mean(-1, keepdims=True)
            return (x - m) / jnp.sqrt(v + eps)

        def _beta(a, b):
            return math.exp(math.lgamma(a) + math.lgamma(b) - math.lgamma(a + b))
        D, H, FF = (256, 16, 1024)
        HD = D // H
        BETA_N = _beta(D / 2, 0.5)
        BETA_H = _beta(HD / 2, 0.5)

        def _to_heads(p):
            B, S, _ = p.shape
            t = logmap0(p).reshape(B, S, H, HD) * (BETA_H / BETA_N)
            return expmap0(jnp.transpose(t, (0, 2, 1, 3)))

        def _from_heads(ph):
            B, _, S, _ = ph.shape
            t = logmap0(ph) * (BETA_N / BETA_H)
            t = jnp.transpose(t, (0, 2, 1, 3)).reshape(B, S, D)
            return expmap0(t)
        ada = t_emb @ w_ada + b_ada
        sh_msa, sc_msa, g_msa, sh_mlp, sc_mlp, g_mlp = jnp.split(ada, 6, axis=-1)
        residual = x
        xn = layer_norm(logmap0(x))
        xm = expmap0(xn * (1 + sc_msa) + sh_msa)
        q = _to_heads(plin(xm, w_q, b_q))
        k = _to_heads(plin(xm, w_k, b_k))
        v = _to_heads(plin(xm, w_v, b_v))
        qt, kt, vt = (logmap0(q), logmap0(k), logmap0(v))
        scores = jnp.einsum('bhqd,bhkd->bhqk', qt, kt) / math.sqrt(HD)
        attn = jax.nn.softmax(scores, axis=-1)
        out_h = expmap0(jnp.einsum('bhqk,bhkd->bhqd', attn, vt))
        attn_out = plin(_from_heads(out_h), w_o, b_o)
        attn_t = g_msa * logmap0(attn_out)
        x = mobius_add(residual, expmap0(attn_t))
        residual = x
        xn = layer_norm(logmap0(x))
        xm = expmap0(xn * (1 + sc_mlp) + sh_mlp)
        ff = plin(plin(xm, w_f1, b_f1), w_f2, b_f2)
        ff_t = g_mlp * logmap0(ff)
        return mobius_add(residual, expmap0(ff_t))

    def _L0_attn_ref(x, wq, wk, wv, wgq, wgk, wgv, r_out_w, gate_local_w, gate_remote_w, w_out):
        import jax, jax.numpy as jnp
        import numpy as np
        D_MODEL = 256
        N_HEADS = 16
        LATENT_HEADS = 8
        LATENT_DIM = 128
        N_LATENTS = 64
        WINDOW = 64
        HEAD_DIM = D_MODEL // N_HEADS
        LAT_HD = LATENT_DIM // LATENT_HEADS
        B, S = (2, 1024)

        def _pool_to_latents(x):
            Bx, Sx, C = x.shape
            chunk = max(1, Sx // N_LATENTS)
            return x.reshape(Bx, N_LATENTS, chunk, C).mean(axis=2)

        def _local_window_attn(Q, K, V):
            Bx, H, Sx, D = Q.shape
            W = WINDOW
            nb = Sx // W
            Qb = Q.reshape(Bx, H, nb, W, D)
            Kp = jnp.pad(K, ((0, 0), (0, 0), (W, 0), (0, 0))).reshape(Bx, H, nb + 1, W, D)
            Vp = jnp.pad(V, ((0, 0), (0, 0), (W, 0), (0, 0))).reshape(Bx, H, nb + 1, W, D)
            Kw = jnp.concatenate([Kp[:, :, :-1], Kp[:, :, 1:]], axis=3)
            Vw = jnp.concatenate([Vp[:, :, :-1], Vp[:, :, 1:]], axis=3)
            i = jnp.arange(W)[:, None]
            j = jnp.arange(2 * W)[None, :]
            base = (j > i) & (j <= i + W)
            blk0 = (jnp.arange(nb) > 0)[:, None, None] | (j >= W)[None, :, :]
            mask = base[None, :, :] & blk0
            sc = jnp.einsum('bhnid,bhnjd->bhnij', Qb, Kw) / np.sqrt(D).astype(np.float32)
            sc = jnp.where(mask[None, None], sc, -jnp.inf)
            p = jax.nn.softmax(sc, axis=-1)
            out = jnp.einsum('bhnij,bhnjd->bhnid', p, Vw)
            return out.reshape(Bx, H, Sx, D)
        Bx, Sx, _ = x.shape
        chunk = max(1, Sx // N_LATENTS)
        Q = (x @ wq).reshape(Bx, Sx, N_HEADS, HEAD_DIM).transpose(0, 2, 1, 3)
        K = (x @ wk).reshape(Bx, Sx, N_HEADS, HEAD_DIM).transpose(0, 2, 1, 3)
        V = (x @ wv).reshape(Bx, Sx, N_HEADS, HEAD_DIM).transpose(0, 2, 1, 3)
        local = _local_window_attn(Q, K, V)
        GQ = (x @ wgq).reshape(Bx, Sx, LATENT_HEADS, LAT_HD).transpose(0, 2, 1, 3)
        GK = _pool_to_latents(x @ wgk).reshape(Bx, N_LATENTS, LATENT_HEADS, LAT_HD).transpose(0, 2, 1, 3)
        GV = _pool_to_latents(x @ wgv).reshape(Bx, N_LATENTS, LATENT_HEADS, LAT_HD).transpose(0, 2, 1, 3)
        lsc = jnp.einsum('bhsd,bhnd->bhsn', GQ, GK) / np.sqrt(LAT_HD).astype(np.float32)
        lmask = jnp.arange(N_LATENTS)[None, :] <= (jnp.arange(Sx) // chunk)[:, None]
        lsc = jnp.where(lmask[None, None], lsc, -jnp.inf)
        lp = jax.nn.softmax(lsc, axis=-1)
        rem = jnp.einsum('bhsn,bhnd->bhsd', lp, GV)
        rem = rem.transpose(0, 2, 1, 3).reshape(Bx, Sx, LATENT_DIM) @ r_out_w
        rem = rem.reshape(Bx, Sx, N_HEADS, HEAD_DIM).transpose(0, 2, 1, 3)
        gl = jax.nn.sigmoid(jnp.einsum('bhsd,hd->bhs', Q, gate_local_w))[..., None]
        gr = jax.nn.sigmoid(jnp.einsum('bhsd,hd->bhs', Q, gate_remote_w))[..., None]
        out = gl * local + gr * rem
        out = out.transpose(0, 2, 1, 3).reshape(Bx, Sx, D_MODEL)
        return out @ w_out

    def _L0_cond2_ref(Efou, y, weight):
        import jax, jax.numpy as jnp
        import numpy as np
        IN_FEATURES = 256
        OUT_FEATURES = 256
        BATCH = 32
        SEQ = 256
        EPS = 1e-08
        scale = 1.0 / np.sqrt(np.float32(weight.shape[0]))
        ys = y * scale
        d = jax.lax.rsqrt(jnp.einsum('bi,io->bo', ys * ys, weight * weight) + EPS)
        out = jnp.einsum('bsi,io->bso', Efou * ys[:, None, :], weight) * d[:, None, :]
        return out

    def _L0_ffn_ref(x, Wg, bg, Wi, Wo, A, B):
        import jax, jax.numpy as jnp
        import numpy as np
        TOP_K = 2
        E = Wg.shape[0]
        logits = jnp.einsum('bsd,ed->bse', x, Wg) + bg
        scores = jax.nn.softmax(logits, axis=-1)
        topv, topi = jax.lax.top_k(scores, TOP_K)
        w = jnp.sum(jax.nn.one_hot(topi, E, dtype=x.dtype) * topv[..., None], axis=-2)
        base = jnp.einsum('bsd,fd->bsf', x, Wi)
        lora_low = jnp.einsum('bsd,erd->bser', x, A)
        lora = jnp.einsum('bser,efr->bsef', lora_low, B)
        h = jax.nn.relu(base[:, :, None, :] + lora)
        expert_out = jnp.einsum('bsef,df->bsed', h, Wo)
        out = jnp.einsum('bse,bsed->bsd', w, expert_out)
        return out
    x = x + _L0_attn_ref(_L0_cond_ref(x, cond_1024[:, None, :], L0_cond_w_q, L0_cond_b_q, L0_cond_w_k, L0_cond_b_k, L0_cond_w_v, L0_cond_b_v, L0_cond_w_o, L0_cond_b_o, L0_cond_w_f1, L0_cond_b_f1, L0_cond_w_f2, L0_cond_b_f2, L0_cond_w_ada, L0_cond_b_ada), L0_attn_wq, L0_attn_wk, L0_attn_wv, L0_attn_wgq, L0_attn_wgk, L0_attn_wgv, L0_attn_r_out_w, L0_attn_gate_local_w, L0_attn_gate_remote_w, L0_attn_w_out)
    x = x + _L0_ffn_ref(_L0_cond2_ref(x, cond_1024, L0_cond2_weight), L0_ffn_Wg, L0_ffn_bg, L0_ffn_Wi, L0_ffn_Wo, L0_ffn_A, L0_ffn_B)
    return x

_drawn_inputs = setup_inputs


def setup_inputs(seed=0):
    import zlib

    import numpy as np

    out = dict(_drawn_inputs(seed))
    spreads = {'L0_cond_b_q': (0.0, 2.0),
     'L0_cond_b_k': (0.0, 2.0),
     'L0_cond_b_v': (0.0, 0.1),
     'L0_cond_b_o': (0.0, 0.1),
     'L0_cond_b_f1': (0.0, 0.1),
     'L0_cond_b_f2': (0.0, 0.1),
     'L0_cond_b_ada': (0.0, 0.1),
     'L0_ffn_bg': (0.0, 0.8)}
    factors = {'L0_cond_w_q': 44.469,
     'L0_cond_w_k': 28.202,
     'L0_cond_w_v': 4.555,
     'L0_attn_wq': 46.171,
     'L0_attn_wk': 200.0,
     'L0_attn_wgq': 200.0,
     'L0_attn_wgk': 200.0,
     'L0_attn_gate_local_w': 41.216,
     'L0_attn_gate_remote_w': 64.0,
     'L0_ffn_Wg': 8.0,
     'L0_ffn_A': 8.0,
     'L0_ffn_B': 8.0}
    for name, (base, spread) in spreads.items():
        noise = np.random.default_rng([zlib.crc32(name.encode()), seed]).standard_normal(out[name].shape)
        drawn = base * np.exp(spread * noise) if base else spread * noise
        out[name] = jnp.asarray(drawn.astype(out[name].dtype))
    for name, factor in factors.items():
        out[name] = (out[name] * factor).astype(out[name].dtype)
    return out
```

```python
import math
from contextlib import ExitStack

import numpy as np

import concourse.bass as bass
from concourse import mybir

F32 = mybir.dt.float32
F32R = mybir.dt.float32r
BF16 = mybir.dt.bfloat16
I32 = mybir.dt.int32
ALU = mybir.AluOpType
ACT = mybir.ActivationFunctionType
AX = mybir.AxisListType

NB, S, D, FF = 16, 256, 256, 1024
NT = 2 * NB
EPS = 1e-7
TMAX = float(np.float32(1.0 - 1e-5))
CL = math.atanh(TMAX)


def _beta(a, b):
    return math.exp(math.lgamma(a) + math.lgamma(b) - math.lgamma(a + b))


RT = _beta(8, 0.5) / _beta(128, 0.5)


class Lane:

    def __init__(self, nc, ctx, name, limit=16000):
        self.nc, self.ctx, self.name, self.limit = nc, ctx, name, limit
        self.ops, self.count, self.turn = [], limit, 0

    def put(self, fn, *after, mark=True):
        token = None
        if mark:
            if self.count >= self.limit:
                self.sem = self.ctx.enter_context(self.nc.semaphore(f"s_{self.name}{self.turn}"))
                self.turn += 1
                self.count = 0
            self.count += 1
            token = (self.sem, self.count)
        self.ops.append((fn, flat(after), token))
        return token

    def dma(self, fn, sem, value, *after):
        self.ops.append((fn, flat(after), (sem, 16)))
        return (sem, value)

    def play(self, eng):
        seen = {}
        for fn, after, token in self.ops:
            for sem, value in after:
                if seen.get(sem.name, 0) < value:
                    seen[sem.name] = value
                    eng.wait_ge(sem, value)
            ins = fn(eng)
            if token is not None:
                ins.then_inc(token[0], 16 if token[1] == 16 and "d_" in token[0].name else 1)


def flat(x):
    if x is None:
        return []
    if isinstance(x, tuple) and len(x) == 2 and isinstance(x[1], int) and not isinstance(x[0], (tuple, list)):
        return [x]
    return [t for y in x for t in flat(y)]


class Ring:

    def __init__(self, tiles):
        self.tiles, self.free = tiles, [(None, i) for i in range(len(tiles))]

    def take(self):
        assert self.free, "no tile is free"
        over, i = self.free.pop(0)
        return self.tiles[i], over, i

    def give(self, i, *over):
        self.free.append((flat(over), i))


def grab(ring):
    while not ring.free:
        yield
    return ring.take()


def weave(*gens):
    live = [[g, n, 0] for g, n in gens if g is not None]
    counts = []
    while live:
        live.sort(key=lambda s: (s[2] + 1) / s[1])
        s = live[0]
        try:
            next(s[0])
            s[2] += 1
        except StopIteration:
            counts.append((s[0].__name__, s[2]))
            live.remove(s)
    return counts


def program(nc, A, out, nb=NB, taps=None):
    ctx = ExitStack()
    with ctx:
        def sb(name, shape, dt=F32):
            return ctx.enter_context(nc.sbuf_tensor(name, shape, dt))

        pe, act, dve, pool, sp = (Lane(nc, ctx, n) for n in ("pe", "act", "dve", "pool", "sp"))
        loads = {}

        def load(name, dst, src, lane=sp, *after):
            sem = ctx.enter_context(nc.semaphore(f"d_{name}"))
            loads[name] = lane.dma(lambda e: e.dma_start(dst, src), sem, 16, *after)
            return loads[name]

        S2 = Ring([ctx.enter_context(nc.psum_tensor(f"pS{i}", [128, 1024], F32)) for i in range(2)])
        PO = Ring([ctx.enter_context(nc.psum_tensor("pO", [128, 512], F32))])
        G = Ring([ctx.enter_context(nc.psum_tensor(f"pG{i}", [128, 512], F32)) for i in range(3)])

        X = sb("X", [128, NT, D])
        X1 = X
        XR = [sb(f"XR{i}", [128, 2, D]) for i in range(2)]
        ident = sb("ident", [128, 128])
        identb = sb("identb", [128, 128], BF16)
        maskb = sb("maskb", [128, 320 + 320 + 128 + 256], BF16)
        zsel = sb("zsel", [128, 24])
        zselr = sb("zselr", [128, 24])
        hsel = sb("hsel", [128, 2])
        condT = sb("condT", [128, 2, 16])
        adaT = sb("adaT", [128, 12, 16])
        badaT = sb("badaT", [128, 12])
        grow = sb("grow", [16, 512])
        b2 = sb("b2", [128, D])
        b1w2 = sb("b1w2", [128, 258])
        W12 = sb("W12", [128, 2, 256])
        GG = sb("GG", [128, 2, 258])
        wat = sb("wat", [128, 2, 928])
        wgkv = sb("wgkv", [128, 2, 256])
        wr = sb("wr", [128, D])
        wout = sb("wout", [128, 2, D])
        w2c = sb("w2c", [128, 2, D])
        dT = sb("dT", [128, 2, 16])
        ysT = sb("ysT", [128, 2, 16])
        WiT = sb("WiT", [128, 2, FF])
        WoT = sb("WoT", [128, 8, D])
        wrt = sb("wrt", [128, 2, 20])
        bg = sb("bg", [128, 4])
        ltm = sb("ltm", [128, 16])
        Bst = sb("Bst", [128, FF])
        st = sb("st", [128, 2, 24, 16])
        mv = sb("mv", [128, NT, 2])
        bn = sb("bn", [128, 4, 6])
        rX, ssX, rX1, ssX1 = (sb(n, [128, NT]) for n in ("rX", "ssX", "rX1", "ssX1"))
        lp = sb("lp", [128, 10, NT])
        FR = sb("FR", [128, 8192])
        FA = sb("FA", [128, 12800])

        frp, fap = [0], [0]

        FW = sb("FW", [128, 3072])
        SQ = sb("SQ", [128, 2, 768])
        fwp = [0]

        def cut(arena, ptr, *shape):
            n = int(np.prod(shape))
            a = arena[:, ptr[0]:ptr[0] + n]
            ptr[0] += n
            assert ptr[0] <= arena.shape[1], (ptr, arena.shape)
            names = "abcdef"[:len(shape)]
            if len(shape) == 1:
                return a
            kw = {names[i]: shape[i] for i in range(1, len(shape))}
            return a.rearrange(f"p ({' '.join(names)}) -> p {' '.join(names)}", **kw)

        def bc(ap, n):
            shape = list(ap.shape)
            return ap.unsqueeze(len(shape)).broadcast_to(shape + [n])

        def chain(lane, fns, *after):
            tok = after
            for fn in fns:
                tok = lane.put(fn, tok)
                yield tok

        def need(kind, b):
            while b >= 0 and (kind, b) not in T:
                yield

        def ts(o, i, s1, s2, op0, op1=None):
            if op1 is None:
                return lambda e: e.tensor_scalar(o, i, s1, None, op0)
            return lambda e: e.tensor_scalar(o, i, s1, s2, op0, op1)

        def tt(o, a, b, op):
            return lambda e: e.tensor_tensor(o, a, b, op)

        def stt(o, a, s, b, op0, op1):
            return lambda e: e.scalar_tensor_tensor(out=o, in0=a, scalar=s, in1=b, op0=op0, op1=op1)

        def red(o, i, op=ALU.add, negate=False):
            return lambda e: e.tensor_reduce(o, i, AX.X, op, negate=negate)

        def rsqrt(x, y, a, b):
            fns = [ts(a.bitcast(I32), x.bitcast(I32), 1, None, ALU.logical_shift_right),
                   ts(y.bitcast(I32), a.bitcast(I32), -1.0, float(0x5F3759DF), ALU.mult, ALU.add)]
            for _ in range(3):
                fns += [tt(a, y, y, ALU.mult), stt(b, a, -0.5, x, ALU.mult, ALU.mult),
                        stt(y, b, 1.5, y, ALU.add, ALU.mult)]
            return fns

        def mm(o, lhsT, rhs, start, stop, *after, mark=False):
            return pe.put(lambda e: e.matmul(o, lhsT, rhs, start=start, stop=stop, skip_group_check=True),
                          *after, mark=mark)

        def tr(o, i, *after, mark=False):
            return pe.put(lambda e: e.transpose(o, i, ident[:, :]), *after, mark=mark)

        def acopy(o, i, *after):
            return act.put(lambda e: e.activation(o, i, ACT.Copy), *after)

        turn = [0]

        def evac(o, i, *after):
            turn[0] += 1
            if turn[0] % 3 == 0:
                return dve.put(lambda e: e.tensor_copy(o, i), *after)
            return acopy(o, i, *after)

        wqkv, bqkv, wo, bo = (cut(FW, fwp, *n) for n in ((2, 768), (768,), (2, D), (D,)))

        xv = A["x"].rearrange("b (t p) d -> p (b t) d", p=128)
        load("cond", condT[:, :, :], A["condT"].rearrange("(c p) b -> p c b", p=128))
        load("ident", ident[:, :], A["ident"])
        for q in range(4):
            load(f"x{q}", X[:, 8 * q:8 * q + 8, :], xv[:, 8 * q:8 * q + 8, :], act if q % 2 else sp)
        wada = cut(FA, [0], 2, 1536)
        w1T = cut(FA, [3584], 8, 258)
        w2x = cut(FA, [3584 + 2064], 8, 256)
        b1c = cut(FA, [3584 + 2048 + 2064], 8)
        gate = cut(FA, [3584 + 2048 + 2064 + 16], 2, 256)
        mf = cut(FA, [3584 + 2048 + 2064 + 16 + 512], 1024)
        gtmp = cut(FA, [3584 + 2048 + 2064 + 16 + 512 + 1024], 2, 2, 256)
        Bf = cut(FA, [3584 + 2048 + 2064 + 16 + 512 + 1024 + 1024], 1024)
        Bh = cut(FA, [3584 + 2048 + 2064 + 16 + 512 + 2048 + 1024], 1024)
        w2sq = cut(FA, [3072], 2, 256)
        brow = SQ[0:16, 0, 0:512]
        load("wada", wada, A["w_ada"].rearrange("(c p) n -> p c n", p=128))
        load("bada", badaT[:, :], A["badaT"])
        load("brow0", brow[:, 0:256], A["b_ada"][512:768].partition_broadcast(16))
        load("brow1", brow[:, 256:512], A["b_ada"][1280:1536].partition_broadcast(16))
        load("wqkv", wqkv, A["wqkv"].rearrange("(c p) n -> p c n", p=128))
        load("bqkv", bqkv[:, :], A["bqkv"].partition_broadcast(128))
        load("w1T", w1T[:, :, 0:256], A["w1T"].rearrange("(c p) n -> p c n", p=128))
        load("w2", w2x, A["w2"].rearrange("(c p) n -> p c n", p=128), act)
        load("b1c", b1c, A["b1c"], act)
        load("wo", wo, A["w_o"].rearrange("(c p) n -> p c n", p=128))
        load("bo", bo[:, :], A["b_o"].partition_broadcast(128))
        load("mf", mf, A["masks"], act)
        load("zsel", zsel[:, :], A["zsel"], act)
        load("hsel", hsel[:, :], A["hsel"], act)
        load("ltm", ltm[:, :], A["ltm"].partition_broadcast(128), act)
        load("b2", b2[:, :], A["b_f2"].partition_broadcast(128), act)
        load("wat", wat[:, :, 0:896], A["wat"].rearrange("(c p) n -> p c n", p=128))
        load("wgkv", wgkv[:, :, :], A["wgkv"].rearrange("(c p) n -> p c n", p=128))
        load("gate0", gate[:, 0, :], A["gl"].partition_broadcast(128), act)
        load("gate1", gate[:, 1, :], A["gr"].partition_broadcast(128), act)
        load("wr", wr[:, :], A["r_out_w"])
        load("wout", wout[:, :, :], A["w_out"].rearrange("(c p) n -> p c n", p=128))
        load("w2c", w2c[:, :, :], A["weight"].rearrange("(c p) n -> p c n", p=128), act)
        load("wrt", wrt[:, :, :], A["wrt"].rearrange("(c p) n -> p c n", p=128), act)
        load("bg", bg[:, :], A["bg"].partition_broadcast(128), act)
        for r in range(8):
            load(f"B{r}", Bf[16 * r:16 * r + 16, :], A["Bc"], act)
        load("WiT", WiT[:, :, :], A["WiT"].rearrange("(c p) n -> p c n", p=128))
        load("WoT", WoT[:, :, :], A["WoT"].rearrange("(c p) n -> p c n", p=128))

        def ln_prep(mean, var, ss, r, n, *after):
            a, b, y, t, z, p, q, m = (lp[:, i, 0:n] for i in range(8))
            yield from chain(dve, [
                tt(a, mean, mean, ALU.mult), tt(a, a, var, ALU.add),
                ts(ss, a, 256.0, 0.0, ALU.mult, ALU.add), ts(z, ss, EPS * EPS, None, ALU.max)], *after)
            yield from chain(dve, rsqrt(z, y, a, b), dve_last())
            yield from chain(dve, [tt(t, z, y, ALU.mult), ts(t, t, TMAX, None, ALU.min),
                                   ts(q, t, -1.0, 1.0, ALU.mult, ALU.add)], dve_last())
            yield from chain(dve, [lambda e: e.reciprocal(b, q), stt(q, t, 1.0, b, ALU.add, ALU.mult)], dve_last())
            tok = act.put(lambda e: e.activation(p, q, ACT.Ln), dve_last())
            yield from chain(dve, [
                tt(z, t, t, ALU.mult), ts(a, z, 1.0 / 11, None, ALU.mult),
                stt(a, a, 1.0 / 9, z, ALU.add, ALU.mult), stt(a, a, 1.0 / 7, z, ALU.add, ALU.mult),
                stt(a, a, 1.0 / 5, z, ALU.add, ALU.mult), stt(a, a, 1.0 / 3, z, ALU.add, ALU.mult),
                stt(a, a, 1.0, t, ALU.add, ALU.mult), ts(m, t, 0.25, None, ALU.is_lt),
                stt(a, p, -0.5, a, ALU.mult, ALU.add), tt(a, a, m, ALU.mult),
                stt(a, p, 0.5, a, ALU.mult, ALU.add), tt(q, a, y, ALU.mult),
                tt(a, q, q, ALU.mult), tt(a, a, var, ALU.mult), ts(z, a, 1e-6, None, ALU.add)], dve_last(), tok)
            yield from chain(dve, rsqrt(z, y, a, b), dve_last())
            yield from chain(dve, [tt(r, q, y, ALU.mult)], dve_last())

        def dve_last():
            return (dve.sem, dve.count)

        def act_last():
            return (act.sem, act.count)

        def pool_last():
            return (pool.sem, pool.count)

        T = {}
        for q in range(4):
            for i in range(8 * q, 8 * q + 8):
                if i >= 2 * nb:
                    continue
                k = i % 4
                t1 = dve.put(lambda e, i=i, k=k: e.bn_stats(bn[:, k, :], X[:, i, :]), loads[f"x{q}"], T.get(("bn", k)))
                T["bn", k] = dve.put(lambda e, i=i, k=k: e.bn_aggr(mv[:, i, :], bn[:, k, :]), t1)
        NN = 2 * nb
        for _ in ln_prep(mv[:, 0:NN, 0], mv[:, 0:NN, 1], ssX[:, 0:NN], rX[:, 0:NN], NN, T["bn", (NN - 1) % 4]):
            pass
        nmean = dve_last()

        def P_(t):
            return loads[t]

        tb = pool.put(lambda e: e.tensor_copy(identb[:, :], ident[:, :]), P_("ident"))
        tb = pool.put(lambda e: e.tensor_copy(maskb[:, :], mf), P_("mf"))
        pool.put(lambda e: e.tensor_copy(zselr[:, :].bitcast(F32R), zsel[:, :]), P_("zsel"))
        pool.put(lambda e: e.tensor_scalar(wgkv[:, :, :], wgkv[:, :, :], 0.25, None, ALU.mult), P_("wgkv"))
        t1 = pool.put(lambda e: e.memset(w1T[:, :, 257:258], 0.0))
        tb = pool.put(lambda e: e.tensor_copy(w1T[:, :, 256:257], b1c.unsqueeze(2)), P_("b1c"))
        consts = pool_last()

        bank, over, gi = G.take()
        for j in range(12):
            for c in range(2):
                t1 = mm(bank[:, 16 * j:16 * j + 16], wada[:, c, 128 * j:128 * j + 128], condT[:, c, :], c == 0, c == 1,
                        P_("wada"), P_("cond"), mark=j == 11 and c == 1)
        for j in range(12):
            o, i = adaT[:, j, :], bank[:, 16 * j:16 * j + 16]
            if j in (2, 3, 8, 9):
                t2 = dve.put(ts(o, i, badaT[:, j:j + 1], 1.0, ALU.add, ALU.add), t1, P_("bada"))
            else:
                t2 = dve.put(ts(o, i, badaT[:, j:j + 1], None, ALU.add), t1, P_("bada"))
        G.give(gi, t2)
        bank, over, gi = G.take()
        wg2 = wada.rearrange("p c (s k n) -> p c s k n", s=2, k=3)[:, :, :, 2, :]
        for c in range(2):
            t1 = mm(bank[0:16, :].rearrange("p (s n) -> p s n", s=2), condT[:, c, :], wg2[:, c], c == 0, c == 1, over,
                    mark=c == 1)
        T["grow"] = dve.put(tt(grow[:, :], bank[0:16, :], brow[:, :], ALU.add), t1, P_("brow0"), P_("brow1"))
        wada_read = t1
        G.give(gi, T["grow"])

        for ic in range(2):
            for dst, w, n in ((W12, w2x, 256), (GG, w1T, 258)):
                bank, over, gi = G.take()
                for f in range(8):
                    t1 = mm(bank[:, 0:n], w1T[:, f, 128 * ic:128 * ic + 128], w[:, f, 0:n], f == 0, f == 7, over,
                            P_("w1T"), P_("w2"), consts, mark=f == 7)
                t2 = evac(dst[:, ic, :], bank[:, 0:n], t1)
                G.give(gi, t2)
                T["w12", ic, n] = t2
        bank, over, gi = G.take()
        for f in range(8):
            t1 = mm(bank[:, 0:256], b1c[:, f:f + 1].broadcast_to([128, 128]), w2x[:, f, :], f == 0, f == 7, over)
        for f in range(8):
            t1 = mm(bank[:, 256:258], b1c[:, f:f + 1].broadcast_to([128, 128]), w1T[:, f, 256:258], f == 0, f == 7,
                    mark=f == 7)
        T["b1w2"] = evac(b1w2[:, :], bank[:, 0:258], t1)
        G.give(gi, T["b1w2"])
        for g in range(2):
            t1 = pool.put(lambda e, g=g: e.tensor_tensor(gtmp[:, g], wat[:, :, 0:256],
                                                         gate[:, g, :].unsqueeze(1).broadcast_to([128, 2, 256]), ALU.mult),
                          P_("wat"), P_(f"gate{g}"))
            for c in range(2):
                T["wgate"] = dve.put(red(wat[:, c, 896 + 16 * g:912 + 16 * g],
                                         gtmp[:, g, c].rearrange("p (h d) -> p h d", d=16)), t1)
        t1 = dve.put(ts(ysT[:, :, :], condT[:, :, :], 1.0 / 16, None, ALU.mult), P_("cond"))
        yq = lp[:, 8, 0:32].rearrange("p (c b) -> p c b", c=2)
        t2 = dve.put(tt(yq, ysT[:, :, :], ysT[:, :, :], ALU.mult), t1)
        t3 = pool.put(lambda e: e.tensor_tensor(w2sq, w2c[:, :, :], w2c[:, :, :], ALU.mult), P_("w2c"))
        bank, over, gi = G.take()
        for oc in range(2):
            for c in range(2):
                t1 = mm(bank[:, 16 * oc:16 * oc + 16], w2sq[:, c, 128 * oc:128 * oc + 128], yq[:, c, :], c == 0, c == 1,
                        over, t2, t3, mark=True)
        dz, dy, da, db = (lp[:, i, 0:32] for i in (9, 0, 1, 2))
        for _ in chain(dve, [ts(dz, bank[:, 0:32], 1e-8, None, ALU.add)], t1, dve_last()):
            pass
        G.give(gi, dve_last())
        for _ in chain(dve, rsqrt(dz, dy, da, db), dve_last()):
            pass
        T["dT"] = dve.put(lambda e: e.tensor_copy(dT[:, :, :], dy.rearrange("p (c b) -> p c b", c=2)), dve_last())
        t1 = dve.put(lambda e: e.tensor_copy(Bh[:, :].bitcast(F32R), Bf[:, :]), [P_(f"B{r}") for r in range(8)])
        t2 = dve.put(tt(Bf[:, :], Bf[:, :], Bh[:, :], ALU.subtract), t1)
        t3 = dve.put(ts(Bf[:, :], Bf[:, :], hsel[:, 1:2], None, ALU.mult), t2, P_("hsel"))
        T["Bst"] = dve.put(stt(Bst[:, :].bitcast(F32R), Bh[:, :], hsel[:, 0:1], Bf[:, :], ALU.mult, ALU.add), t3)

        setup_done = [dve_last(), act_last(), pool_last(), T["b1w2"], T["Bst"],
                      pe.put(lambda e: e.matmul(bank[0:2, 100:102], ident[:, 0:2], ident[:, 0:2], start=True, stop=True),
                             dve_last(), P_("ident"))]

        if taps is not None and taps.get("stop") == 0:
            return finish_up(nc, ctx, (pe, act, dve, pool, sp), loads, taps, dict(X1=X1, adaT=adaT, W12=W12, GG=GG, dT=dT, b1w2=b1w2, rX=rX), setup_done)
        frp[0], fap[0] = 0, 0
        QsT = [cut(FR, frp, 8, 256) for _ in range(2)]
        KsT = [cut(FR, frp, 8, 256) for _ in range(2)]
        PT = Ring([cut(FA, fap, 1024) for _ in range(4)])
        mT = cut(FA, fap, 2, 256)
        tT = cut(FA, fap, 2, 256)
        HL = cut(FA, fap, 2, 16, 4, 16)
        Vg = [cut(FA, fap, 2, 16, 32) for _ in range(2)]
        U = cut(FA, fap, 2, 768)
        OT = cut(FA, fap, 4, 256)
        O = cut(FA, fap, 2, 256)
        xn = cut(FA, fap, 2, 256)
        JK = sb("JK", [128, 2, 256])
        Z = sb("Z", [128, 2, 256])
        UO = sb("UO", [128, 2, 256])
        sm = sb("sm", [128, 64, 2])
        hall = sb("hall", [128, 520])
        h_a, h_b, h_y, h_s = (hall[:, 104 * i:104 * i + 104].rearrange("p (t n) -> p t n", t=2) for i in range(4))
        k_a, k_b, k_y, k_s, k_f = (sb(n, [128, 2, 16]) for n in ("k_a", "k_b", "k_y", "k_s", "k_f"))

        for v in range(2):
            a = pool.put(lambda e, m=Vg[v]: e.memset(m, 0.0), setup_done)
            T["vg", v] = pool.put(lambda e, m=Vg[v]: e.memset(m[:, :, :, 16:17], 1.0), a)
        ph1 = [setup_done, T["vg", 1], [P_(k) for k in ("wqkv", "bqkv", "wo", "bo")]]

        def s_mod(b, src, mean, r, sh, base, *after):
            for t in range(2):
                i = 2 * b + t
                tk = dve.put(ts(xn[:, t, :], src[:, i, :], mean[:, i:i + 1], r[:, i:i + 1], ALU.subtract, ALU.mult), *after, T.get(("xnT", base, b - 1)))
                yield
            bank, over, gi = yield from grab(G)
            for t in range(2):
                for c in range(2):
                    tp = tr(bank[:, 256 * c + 128 * t:256 * c + 128 * t + 128], xn[:, t, 128 * c:128 * c + 128], over, tk,
                            mark=t + c == 2)
            T["xnT", base, b] = tp
            yield
            for c in range(2):
                tk = act.put(lambda e, c=c, bank=bank, mT=mT: e.activation(mT[:, c, :], bank[:, 256 * c:256 * c + 256], ACT.Identity,
                                                         bias=adaT[:, sh + c, b:b + 1], scale=adaT[:, sh + 2 + c, b:b + 1]),
                             tp, T.get(("mTread", base, b - 1)))
                yield
            G.give(gi, tk)
            T["mT", base, b] = tk
            bank, over, gi = yield from grab(G)
            for t in range(2):
                for c in range(2):
                    tp = tr(bank[:, 256 * t + 128 * c:256 * t + 128 * c + 128], mT[:, c, 128 * t:128 * t + 128], over, tk,
                            mark=t + c == 2)
            for t in range(2):
                tk = act.put(lambda e, t=t, bank=bank: e.activation(JK[:, t, :], bank[:, 256 * t:256 * t + 256], ACT.Square,
                                                         accum_out=sm[:, 0, t:t + 1]), tp, T.get(("sm0", base, b - 1)))
                yield
            T["mss", base, b] = tk
            T["mbank"] = (bank, gi, tk, tp)

        def s_qkv(b):
            yield from s_mod(b, X, mv[:, :, 0], rX, 0, 1, ph1)
            bank, gi, tk, tp = T["mbank"]
            G.give(gi, tk)
            z, y, a, c_ = (sm[:, i, :] for i in (1, 2, 3, 4))
            yield from chain(dve, [ts(z, sm[:, 0, :], EPS * EPS, None, ALU.max)] + rsqrt(z, y, a, c_)
                             + [ts(y, y, CL, 1.0, ALU.mult, ALU.min)], T["mss", 1, b])
            T["sm0", 1, b] = s1 = dve_last()
            for t in range(2):
                b0, o0, g0 = yield from grab(G)
                for c in range(2):
                    t0 = mm(b0[:, :], mT[:, c, 128 * t:128 * t + 128], wqkv[:, c, 0:512], c == 0, c == 1, o0,
                            T["mT", 1, b], mark=c == 1)
                yield
                b1, o1, g1 = yield from grab(G)
                for c in range(2):
                    t1 = mm(b1[:, 0:256], mT[:, c, 128 * t:128 * t + 128], wqkv[:, c, 512:768], c == 0, c == 1, o1,
                            mark=c == 1)
                yield
                war = T.get(("Uread", b - 1))
                tk = dve.put(stt(U[:, t, 0:512], b0[:, :], sm[:, 2, t:t + 1], bqkv[:, 0:512], ALU.mult, ALU.add), t0, s1, war)
                G.give(g0, tk)
                yield
                tk = dve.put(stt(U[:, t, 512:768], b1[:, 0:256], sm[:, 2, t:t + 1], bqkv[:, 512:768], ALU.mult, ALU.add),
                             t1, s1, war)
                G.give(g1, tk)
                yield
                tk = pool.put(tt(SQ[:, t, :], U[:, t, :], U[:, t, :], ALU.mult), tk, T.get(("hss", b - 1, t)))
                yield
                T["hss", b, t] = dve.put(red(h_s[:, t, 0:48], SQ[:, t, :].rearrange("p (h d) -> p h d", d=16)), tk,
                                         T.get(("hf", b - 1)))
                yield
            T["mTread", 1, b] = t1
            hf = [red(h_s[:, :, 48:51], h_s[:, :, 0:48].rearrange("p t (g h) -> p t g h", g=3)),
                  ts(h_s[:, :, 0:51], h_s[:, :, 0:51], EPS * EPS, None, ALU.max)]
            hf += rsqrt(h_s[:, :, 0:51], h_y[:, :, 0:51], h_a[:, :, 0:51], h_b[:, :, 0:51])
            hf += [ts(h_a[:, :, 48:51], h_y[:, :, 48:51], CL, 1.0, ALU.mult, ALU.min),
                   ts(h_a[:, :, 48:51], h_a[:, :, 48:51], RT, None, ALU.mult)]
            yield from chain(dve, hf, [T["hss", b, t] for t in range(2)], T.get(("hread", b - 1)))
            for t in range(2):
                tk = dve.put(stt(h_b[:, t, 0:48].rearrange("p (g h) -> p g h", g=3),
                                 h_y[:, t, 0:48].rearrange("p (g h) -> p g h", g=3), CL,
                                 bc(h_a[:, t, 48:51], 16), ALU.mult, ALU.min), dve_last())
            T["hf", b] = tk
            yield
            vg = Vg[b % 2]
            for t in range(2):
                uv = U[:, t, :].rearrange("p (h d) -> p h d", d=16)
                tv = dve.put(tt(vg[:, t, :, 0:16], uv[:, 32:48], bc(h_b[:, t, 32:48], 16), ALU.mult), tk,
                             T.get(("pv", b - 2)))
                yield
                tq = dve.put(tt(uv[:, 0:32], uv[:, 0:32], bc(h_b[:, t, 0:32], 16), ALU.mult), tk)
                yield
                for g in range(2):
                    ug = uv[:, 16 * g:16 * g + 16].unsqueeze(2).broadcast_to([128, 16, 2, 16])
                    hi, lo = hilo(HL[:, g], g)
                    th = pool.put(lambda e, hi=hi, ug=ug: e.tensor_copy(hi, ug), tq, T.get(("hlread", g)))
                    yield
                    T["hl", g] = dve.put(tt(lo, ug, HL[:, g, :, 0, :].unsqueeze(2).broadcast_to([128, 16, 2, 16]),
                                            ALU.subtract), th, T.get(("hlread", g)))
                    yield
                    yield from stack(HL[:, g], 8, (QsT, KsT)[g][b % 2], t, T["hl", g], T.get(("scores", b - 2)))
                    T["hlread", g] = T["stackT"]
            T["st", b] = T["stdone"]
            T["Vg", b] = tv
            T["hread", b] = tq
            T["Uread", b] = T["hl", 1]

        def hilo(v, kind):
            v = v.bitcast(F32R)
            return (v[:, :, 0:2, :], v[:, :, 2:4, :]) if kind == 0 else (v[:, :, 0:4:2, :], v[:, :, 1:4:2, :])

        def stack(hl, npair, dst, t, ready, war):
            flat_ = hl.rearrange("p h a d -> p (h a d)")
            for p4 in range(npair // 4):
                bank, over, gi = yield from grab(G)
                for j in range(4):
                    tp = tr(bank[:, 128 * j:128 * j + 128], flat_[:, 512 * p4 + 128 * j:512 * p4 + 128 * j + 128],
                            over, ready, mark=j == 3)
                tk = evac(dst[:, 4 * p4:4 * p4 + 4, 128 * t:128 * t + 128].bitcast(F32R),
                          bank[:, :].rearrange("p (a n) -> p a n", a=4), tp, war)
                G.give(gi, tk)
                yield
            T["stackT"] = tp
            T["stdone"] = [act_last(), dve_last()]

        def s_att(b):
            q_, k_, vg = QsT[b % 2], KsT[b % 2], Vg[b % 2]
            ready = T["st", b]
            pend = []
            for p in range(8):
                ps, over, si = yield from grab(S2)
                for j in range(2):
                    for kt in range(2):
                        tp = mm(ps[:, 512 * j + 256 * kt:512 * j + 256 * kt + 256],
                                k_[64 * j:64 * j + 64, p, 128 * kt:128 * kt + 128].bitcast(F32R),
                                q_[64 * j:64 * j + 64, p, :].bitcast(F32R), True, True, over, ready, mark=j + kt == 2)
                yield
                pt, over, pi = yield from grab(PT)
                tk = act.put(lambda e, pt=pt, ps=ps: e.activation(pt, ps[:, :], ACT.Exp, scale=0.25), tp, over)
                S2.give(si, tk)
                pend.append((pt, pi, tk))
                yield
                if p == 7:
                    T["scores", b] = tp
                if p % 2 == 1:
                    g = p // 2
                    if g % 2 == 0:
                        po, oover, oi = yield from grab(PO)
                    for kt in range(2):
                        for j in range(4):
                            pt, pi, tk = pend[j // 2]
                            h = 4 * g + j
                            tp = mm(po[32 * j:32 * j + 32, 256 * (g % 2):256 * (g % 2) + 256], vg[:, kt, h, :],
                                    pt[:, 512 * (j % 2) + 256 * kt:512 * (j % 2) + 256 * kt + 256], kt == 0, kt == 1,
                                    oover, tk, T["Vg", b], pend[1][2], mark=kt == 1 and j == 3)
                        yield
                    for pt, pi, tk in pend:
                        PT.give(pi, tp)
                    pend = []
                    T["pv", b] = tp
                    if g % 2 == 1:
                        yield from need("OTread", b - 1)
                        tk = evac(OT[:, g - 1:g + 1, :], po[:, :].rearrange("p (a n) -> p a n", a=2), tp,
                                  T.get(("OTread", b - 1)))
                        PO.give(oi, tk)
                        T["OT", b, g // 2] = tk
                        yield

        def s_out(b):
            ready = [T["OT", b, 0], T["OT", b, 1]]
            for t in range(2):
                bank, over, gi = yield from grab(G)
                for g in range(4):
                    tp = tr(bank[:, 128 * g:128 * g + 128], OT[:, g, 128 * t:128 * t + 128], over, ready, mark=g == 3)
                bv = bank[:, :].rearrange("p (h n) -> p h n", n=32)
                yield
                tk = dve.put(lambda e, t=t, bv=bv: e.reciprocal(k_f[:, t, :], bv[:, :, 16]), tp, T.get(("kf", b - 1)))
                ov = O[:, t, :].rearrange("p (h d) -> p h d", d=16)
                yield
                to = dve.put(tt(ov, bv[:, :, 0:16], bc(k_f[:, t, :], 16), ALU.mult), tk, T.get(("Oread", b - 1)))
                G.give(gi, to)
                yield
                tq = pool.put(tt(JK2[:, t, :], O[:, t, :], O[:, t, :], ALU.mult), to, T.get(("ks", b - 1, t)))
                yield
                T["ks", b, t] = dve.put(red(k_s[:, t, :], JK2[:, t, :].rearrange("p (h d) -> p h d", d=16)), tq)
                yield
            T["OTread", b] = tp
            n1, z1, y1, a1, c1 = (sm[:, i, :] for i in (5, 6, 7, 8, 9))
            fns = [ts(k_s[:, :, :], k_s[:, :, :], EPS * EPS, None, ALU.max)]
            fns += rsqrt(k_s[:, :, :], k_y[:, :, :], k_a[:, :, :], k_b[:, :, :])
            fns += [ts(k_y[:, :, :], k_y[:, :, :], CL / RT, 1.0 / RT, ALU.mult, ALU.min),
                    tt(k_a[:, :, :], k_y[:, :, :], k_y[:, :, :], ALU.mult),
                    tt(k_a[:, :, :], k_a[:, :, :], k_s[:, :, :], ALU.mult),
                    red(z1, k_a[:, :, :]), ts(z1, z1, EPS * EPS, None, ALU.max)]
            fns += rsqrt(z1, y1, a1, c1) + [ts(y1, y1, CL, 1.0, ALU.mult, ALU.min)]
            yield from chain(dve, fns, T["ks", b, 0], T["ks", b, 1])
            tk = dve_last()
            for t in range(2):
                ov = O[:, t, :].rearrange("p (h d) -> p h d", d=16)
                tv = dve.put(tt(ov, ov, bc(k_y[:, t, :], 16), ALU.mult), tk)
                yield
            T["kf", b] = tv
            bank, over, gi = yield from grab(G)
            for t in range(2):
                for c in range(2):
                    tp = tr(bank[:, 256 * c + 128 * t:256 * c + 128 * t + 128], O[:, t, 128 * c:128 * c + 128], over, tv,
                            mark=t + c == 2)
            T["Oread", b] = tp
            yield
            te = evac(tT, bank[:, :].rearrange("p (c n) -> p c n", c=2), tp, T.get(("tTread", b - 1)))
            G.give(gi, te)
            yield
            bank, over, gi = yield from grab(G)
            for t in range(2):
                for c in range(2):
                    tp = mm(bank[:, 256 * t:256 * t + 256], tT[:, c, 128 * t:128 * t + 128], wo[:, c, :], c == 0, c == 1,
                            over, te, mark=t + c == 2)
            T["tTread", b] = tp
            yield
            for t in range(2):
                tu = dve.put(stt(UO[:, t, :], bank[:, 256 * t:256 * t + 256], sm[:, 7, t:t + 1], bo[:, :], ALU.mult, ALU.add),
                             tp, tk, T.get(("UOread",)))
                yield
            G.give(gi, tu)
            yield from finish(b, 0, X, ssX, X1, tu)
            for t in range(2):
                i = 2 * b + t
                t1 = dve.put(lambda e, i=i, t=t: e.bn_stats(bn[:, t, :], X1[:, i, :]), T["x1", b, t], T.get(("bn", t)))
                yield
                T["bn", t] = dve.put(lambda e, i=i, t=t: e.bn_aggr(mv2[:, i, :], bn[:, t, :]), t1)
                yield

        def finish(b, half, src, ssx, dst, tu):
            bank, over, gi = yield from grab(G)
            tp = mm(bank[:, 0:256], ident[0:16, b:b + 1].broadcast_to([16, 128]), grow[:, 256 * half:256 * half + 256],
                    True, True, over, T["grow"], mark=True)
            yield
            for t in range(2):
                tz = dve.put(tt(Z[:, t, :], UO[:, t, :], bank[:, 0:256], ALU.mult), tp, tu, T.get(("Zread",)))
                yield
            G.give(gi, tz)
            r0 = 10 + 0
            s = lambda i: sm[:, r0 + i, :]
            for t in range(2):
                ta = act.put(lambda e, t=t: e.activation(JK[:, t, :], UO[:, t, :], ACT.Square,
                                                         accum_out=sm[:, r0, t:t + 1]), tu, T.get(("finsm",)), act_last())
                yield
                ta = act.put(lambda e, t=t: e.activation(JK[:, t, :], Z[:, t, :], ACT.Square,
                                                         accum_out=sm[:, r0 + 1, t:t + 1]), tz, ta)
                yield
                i = 2 * b + t
                tx = dve.put(lambda e, t=t, i=i: e.tensor_tensor_reduce(out=JD[:, :], in0=src[:, i, :], in1=Z[:, t, :],
                                                                        scale=1.0, scalar=0.0, op0=ALU.mult, op1=ALU.add,
                                                                        accum_out=sm[:, r0 + 2, t:t + 1]), tz, dve_last())
                yield
            T["UOread",] = ta
            x2 = ssx[:, 2 * b:2 * b + 2]
            nn = sm[:, r0:r0 + 2, :]
            yy = sm[:, r0 + 3:r0 + 5, :]
            aa = sm[:, r0 + 5:r0 + 7, :]
            bb = sm[:, r0 + 7:r0 + 9, :]
            zz = sm[:, r0 + 9:r0 + 11, :]
            so, nz, th, psi = s(11), s(12), s(13), s(14)
            yield from chain(dve, [ts(zz, nn, 1e-30, None, ALU.max)] + rsqrt(zz, yy, aa, bb)
                             + [ts(so, s(3), CL, 1.0, ALU.mult, ALU.min), tt(nz, s(10), s(4), ALU.mult),
                                tt(nz, nz, so, ALU.mult), ts(nz, nz, EPS, None, ALU.max)], ta, tx)
            tw = act.put(lambda e: e.activation(th, nz, ACT.Tanh), dve_last())
            yield
            y2, xy, Aa, den, ca, cb = s(15), s(16), s(17), s(18), s(19), s(20)
            yield from chain(dve, [lambda e: e.reciprocal(psi, nz), tt(psi, psi, so, ALU.mult),
                                   tt(psi, psi, th, ALU.mult), tt(y2, psi, psi, ALU.mult), tt(y2, y2, s(1), ALU.mult),
                                   tt(xy, psi, s(2), ALU.mult), ts(xy, xy, 2.0, 1.0, ALU.mult, ALU.add),
                                   tt(Aa, xy, y2, ALU.add), tt(den, x2, y2, ALU.mult), tt(den, den, xy, ALU.add),
                                   ts(den, den, EPS, None, ALU.max), lambda e: e.reciprocal(cb, den),
                                   tt(ca, Aa, cb, ALU.mult), tt(cb, cb, psi, ALU.mult),
                                   ts(den, x2, -1.0, 1.0, ALU.mult, ALU.add), tt(cb, cb, den, ALU.mult)], tw, dve_last())
            tc = dve_last()
            for t in range(2):
                i = 2 * b + t
                o = dst[:, i, :]
                t1 = dve.put(ts(o, src[:, i, :], sm[:, r0 + 19, t:t + 1], None, ALU.mult), tc, T.get(("dstfree",)))
                yield
                T["x1", b, t] = dve.put(stt(o, Z[:, t, :], sm[:, r0 + 20, t:t + 1], o, ALU.mult, ALU.add), t1)
                yield
            T["Zread",] = T["finsm",] = T["x1", b, 1]

        JK2 = sb("JK2", [128, 2, 256])
        JD = sb("JD", [128, 256])
        mv2 = sb("mv2", [128, NT, 2])

        info = []
        for b in range(nb + 2):
            info.append(weave((s_att(b - 1) if 1 <= b <= nb else None, 28),
                              (s_qkv(b) if b < nb else None, 70),
                              (s_out(b - 2) if b >= 2 else None, 110)))
        program.info1 = info[min(2, len(info) - 1)]

        for _ in ln_prep(mv2[:, 0:NN, 0], mv2[:, 0:NN, 1], ssX1[:, 0:NN], rX1[:, 0:NN], NN, dve_last()):
            pass
        pe_end = pe.put(lambda e: e.matmul(bank[0:2, 100:102], ident[:, 0:2], ident[:, 0:2], start=True, stop=True),
                        dve_last(), [f[0] for f in G.free if f[0]])
        ph2 = [pe_end, dve_last(), act_last(), pool_last()]
        G.free = [(flat([f[0], ph2]), f[1]) for f in G.free]
        if taps is not None and taps.get("stop") == 1:
            return finish_up(nc, ctx, (pe, act, dve, pool, sp), loads, taps, dict(X1=X1), ph2)

        fap[0], frp[0], fwp[0] = 0, 0, 0
        QsT = [cut(FR, frp, 8, 256) for _ in range(2)]
        KsT = [cut(FR, frp, 8, 256) for _ in range(2)]
        GR = sb("GR", [128, 1536])
        GQsT = GR[:, 0:1024].rearrange("p (a n) -> p a n", a=4)
        GKsT = GR[:, 1024:1536].rearrange("p (a n) -> p a n", a=4)
        NMT = sb("NMT", [128, 256])
        PT = Ring([cut(FA, fap, 1024) for _ in range(4)])
        PT.free = [(ph2, i) for i in range(4)]
        Vg = [cut(FA, fap, 2, 16, 32) for _ in range(2)]
        GV = [cut(FA, fap, 8, 32) for _ in range(2)]
        HLs = [cut(FA, fap, 16, 4, 16) for _ in range(2)]
        OT = cut(FA, fap, 4, 256)
        OTL = cut(FA, fap, 2, 256)
        OO = cut(FA, fap, 2, 256)
        xsT = cut(FA, fap, 2, 256)
        zT = cut(FA, fap, 2, 256)
        h0p = cut(FA, fap, 2, 128)
        UG = cut(FA, fap, 2, 258)
        RL = JK2[:, 0, :].rearrange("p (t n) -> p t n", t=2)
        rT = JK2[:, 1, :]
        xn = SQ[:, 0, 0:512].rearrange("p (t n) -> p t n", t=2)
        mT = SQ[:, 1, 0:512].rearrange("p (t n) -> p t n", t=2)
        R2 = cut(FW, fwp, 1024)
        H = R2
        h0T = cut(FW, fwp, 2, 256)
        HT = cut(FW, fwp, 8, 128)
        nm = lp[:, 0:2, 0:24]
        nmhl = hall[:, 0:256].rearrange("p (t r n) -> p t r n", t=2, r=2)
        gt = [hall[:, 256 + 64 * i:320 + 64 * i].rearrange("p (t n) -> p t n", t=2) for i in range(2)]
        RW = SQ[:, 0, 512:768]
        LW = SQ[:, 1, 512:768].rearrange("p (t s a d) -> p t s a d", t=2, s=2, a=4)
        MO = [0, 320, 640, 768]

        for v in range(2):
            pool.put(lambda e, m=Vg[v]: e.memset(m, 0.0), ph2)
            a_ = pool.put(lambda e, v=v: e.memset(GV[v], 0.0), ph2)
        pool.put(lambda e: e.memset(h0p, 0.0), ph2)
        pool.put(lambda e: e.memset(nmhl, 0.0), ph2)
        for v in range(2):
            pool.put(lambda e, m=Vg[v]: e.memset(m[:, :, :, 16:17], 1.0), a_)
            pool.put(lambda e, v=v: e.memset(GV[v][:, :, 16:17], 1.0), a_)
        init2 = [ph2, pool_last(), [P_(k) for k in ("wr", "wout", "w2c", "wrt", "bg", "ltm", "wat", "wgkv", "b2")]]
        for k in [k for k in T if isinstance(k, tuple) and k[0] in ("xnT", "mTread", "sm0", "hlread", "Uread", "Zread",
                                                                   "UOread", "finsm", "scores", "pv", "OTread")]:
            T.pop(k)
        outs = []

        def maskmm(o, off, n, rep, over):
            rhs = maskb[:, off:off + n]
            if rep > 1:
                rhs = rhs.unsqueeze(1).broadcast_to([128, rep, n])
                o = o.rearrange("p (r n) -> p r n", r=rep)
            return mm(o, identb[:, :], rhs, True, False, over, init2)

        def f32r(a):
            return a.bitcast(F32R)

        def b_ffn(b):
            yield from s_mod(b, X, mv2[:, :, 0], rX1, 6, 2, init2)
            mb, mgi, tk, tp = T["mbank"]
            for t in range(2):
                bank, over, gi = yield from grab(G)
                for c in range(2):
                    tp = mm(bank[:, 0:258], mT[:, c, 128 * t:128 * t + 128], GG[:, c, :], c == 0, c == 1, over,
                            T["mT", 2, b], mark=c == 1)
                tu = acopy(UG[:, t, :], bank[:, 0:258], tp, T.get(("UGread", b - 1)))
                G.give(gi, tu)
                yield
                tq = dve.put(lambda e, t=t, mb=mb: e.tensor_tensor_reduce(
                    out=JD[:, :], in0=mb[:, 256 * t:256 * t + 256], in1=UG[:, t, 0:256], scale=1.0, scalar=0.0,
                    op0=ALU.mult, op1=ALU.add, accum_out=sm[:, 1, t:t + 1]), tu, tk, dve_last())
                yield
            G.give(mgi, [tk, tq])
            z, y, a, c_, q, k = (sm[:, i, :] for i in (2, 3, 4, 5, 6, 7))
            yield from chain(dve, [ts(z, sm[:, 0, :], EPS * EPS, None, ALU.max)] + rsqrt(z, y, a, c_)
                             + [ts(y, y, CL, 1.0, ALU.mult, ALU.min), tt(q, sm[:, 1, :], y, ALU.mult),
                                stt(q, UG[:, :, 256], 2.0, q, ALU.mult, ALU.add), tt(q, q, y, ALU.mult),
                                ts(q, q, b1w2[:, 256:257], EPS * EPS, ALU.add, ALU.max)]
                             + rsqrt(q, z, a, c_)
                             + [ts(z, z, CL, 1.0, ALU.mult, ALU.min), tt(k, z, y, ALU.mult)], T["mss", 2, b], tq)
            ck = T["sm0", 2, b] = T["UGread", b] = dve_last()
            bank, over, gi = yield from grab(G)
            for t in range(2):
                for c in range(2):
                    tp = mm(bank[:, 256 * t:256 * t + 256], mT[:, c, 128 * t:128 * t + 128], W12[:, c, :], c == 0, c == 1,
                            over, mark=t + c == 2)
            T["mTread", 2, b] = tp
            yield
            for t in range(2):
                t1 = dve.put(stt(UO[:, t, :], b1w2[:, 0:256], sm[:, 2, t:t + 1], b2[:, :], ALU.mult, ALU.add), ck,
                             P_("b2"), T.get(("UOread",)))
                yield
                tu = dve.put(stt(UO[:, t, :], bank[:, 256 * t:256 * t + 256], sm[:, 7, t:t + 1], UO[:, t, :],
                                 ALU.mult, ALU.add), t1, tp)
                yield
            G.give(gi, tu)
            yield from finish(b, 1, X, ssX1, X, tu)

        hlturn = [0]

        def split(src, n, kind, ready):
            v = hlturn[0] % 2
            hlturn[0] += 1
            hl = HLs[v][:, 0:n]
            hi, lo = hilo(hl, kind)
            sv = src.rearrange("p (h d) -> p h d", d=16).unsqueeze(2).broadcast_to([128, n, 2, 16])
            th = acopy(hi, sv, ready, T.get(("hlread", v)))
            yield
            tl = dve.put(tt(lo, sv, hl[:, :, 0, :].unsqueeze(2).broadcast_to([128, n, 2, 16]), ALU.subtract), th)
            yield
            return hl, v, tl

        def b_proj(b):
            hx = [X[:, 2 * b + t, :] for t in range(2)]
            bank, over, gi = yield from grab(G)
            for t in range(2):
                for c in range(2):
                    tp = tr(bank[:, 256 * c + 128 * t:256 * c + 128 * t + 128], hx[t][:, 128 * c:128 * c + 128], over,
                            T["x1", b, t], mark=t + c == 2)
            te = evac(h0T, bank[:, :].rearrange("p (c n) -> p c n", c=2), tp, T.get(("h0read", b - 1)))
            G.give(gi, te)
            yield
            for c in range(2):
                tp_ = dve.put(red(h0p[:, c, 0:64], h0T[:, c, :].rearrange("p (n k) -> p n k", k=4)), te, init2,
                              T.get(("h0read", b - 1)))
                yield
            bank, over, gi = yield from grab(G)
            for c in range(2):
                tp = mm(bank[:, 0:256], h0p[:, c, :], wgkv[:, c, :], c == 0, c == 1, over, tp_, mark=c == 1)
            yield
            tg = acopy(GV[b % 2][:, :, 0:16], bank[:, 128:256].rearrange("p (h d) -> p h d", d=16), tp,
                       T.get(("pvl", b - 2)))
            yield
            hl, v, tl = yield from split(bank[:, 0:128], 8, 1, tp)
            G.give(gi, [tl, tg])
            yield from need("lsc", b - 1)
            yield from stack(hl, 4, GKsT, 0, tl, T.get(("lsc", b - 1)))
            T["hlread", v] = T["stackT"]
            for t in range(2):
                ba, over, ga = yield from grab(G)
                for c in range(2):
                    tp = mm(ba[:, :], h0T[:, c, 128 * t:128 * t + 128], wat[:, c, 0:512], c == 0, c == 1, over, te,
                            mark=c == 1)
                yield
                tl = None
                for g in range(2):
                    hl, v, tl = yield from split(ba[:, 256 * g:256 * g + 256], 16, g, [tp, tl])
                    if g == 1:
                        G.give(ga, tl)
                    yield from stack(hl, 8, (QsT, KsT)[g][b % 2], t, tl, T.get(("scores", b - 2)))
                    T["hlread", v] = T["stackT"]
                bb, over, gb_ = yield from grab(G)
                for c in range(2):
                    tp = mm(bb[:, 0:416], h0T[:, c, 128 * t:128 * t + 128], wat[:, c, 512:928], c == 0, c == 1, over, te,
                            mark=c == 1)
                yield
                tv = dve.put(lambda e, t=t, bb=bb: e.tensor_copy(Vg[b % 2][:, t, :, 0:16],
                                                                 bb[:, 0:256].rearrange("p (h d) -> p h d", d=16)),
                             tp, T.get(("pv", b - 2)))
                yield
                yield from need("gtread", b - 2)
                tg2 = act.put(lambda e, t=t, bb=bb: e.activation(gt[b % 2][:, t, :], bb[:, 384:416], ACT.Exp, scale=-1.0),
                              tv, T.get(("gtread", b - 2)))
                yield
                hl, v, tl = yield from split(bb[:, 256:384], 8, 0, [tp, tv])
                G.give(gb_, [tl, tg2, tv])
                yield from stack(hl, 4, GQsT, t, tl, T.get(("lsc", b - 1)))
                T["hlread", v] = T["stackT"]
            T["h0read", b] = tp
            T["proj", b] = [act_last(), dve_last()]
            g_ = gt[b % 2]
            yield from chain(dve, [ts(g_, g_, 1.0, None, ALU.add), lambda e: e.reciprocal(g_, g_)], tg2)
            T["gt", b] = dve_last()

        def b_att(b):
            q_, k_, vg, gv = QsT[b % 2], KsT[b % 2], Vg[b % 2], GV[b % 2]
            sem = ctx.enter_context(nc.semaphore(f"d_xr{b}"))
            T["xr", b] = sp.dma(lambda e: e.dma_start(XR[b % 2][:, :, :], xv[:, 2 * b:2 * b + 2, :]), sem, 16,
                                T.get(("out", b - 2)))
            ready = T["proj", b]

            def sc(o, lk, lsl, rk, rsl, h, start, stop, *after, mark=False):
                r = 64 * (h % 2)
                return mm(o, f32r(lk[r:r + 64, h // 2, lsl]), f32r(rk[r:r + 64, h // 2, rsl]), start, stop, *after,
                          mark=mark)

            war = T.get(("nmT", b - 1))
            jobs = [("a", 0), ("a", 8)] + [("b", 4 * i) for i in range(4)] + [("l", 0)]
            for kind, h0 in jobs:
                ps, over, si = yield from grab(S2)
                for i in range(2):
                    pb = ps[:, 512 * i:512 * i + 512]
                    if kind == "a":
                        maskmm(pb, MO[0], 128, 4, over)
                        for j in range(4):
                            tp = sc(pb[:, 128 * j:128 * j + 128], q_, slice(0, 128), k_, slice(0, 128), h0 + i + 2 * j,
                                    False, True, ready, mark=j == 3)
                        o, i_ = nm[:, 0, h0 + i:h0 + 8:2], pb.rearrange("p (h n) -> p h n", h=4)
                    elif kind == "b":
                        maskmm(pb[:, 0:384], MO[0] + 128, 192, 2, over)
                        for j in range(2):
                            tp = sc(pb[:, 192 * j:192 * j + 192], q_, slice(128, 256), k_, slice(64, 256),
                                    h0 + i + 2 * j, False, True, ready, mark=j == 1)
                        o, i_ = nm[:, 1, h0 + i:h0 + 4:2], pb[:, 0:384].rearrange("p (h n) -> p h n", h=2)
                    else:
                        maskmm(pb, MO[2], 128, 4, over)
                        for j in range(4):
                            for t in range(2):
                                tp = sc(pb[:, 128 * j + 64 * t:128 * j + 64 * t + 64], GQsT,
                                        slice(128 * t, 128 * t + 128), GKsT, slice(0, 64), i + 2 * j, False, True, ready,
                                        mark=j + t == 4)
                        o = nm[:, :, 16 + i:24:2].rearrange("p t h -> p h t")
                        i_ = pb.rearrange("p (h t n) -> p h t n", h=4, t=2)
                    yield
                    tk = dve.put(red(o, i_, ALU.max, negate=True), tp, T.get(("nmhl", b - 1)))
                    yield
                S2.give(si, tk)
            n2 = nm.unsqueeze(2).broadcast_to([128, 2, 2, 24])
            th = dve.put(lambda e: e.tensor_copy(f32r(nmhl[:, :, :, 0:24]), n2), tk, war, init2)
            yield
            tl = dve.put(tt(f32r(nmhl[:, :, :, 24:48]), n2, nmhl[:, :, :, 0:24], ALU.subtract), th)
            T["nmhl", b] = tl
            bank, over, gi = yield from grab(G)
            for t in range(2):
                tp = tr(bank[:, 128 * t:128 * t + 128], nmhl[:, t].rearrange("p r n -> p (r n)"), over, tl, mark=t == 1)
            T["nmT", b] = tp
            tn = dve.put(lambda e, bank=bank: e.tensor_copy(f32r(NMT[:, :]), bank[:, 0:256]), tp,
                         T.get(("sTdone", b - 1)))
            G.give(gi, tn)
            yield

            def sub(o, h, qs, *after):
                r = 64 * (h % 2)
                return mm(o, f32r(zselr[r:r + 48, h:h + 1]).broadcast_to([48, 128]), f32r(NMT[r:r + 48, qs]), False, False,
                          *after)

            po, oover, oi = yield from grab(PO)
            for g in range(2):
                ps, over, si = yield from grab(S2)
                for i in range(2):
                    maskmm(ps[:, 512 * i:512 * i + 512], MO[3], 256, 2, over)
                    for j in range(2):
                        h = 4 * g + i + 2 * j
                        o = ps[:, 512 * i + 256 * j:512 * i + 256 * j + 256]
                        sub(o, 16 + h, slice(0, 256), tn)
                        tp = sc(o, GKsT, slice(0, 128), GQsT, slice(0, 256), h, False, True, mark=i + j == 2)
                    yield
                pt, over, pi = yield from grab(PT)
                tk = act.put(lambda e, pt=pt, ps=ps: e.activation(pt, ps[:, :], ACT.Exp, scale=0.25), tp, over)
                S2.give(si, tk)
                yield
                T["lsc", b] = tp
                for j in range(4):
                    tp = mm(po[32 * j:32 * j + 32, 256 * g:256 * g + 256], gv[:, 4 * g + j, :],
                            pt[:, 512 * (j % 2) + 256 * (j // 2):512 * (j % 2) + 256 * (j // 2) + 256], True,
                            True, oover, tk, mark=j == 3)
                PT.give(pi, tp)
                T["pvl", b] = tp
                yield
            yield from need("OTread", b - 1)
            tk = evac(OTL, po[:, :].rearrange("p (a n) -> p a n", a=2), tp, T.get(("OTread", b - 1)))
            PO.give(oi, tk)
            pend = []
            for p in range(8):
                ps, over, si = yield from grab(S2)
                for j in range(2):
                    h = 2 * p + j
                    pb = ps[:, 512 * j:512 * j + 320]
                    maskmm(pb, MO[1], 320, 1, over)
                    for o, ks, qs in ((pb[:, 0:192], slice(0, 128), slice(0, 192)),
                                      (pb[:, 192:320], slice(128, 256), slice(128, 256))):
                        sub(o, h, qs, tn)
                        tp = sc(o, k_, ks, q_, qs, h, False, True, mark=j == 1 and ks.start == 128)
                    yield
                if p == 7:
                    T["scores", b] = T["sTdone", b] = tp
                pt, over, pi = yield from grab(PT)
                tk = act.put(lambda e, pt=pt, ps=ps: e.activation(
                    pt[:, 0:640].rearrange("p (h n) -> p h n", h=2),
                    ps[:, :].rearrange("p (h n) -> p h n", h=2)[:, :, 0:320], ACT.Exp, scale=0.25), tp, over)
                S2.give(si, tk)
                pend.append((pt, pi, tk))
                yield
                if p % 2 == 1:
                    g = p // 2
                    if g % 2 == 0:
                        po, oover, oi = yield from grab(PO)
                    base = 256 * (g % 2)
                    for kt in range(2):
                        for j in range(4):
                            pt, pi, tk = pend[j // 2]
                            off = 320 * (j % 2)
                            o = po[32 * j:32 * j + 32, base:base + 192] if kt == 0 else po[32 * j:32 * j + 32, base + 128:base + 256]
                            r = pt[:, off:off + 192] if kt == 0 else pt[:, off + 192:off + 320]
                            tp = mm(o, vg[:, kt, 4 * g + j, :], r, kt == 0, kt == 1, oover, pend[1][2],
                                    mark=kt == 1 and j == 3)
                        yield
                    for pt, pi, tk in pend:
                        PT.give(pi, tp)
                    pend = []
                    T["pv", b] = tp
                    if g % 2 == 1:
                        yield from need("OTread", b - 1)
                        tk = evac(OT[:, g - 1:g + 1, :], po[:, :].rearrange("p (a n) -> p a n", a=2), tp,
                                  T.get(("OTread", b - 1)))
                        PO.give(oi, tk)
                        yield
            T["OT2", b] = [act_last(), dve_last()]
            yield

        def b_out(b):
            ready = T["OT2", b]
            xr = XR[b % 2]
            gl, gr = gt[b % 2][:, :, 0:16], gt[b % 2][:, :, 16:32]
            for t in range(2):
                bank, over, gi = yield from grab(G)
                for g in range(2):
                    tp = tr(bank[:, 128 * g:128 * g + 128], OTL[:, g, 128 * t:128 * t + 128], over, ready, mark=g == 1)
                bv = bank[:, 0:256].rearrange("p (h n) -> p h n", n=32)
                yield
                tk = dve.put(lambda e, t=t, bv=bv: e.reciprocal(k_a[:, t, 0:8], bv[:, :, 16]), tp)
                yield
                tr_ = dve.put(tt(RL[:, t, :].rearrange("p (h d) -> p h d", d=16), bv[:, :, 0:16], bc(k_a[:, t, 0:8], 16),
                                 ALU.mult), tk, T.get(("RLread",)))
                G.give(gi, tr_)
                yield
                bank, over, gi = yield from grab(G)
                for g in range(4):
                    tp = tr(bank[:, 128 * g:128 * g + 128], OT[:, g, 128 * t:128 * t + 128], over, ready, mark=g == 3)
                bv = bank[:, :].rearrange("p (h n) -> p h n", n=32)
                yield
                tk = dve.put(lambda e, t=t, bv=bv: e.reciprocal(k_b[:, t, :], bv[:, :, 16]), tp)
                yield
                tk = dve.put(tt(k_b[:, t, :], k_b[:, t, :], gl[:, t, :], ALU.mult), tk, T["gt", b])
                yield
                to = dve.put(tt(OO[:, t, :].rearrange("p (h d) -> p h d", d=16), bv[:, :, 0:16], bc(k_b[:, t, :], 16),
                                ALU.mult), tk, T.get(("OOread",)))
                G.give(gi, to)
                yield
            T["OTread", b] = tp
            bank, over, gi = yield from grab(G)
            for t in range(2):
                tp = tr(bank[:, 128 * t:128 * t + 128], RL[:, t, :], over, tr_, mark=t == 1)
            T["RLread",] = tp
            te = evac(rT, bank[:, 0:256], tp, T.get(("rTread",)))
            G.give(gi, te)
            yield
            bank, over, gi = yield from grab(G)
            for t in range(2):
                tp = mm(bank[:, 256 * t:256 * t + 256], rT[:, 128 * t:128 * t + 128], wr[:, :], True, True, over, te,
                        mark=t == 1)
            T["rTread",] = tp
            yield
            for t in range(2):
                bv = bank[:, 256 * t:256 * t + 256].rearrange("p (h d) -> p h d", d=16)
                t1 = dve.put(tt(xsT[:, t, :].rearrange("p (h d) -> p h d", d=16), bv, bc(gr[:, t, :], 16), ALU.mult), tp,
                             T.get(("xsread",)))
                yield
                to = dve.put(tt(OO[:, t, :], OO[:, t, :], xsT[:, t, :], ALU.add), t1)
                yield
            T["gtread", b] = to
            G.give(gi, to)
            bank, over, gi = yield from grab(G)
            for t in range(2):
                for c in range(2):
                    tp = tr(bank[:, 256 * c + 128 * t:256 * c + 128 * t + 128], OO[:, t, 128 * c:128 * c + 128], over, to,
                            mark=t + c == 2)
            T["OOread",] = tp
            te = evac(xsT, bank[:, :].rearrange("p (c n) -> p c n", c=2), tp, to, T.get(("xsread",)))
            G.give(gi, te)
            yield
            bank, over, gi = yield from grab(G)
            for t in range(2):
                for c in range(2):
                    tp = mm(bank[:, 256 * t:256 * t + 256], xsT[:, c, 128 * t:128 * t + 128], wout[:, c, :], c == 0,
                            c == 1, over, te, mark=t + c == 2)
            yield
            tx = dve.put(tt(xr[:, :, :], xr[:, :, :], bank[:, :].rearrange("p (t n) -> p t n", t=2), ALU.add), tp,
                         T["xr", b])
            G.give(gi, tx)
            yield
            bank, over, gi = yield from grab(G)
            for t in range(2):
                for c in range(2):
                    tq = tr(bank[:, 256 * c + 128 * t:256 * c + 128 * t + 128], xr[:, t, 128 * c:128 * c + 128], over, tx,
                            mark=t + c == 2)
            yield
            for c in range(2):
                te = act.put(lambda e, c=c, bank=bank: e.activation(xsT[:, c, :], bank[:, 256 * c:256 * c + 256], ACT.Copy,
                                                                    scale=ysT[:, c, b:b + 1]), tq, tp)
                yield
            G.give(gi, te)
            bank, over, gi = yield from grab(G)
            for oc in range(2):
                for c in range(2):
                    tp = mm(bank[:, 256 * oc:256 * oc + 256], w2c[:, c, 128 * oc:128 * oc + 128], xsT[:, c, :], c == 0,
                            c == 1, over, te, mark=oc + c == 2)
            T["xsread",] = tp
            yield
            for oc in range(2):
                te = act.put(lambda e, oc=oc, bank=bank: e.activation(zT[:, oc, :], bank[:, 256 * oc:256 * oc + 256],
                                                                      ACT.Copy, scale=dT[:, oc, b:b + 1]), tp,
                             T.get(("zread",)))
                yield
            G.give(gi, te)
            bank, over, gi = yield from grab(G)
            for t in range(2):
                for c in range(2):
                    tp = mm(bank[:, 20 * t:20 * t + 20], zT[:, c, 128 * t:128 * t + 128], wrt[:, c, :], c == 0, c == 1,
                            over, te, mark=t + c == 2)
            yield
            rv = bank[:, 0:40].rearrange("p (t n) -> p t n", t=2)

            def w(i, *shape):
                a = RW[:, i:i + int(np.prod(shape))]
                if len(shape) == 1:
                    return a
                names = "abc"[:len(shape)]
                return a.rearrange(f"p ({' '.join(names)}) -> p {' '.join(names)}",
                                   **{names[i]: shape[i] for i in range(1, len(shape))})

            lg, mx, pr, cm, eq = w(0, 2, 4), w(8, 2), w(10, 2, 4), w(18, 2, 4, 4), w(50, 2, 4, 4)
            rk, oh, w12, lf = w(82, 2, 4), w(90, 2, 2, 4), w(106, 2, 2), w(110, 2, 2, 16)
            rho, sm_, tmp = w(174, 2), w(176, 2), w(178, 2, 2, 4)
            yield from chain(dve, [tt(lg, rv[:, :, 0:4], bg[:, :].unsqueeze(1).broadcast_to([128, 2, 4]), ALU.add),
                                   red(mx, lg, ALU.max, negate=True), tt(lg, lg, bc(mx, 4), ALU.add)], tp,
                             T.get(("rwread",)))
            ta = act.put(lambda e: e.activation(pr, lg, ACT.Exp), dve_last())
            yield
            pj = pr.unsqueeze(2).broadcast_to([128, 2, 4, 4])
            lt4 = ltm[:, :].rearrange("p (i j) -> p i j", j=4)
            fns = [red(sm_, pr), lambda e: e.reciprocal(sm_, sm_), tt(pr, pr, bc(sm_, 4), ALU.mult),
                   tt(cm, pj, bc(pr, 4), ALU.is_gt), tt(eq, pj, bc(pr, 4), ALU.is_equal)]
            fns += [tt(eq[:, t], eq[:, t], lt4, ALU.mult) for t in range(2)]
            fns += [tt(cm, cm, eq, ALU.add), red(rk, cm), ts(oh[:, :, 0, :], rk, 0.0, None, ALU.is_equal),
                    ts(oh[:, :, 1, :], rk, 1.0, None, ALU.is_equal),
                    tt(tmp, oh, pr.unsqueeze(2).broadcast_to([128, 2, 2, 4]), ALU.mult), red(w12, tmp),
                    lambda e: e.reciprocal(rho, w12[:, :, 0]), tt(rho, rho, w12[:, :, 1], ALU.mult),
                    tt(oh[:, :, 0, :], oh[:, :, 0, :], oh[:, :, 1, :], ALU.subtract)]
            lw4 = lf.rearrange("p t s (e r) -> p t s e r", r=4)
            lo4 = rv[:, :, 4:20].rearrange("p t (e r) -> p t e r", r=4)
            for t in range(2):
                fns += [tt(lw4[:, t, s_], lo4[:, t], bc(oh[:, t, 1 - s_, :], 4), ALU.mult) for s_ in range(2)]
            yield from chain(dve, fns, ta)
            G.give(gi, dve_last())
            hi, lo = LW[:, :, :, 0:2, :].rearrange("p t s a d -> p (t s) a d"), \
                LW[:, :, :, 2:4, :].rearrange("p t s a d -> p (t s) a d")
            lfb = lf.rearrange("p t s d -> p (t s) d").unsqueeze(2).broadcast_to([128, 4, 2, 16])
            yield from chain(dve, [lambda e: e.tensor_copy(f32r(hi), lfb), tt(f32r(lo), lfb, hi, ALU.subtract)],
                             dve_last(), T.get(("LWread",)))
            tl = dve_last()
            for t in range(2):
                bank, over, gi = yield from grab(G)
                tp = tr(bank[:, 0:128], LW[:, t].rearrange("p s a d -> p (s a d)"), over, tl, mark=True)
                T["LWread",] = tp
                te = acopy(f32r(LT[:, :]), bank[:, 0:128], tp, T.get(("LTread",)))
                G.give(gi, te)
                yield
                ps, over, si = yield from grab(S2)
                for hf in range(2):
                    o = ps[:, 512 * hf:512 * hf + 512]
                    for c in range(2):
                        mm(o, zT[:, c, 128 * t:128 * t + 128], WiT[:, c, 512 * hf:512 * hf + 512], c == 0, False, over,
                           P_("WiT"))
                    tp = mm(o, f32r(LT[0:64, :]), f32r(Bst[0:64, 512 * hf:512 * hf + 512]), False, True,
                            te, mark=hf == 1)
                    yield
                ta = act.put(lambda e, t=t, ps=ps: e.activation(R2, ps[:, :], ACT.Relu, scale=rho[:, t:t + 1]), tp,
                             T.get(("Hread",)))
                yield
                for hf in range(2):
                    o = ps[:, 512 * hf:512 * hf + 512]
                    tp = mm(o, f32r(LT[64:128, :]), f32r(Bst[64:128, 512 * hf:512 * hf + 512]), False,
                            True, ta, mark=hf == 1)
                T["LTread",] = tp
                yield
                th = dve.put(stt(H, ps[:, :], 0.0, R2, ALU.max, ALU.add), tp, ta)
                S2.give(si, th)
                yield
                tes = []
                for q4 in range(2):
                    bank, over, gi = yield from grab(G)
                    for j in range(4):
                        tp = tr(bank[:, 128 * j:128 * j + 128], H[:, 512 * q4 + 128 * j:512 * q4 + 128 * j + 128], over,
                                th, mark=j == 3)
                    te2 = evac(HT[:, 4 * q4:4 * q4 + 4, :], bank[:, :].rearrange("p (a n) -> p a n", a=4), tp,
                               T.get(("HTread",)))
                    tes.append(te2)
                    G.give(gi, te2)
                    yield
                T["Hread",] = tp
                bank, over, gi = yield from grab(G)
                for c in range(8):
                    tp = mm(bank[:, 0:256], HT[:, c, :], WoT[:, c, :], c == 0, c == 7, over, tes, P_("WoT"), mark=c == 7)
                T["HTread",] = tp
                yield
                tx = dve.put(stt(xr[:, t, :], bank[:, 0:256], w12[:, t, 0:1], xr[:, t, :], ALU.mult, ALU.add), tp, tx, tq)
                G.give(gi, tx)
                yield
            T["zread",] = tp
            T["rwread",] = tx
            sem = ctx.enter_context(nc.semaphore(f"d_out{b}"))
            T["out", b] = sp.dma(lambda e, xr=xr: e.dma_start(
                out[b].rearrange("(t p) d -> p t d", p=128), xr[:, :, :]), sem, 16, tx)
            outs.append(T["out", b])
            yield

        def b_first(b):
            yield from b_ffn(b)
            yield from b_proj(b)

        LT = sb("LT", [128, 128])
        for b in range(nb + 2):
            info = weave((b_att(b - 1) if 1 <= b <= nb else None, 80),
                         (b_first(b) if b < nb else None, 150),
                         (b_out(b - 2) if b >= 2 else None, 110))
        program.info2 = info
        sp.ops.append((lambda e: e.nop(), flat(outs), None))
        run_lanes(nc, ctx, (pe, act, dve, pool, sp))


def finish_up(nc, ctx, lanes, loads, taps, bufs, done):
    pe, act, dve, pool, sp = lanes
    n = 0
    for name, ap in taps["out"]:
        sem = ctx.enter_context(nc.semaphore(f"d_tap{name}"))
        src = bufs[name]
        n += 1
        tok = sp.dma(lambda e, ap=ap, src=src: e.dma_start(ap, src[:]), sem, 16, done)
        sp.ops.append((lambda e: e.nop(), flat(tok), None))
    run_lanes(nc, ctx, lanes)


def run_lanes(nc, ctx, lanes):
    pe, act, dve, pool, sp = lanes
    block = ctx.enter_context(nc.Block())

    @block.tensor
    def _(e):
        pe.play(e)

    @block.scalar
    def _(e):
        act.play(e)

    @block.vector
    def _(e):
        dve.play(e)

    @block.gpsimd
    def _(e):
        pool.play(e)

    @block.sync
    def _(e):
        sp.play(e)


def _inputs(inp):
    f = lambda k: np.asarray(inp[k])
    T_ = lambda a: np.ascontiguousarray(a.T)
    cat = lambda *a: np.ascontiguousarray(np.concatenate(a, axis=-1))
    q = np.arange(128)
    neg = np.float32(-1e30)

    def allow(m):
        return np.where(m, np.float32(0), neg).astype(np.float32)

    k0 = np.arange(128)
    m_t0 = allow((k0[None] <= q[:, None]) & (k0[None] > q[:, None] - 64))
    k1 = 64 + np.arange(192)
    m_t1 = allow((k1[None] <= 128 + q[:, None]) & (k1[None] > 128 + q[:, None] - 64))
    qa = np.arange(192)
    m_k0 = allow((qa[None] >= q[:, None]) & (qa[None] < q[:, None] + 64))
    qb = np.arange(128)
    m_k1 = allow((qb[None] >= q[:, None]) & (qb[None] < q[:, None] + 64))
    lat = np.arange(64)
    m_l = [allow(lat[None] <= (128 * t + q[:, None]) // 4) for t in range(2)]
    ql = np.arange(256)
    m_lt = allow((q[:, None] <= ql[None] // 4) & (q[:, None] < 64))
    masks = cat(m_t0, m_t1, m_k0, m_k1, m_l[0], m_l[1], m_lt)
    zsel = np.zeros((128, 24), np.float32)
    for r in (0, 24, 64, 88):
        zsel[r + np.arange(24), np.arange(24)] = 1
    hs = np.zeros((128, 2), np.float32)
    hs[:, 0] = (np.arange(128) // 16) % 2 == 0
    hs[:, 1] = 1 - hs[:, 0]
    ltm = np.array([[1.0 if j < i else 0.0 for j in range(4)] for i in range(4)], np.float32).reshape(16)
    c = "L0_cond_"
    a = "L0_attn_"
    w = "L0_ffn_"
    return {
        "x": f("x"), "condT": T_(f("cond_1024")), "ident": np.eye(128, dtype=np.float32), "masks": masks,
        "zsel": zsel, "hsel": hs, "ltm": ltm,
        "w_ada": f(c + "w_ada"), "b_ada": f(c + "b_ada"), "badaT": T_(f(c + "b_ada").reshape(12, 128)),
        "wqkv": cat(f(c + "w_q"), f(c + "w_k"), f(c + "w_v")), "bqkv": cat(f(c + "b_q"), f(c + "b_k"), f(c + "b_v")),
        "w_o": f(c + "w_o"), "b_o": f(c + "b_o"), "w1T": T_(f(c + "w_f1")), "b1c": T_(f(c + "b_f1").reshape(8, 128)),
        "w2": f(c + "w_f2"), "b_f2": f(c + "b_f2"),
        "wat": cat(f(a + "wq"), f(a + "wk"), f(a + "wv"), f(a + "wgq")), "wgkv": cat(f(a + "wgk"), f(a + "wgv")),
        "gl": f(a + "gate_local_w").reshape(256), "gr": f(a + "gate_remote_w").reshape(256),
        "r_out_w": f(a + "r_out_w"), "w_out": f(a + "w_out"), "weight": f("L0_cond2_weight"),
        "wrt": cat(T_(f(w + "Wg")), T_(f(w + "A").reshape(16, 256))), "bg": f(w + "bg"),
        "WiT": T_(f(w + "Wi")), "WoT": T_(f(w + "Wo")),
        "Bc": np.ascontiguousarray(np.transpose(f(w + "B"), (0, 2, 1)).reshape(16, 1024)),
    }


_OUT = (NB, S, D)


def kernel(**inputs):
    import concourse.bacc as _bacc
    from concourse.bass_utils import run_bass_kernel_spmd as _run

    nc = _bacc.Bacc("TRN2", target_bir_lowering=False, num_devices=1)
    arrays, args = {}, {}
    for name, a in _inputs(inputs).items():
        arrays[f"in_{name}"] = a
        args[name] = nc.dram_tensor(f"in_{name}", a.shape, F32, kind="ExternalInput").ap()
    o = nc.dram_tensor("out_0", _OUT, F32, kind="ExternalOutput").ap()
    program(nc, args, o)
    r = _run(nc, [arrays], core_ids=[0])
    return r.results[0]["out_0"]
```

```python
import math
from contextlib import ExitStack

import numpy as np

import concourse.bass as bass
from concourse import mybir

F32 = mybir.dt.float32
F32R = mybir.dt.float32r
BF16 = mybir.dt.bfloat16
I32 = mybir.dt.int32
ALU = mybir.AluOpType
ACT = mybir.ActivationFunctionType
AX = mybir.AxisListType

NB, S, D, FF = 16, 256, 256, 1024
NT = 2 * NB
EPS = 1e-7
TMAX = float(np.float32(1.0 - 1e-5))
CL = math.atanh(TMAX)


def _beta(a, b):
    return math.exp(math.lgamma(a) + math.lgamma(b) - math.lgamma(a + b))


RT = _beta(8, 0.5) / _beta(128, 0.5)


class Lane:

    done, latest = {}, 0

    def __init__(self, nc, ctx, name, usual=100, limit=16000):
        self.free, self.usual = 0, usual
        self.nc, self.ctx, self.name, self.limit = nc, ctx, name, limit
        self.ops, self.count, self.turn = [], limit, 0

    def put(self, fn, *after, mark=True, cost=None):
        after = flat(after)
        start = max([self.free] + [Lane.done.get((s.name, v), 0) + 70 for s, v in after])
        self.free = start + (self.usual if cost is None else cost)
        Lane.latest = max(Lane.latest, self.free)
        token = None
        if mark:
            if self.count >= self.limit:
                self.sem = self.ctx.enter_context(self.nc.semaphore(f"s_{self.name}{self.turn}"))
                self.turn += 1
                self.count = 0
            self.count += 1
            token = (self.sem, self.count)
            Lane.done[self.sem.name, self.count] = self.free
        self.ops.append((fn, after, token))
        return token

    def dma(self, fn, sem, value, *after):
        self.ops.append((fn, flat(after), (sem, 16)))
        return (sem, value)

    def play(self, eng):
        seen = {}
        for fn, after, token in self.ops:
            for sem, value in after:
                if seen.get(sem.name, 0) < value:
                    seen[sem.name] = value
                    eng.wait_ge(sem, value)
            ins = fn(eng)
            if token is not None:
                ins.then_inc(token[0], 16 if token[1] == 16 and "d_" in token[0].name else 1)


def flat(x):
    if x is None:
        return []
    if isinstance(x, tuple) and len(x) == 2 and isinstance(x[1], int) and not isinstance(x[0], (tuple, list)):
        return [x]
    return [t for y in x for t in flat(y)]


class Ring:

    def __init__(self, tiles):
        self.tiles, self.free = tiles, [(None, i) for i in range(len(tiles))]

    def take(self):
        assert self.free, "no tile is free"
        over, i = self.free.pop(0)
        return self.tiles[i], over, i

    def give(self, i, *over):
        self.free.append((flat(over), i))


def grab(ring):
    while not ring.free:
        yield None
    when = max([Lane.done.get((t[0].name, t[1]), 0) for t in flat(ring.free[0][0])] + [0])
    yield when - 100
    while not ring.free:
        yield None
    return ring.take()


def weave(*threads):
    start = max([0] + [Lane.latest])
    live = [[start, i, g, False] for i, g in enumerate(threads)]
    idle = 0
    while live:
        live.sort(key=lambda x: x[:2])
        s = live[0]
        Lane.latest = 0
        try:
            hint = next(s[2])
        except StopIteration:
            live.pop(0)
            idle = 0
            continue
        if Lane.latest:
            s[0], s[3], idle = Lane.latest, False, 0
        elif isinstance(hint, (int, float)) and hint > s[0]:
            s[0], s[3] = hint, False
        elif isinstance(hint, (int, float)):
            idle = 0
        else:
            idle += 1
            assert idle < 50 * len(live), "the stages wait for each other"
            s[3] = True
            s[0] = max(s[0], min([x[0] for x in live if not x[3]] or [s[0]])) + 1


def program(nc, A, out, nb=NB, taps=None):
    ctx = ExitStack()
    with ctx:
        def sb(name, shape, dt=F32):
            return ctx.enter_context(nc.sbuf_tensor(name, shape, dt))

        pe, act, dve, pool, sp = (
            Lane(nc, ctx, *n) for n in (("pe", 100), ("act", 400), ("dve", 300), ("pool", 1200), ("sp", 0)))
        Lane.done, Lane.latest = {}, 0
        loads = {}

        def load(name, dst, src, lane=sp, *after):
            sem = ctx.enter_context(nc.semaphore(f"d_{name}"))
            loads[name] = lane.dma(lambda e: e.dma_start(dst, src), sem, 16, *after)
            return loads[name]

        S2 = Ring([ctx.enter_context(nc.psum_tensor(f"pS{i}", [128, 1024], F32)) for i in range(2)])
        PO = Ring([ctx.enter_context(nc.psum_tensor("pO", [128, 512], F32))])
        G = Ring([ctx.enter_context(nc.psum_tensor(f"pG{i}", [128, 512], F32)) for i in range(3)])

        X = sb("X", [128, NT, D])
        X1 = X
        GR = sb("GR", [128, 1536])
        XR = [sb(f"XR{i}", [128, 2, D]) for i in range(2)]
        ident = sb("ident", [128, 128])
        identb = sb("identb", [128, 128], BF16)
        identr = sb("identr", [128, 128])
        maskb = sb("maskb", [128, 320 + 320 + 128 + 256], BF16)
        zsel = sb("zsel", [128, 24])
        zselr = sb("zselr", [128, 24])
        hsel = sb("hsel", [128, 2])
        condT = sb("condT", [128, 2, 16])
        adaT = sb("adaT", [128, 12, 16])
        badaT = sb("badaT", [128, 12])
        grow = sb("grow", [16, 512])
        b2 = sb("b2", [128, D])
        b1w2 = sb("b1w2", [128, 258])
        W12 = sb("W12", [128, 2, 256])
        GG = sb("GG", [128, 2, 258])
        wat = sb("wat", [128, 2, 928])
        wgkv = sb("wgkv", [128, 2, 256])
        wr = sb("wr", [128, D])
        wout = sb("wout", [128, 2, D])
        w2c = sb("w2c", [128, 2, D])
        dT = sb("dT", [128, 2, 16])
        ysT = sb("ysT", [128, 2, 16])
        WiT = sb("WiT", [128, 2, FF])
        WoT = sb("WoT", [128, 8, D])
        wrt = sb("wrt", [128, 2, 20])
        bg = sb("bg", [128, 4])
        ltm = sb("ltm", [128, 16])
        Bst = sb("Bst", [128, FF])
        mv = sb("mv", [128, NT, 2])
        bn = sb("bn", [128, 4, 6])
        rX, ssX, rX1, ssX1 = (sb(n, [128, NT]) for n in ("rX", "ssX", "rX1", "ssX1"))
        lp = sb("lp", [128, 10, NT])
        FR = sb("FR", [128, 8192])
        FA = sb("FA", [128, 10752])
        RND = sb("RND", [128, 2048])

        frp, fap = [0], [0]

        FW = sb("FW", [128, 3072])
        SQ = sb("SQ", [128, 2, 768])
        fwp = [0]

        def cut(arena, ptr, *shape):
            n = int(np.prod(shape))
            a = arena[:, ptr[0]:ptr[0] + n]
            ptr[0] += n
            assert ptr[0] <= arena.shape[1], (ptr, arena.shape)
            names = "abcdef"[:len(shape)]
            if len(shape) == 1:
                return a
            kw = {names[i]: shape[i] for i in range(1, len(shape))}
            return a.rearrange(f"p ({' '.join(names)}) -> p {' '.join(names)}", **kw)

        def bc(ap, n):
            shape = list(ap.shape)
            return ap.unsqueeze(len(shape)).broadcast_to(shape + [n])

        def chain(lane, fns, *after):
            tok = after
            for fn in fns:
                tok = lane.put(fn, tok, cost=110)
                yield

        def size(ap):
            return int(np.prod(ap.shape[1:]))

        def thread(fn, name, before, *free):
            for b in range(nb):
                if before:
                    yield from need(before, b)
                for kind, lag in free:
                    yield from need(kind, b - lag)
                yield from fn(b)
                T[name, b] = True

        def need(kind, b):
            while b >= 0 and (kind, b) not in T:
                yield

        def ts(o, i, s1, s2, op0, op1=None):
            if op1 is None:
                return lambda e: e.tensor_scalar(o, i, s1, None, op0)
            return lambda e: e.tensor_scalar(o, i, s1, s2, op0, op1)

        def tt(o, a, b, op):
            return lambda e: e.tensor_tensor(o, a, b, op)

        def stt(o, a, s, b, op0, op1):
            return lambda e: e.scalar_tensor_tensor(out=o, in0=a, scalar=s, in1=b, op0=op0, op1=op1)

        def red(o, i, op=ALU.add, negate=False):
            return lambda e: e.tensor_reduce(o, i, AX.X, op, negate=negate)

        def rsqrt(x, y, a, b):
            fns = [ts(a.bitcast(I32), x.bitcast(I32), 1, None, ALU.logical_shift_right),
                   ts(y.bitcast(I32), a.bitcast(I32), -1.0, float(0x5F3759DF), ALU.mult, ALU.add)]
            for _ in range(3):
                fns += [tt(a, y, y, ALU.mult), stt(b, a, -0.5, x, ALU.mult, ALU.mult),
                        stt(y, b, 1.5, y, ALU.add, ALU.mult)]
            return fns

        def mm(o, lhsT, rhs, start, stop, *after, mark=False):
            passes = 4 if rhs.dtype == F32 else 1
            cost = max(passes * size(rhs), 128 * passes) / 2.4 / (4 if lhsT.shape[-1] == 32 else 1)
            return pe.put(lambda e: e.matmul(o, lhsT, rhs, start=start, stop=stop, skip_group_check=True),
                          *after, mark=mark, cost=cost)

        def tr(o, i, *after, mark=False):
            return pe.put(lambda e: e.transpose(o, i, ident[:, :]), *after, mark=mark)

        def acopy(o, i, *after):
            return act.put(lambda e: e.activation(o, i, ACT.Copy), *after)

        turn = [0]

        def evac(o, i, *after):
            turn[0] += 1
            if turn[0] % 3 == 0:
                return dve.put(lambda e: e.tensor_copy(o, i), *after)
            return acopy(o, i, *after)

        wqkv, bqkv, wo, bo = (cut(FW, fwp, *n) for n in ((2, 768), (768,), (2, D), (D,)))

        xv = A["x"].rearrange("b (t p) d -> p (b t) d", p=128)
        load("cond", condT[:, :, :], A["condT"].rearrange("(c p) b -> p c b", p=128))
        load("ident", ident[:, :], A["ident"])
        for q in range(4):
            load(f"x{q}", X[:, 8 * q:8 * q + 8, :], xv[:, 8 * q:8 * q + 8, :], act if q % 2 else sp)
        wada = cut(FA, [0], 2, 1536)
        w1T = cut(FA, [3584], 8, 258)
        w2x = cut(FA, [3584 + 2064], 8, 256)
        b1c = cut(FA, [3584 + 2048 + 2064], 8)
        gate = cut(FA, [3584 + 2048 + 2064 + 16], 2, 256)
        mf = cut(FA, [3584 + 2048 + 2064 + 16 + 512], 1024)
        gtmp = cut(FA, [3584 + 2048 + 2064 + 16 + 512 + 1024], 2, 2, 256)
        Bf = cut(FA, [1024], 1024)
        Bh = cut(FA, [0], 1024)
        w2sq = cut(FA, [3072], 2, 256)
        brow = SQ[0:16, 0, 0:512]
        load("wada", wada, A["w_ada"].rearrange("(c p) n -> p c n", p=128))
        load("bada", badaT[:, :], A["badaT"])
        load("brow0", brow[:, 0:256], A["b_ada"][512:768].partition_broadcast(16))
        load("brow1", brow[:, 256:512], A["b_ada"][1280:1536].partition_broadcast(16))
        load("wqkv", wqkv, A["wqkv"].rearrange("(c p) n -> p c n", p=128))
        load("bqkv", bqkv[:, :], A["bqkv"].partition_broadcast(128))
        load("w1T", w1T[:, :, 0:256], A["w1T"].rearrange("(c p) n -> p c n", p=128))
        load("w2", w2x, A["w2"].rearrange("(c p) n -> p c n", p=128), act)
        load("b1c", b1c, A["b1c"], act)
        load("wo", wo, A["w_o"].rearrange("(c p) n -> p c n", p=128))
        load("bo", bo[:, :], A["b_o"].partition_broadcast(128))
        load("mf", mf, A["masks"], act)
        load("zsel", zsel[:, :], A["zsel"], act)
        load("hsel", hsel[:, :], A["hsel"], act)
        load("ltm", ltm[:, :], A["ltm"].partition_broadcast(128), act)
        load("b2", b2[:, :], A["b_f2"].partition_broadcast(128), act)
        load("wat", wat[:, :, 0:896], A["wat"].rearrange("(c p) n -> p c n", p=128))
        load("wgkv", wgkv[:, :, :], A["wgkv"].rearrange("(c p) n -> p c n", p=128))
        load("gate0", gate[:, 0, :], A["gl"].partition_broadcast(128), act)
        load("gate1", gate[:, 1, :], A["gr"].partition_broadcast(128), act)
        load("wr", wr[:, :], A["r_out_w"])
        load("wout", wout[:, :, :], A["w_out"].rearrange("(c p) n -> p c n", p=128))
        load("w2c", w2c[:, :, :], A["weight"].rearrange("(c p) n -> p c n", p=128), act)
        load("wrt", wrt[:, :, :], A["wrt"].rearrange("(c p) n -> p c n", p=128), act)
        load("bg", bg[:, :], A["bg"].partition_broadcast(128), act)
        load("WiT", WiT[:, :, :], A["WiT"].rearrange("(c p) n -> p c n", p=128))
        load("WoT", WoT[:, :, :], A["WoT"].rearrange("(c p) n -> p c n", p=128))

        def ln_prep(mean, var, ss, r, n, *after):
            a, b, y, t, z, p, q, m = (lp[:, i, 0:n] for i in range(8))
            yield from chain(dve, [
                tt(a, mean, mean, ALU.mult), tt(a, a, var, ALU.add),
                ts(ss, a, 256.0, 0.0, ALU.mult, ALU.add), ts(z, ss, EPS * EPS, None, ALU.max)], *after)
            yield from chain(dve, rsqrt(z, y, a, b), dve_last())
            yield from chain(dve, [tt(t, z, y, ALU.mult), ts(t, t, TMAX, None, ALU.min),
                                   ts(q, t, -1.0, 1.0, ALU.mult, ALU.add)], dve_last())
            yield from chain(dve, [lambda e: e.reciprocal(b, q), stt(q, t, 1.0, b, ALU.add, ALU.mult)], dve_last())
            tok = act.put(lambda e: e.activation(p, q, ACT.Ln), dve_last())
            yield from chain(dve, [
                tt(z, t, t, ALU.mult), ts(a, z, 1.0 / 11, None, ALU.mult),
                stt(a, a, 1.0 / 9, z, ALU.add, ALU.mult), stt(a, a, 1.0 / 7, z, ALU.add, ALU.mult),
                stt(a, a, 1.0 / 5, z, ALU.add, ALU.mult), stt(a, a, 1.0 / 3, z, ALU.add, ALU.mult),
                stt(a, a, 1.0, t, ALU.add, ALU.mult), ts(m, t, 0.25, None, ALU.is_lt),
                stt(a, p, -0.5, a, ALU.mult, ALU.add), tt(a, a, m, ALU.mult),
                stt(a, p, 0.5, a, ALU.mult, ALU.add), tt(q, a, y, ALU.mult),
                tt(a, q, q, ALU.mult), tt(a, a, var, ALU.mult), ts(z, a, 1e-6, None, ALU.add)], dve_last(), tok)
            yield from chain(dve, rsqrt(z, y, a, b), dve_last())
            yield from chain(dve, [tt(r, q, y, ALU.mult)], dve_last())

        def dve_last():
            return (dve.sem, dve.count)

        def act_last():
            return (act.sem, act.count)

        def pool_last():
            return (pool.sem, pool.count)

        T = {}
        for q in range(4):
            for i in range(8 * q, 8 * q + 8):
                if i >= 2 * nb:
                    continue
                k = i % 4
                t1 = dve.put(lambda e, i=i, k=k: e.bn_stats(bn[:, k, :], X[:, i, :]), loads[f"x{q}"], T.get(("bn", k)))
                T["bn", k] = dve.put(lambda e, i=i, k=k: e.bn_aggr(mv[:, i, :], bn[:, k, :]), t1)
        NN = 2 * nb
        for _ in ln_prep(mv[:, 0:NN, 0], mv[:, 0:NN, 1], ssX[:, 0:NN], rX[:, 0:NN], NN, T["bn", (NN - 1) % 4]):
            pass
        nmean = dve_last()

        def P_(t):
            return loads[t]

        tb = pool.put(lambda e: e.tensor_copy(identb[:, :], ident[:, :]), P_("ident"))
        pool.put(lambda e: e.tensor_copy(identr[:, :].bitcast(F32R), ident[:, :]), P_("ident"))
        tb = pool.put(lambda e: e.tensor_copy(maskb[:, :], mf), P_("mf"))
        pool.put(lambda e: e.tensor_copy(zselr[:, :].bitcast(F32R), zsel[:, :]), P_("zsel"))
        pool.put(lambda e: e.tensor_scalar(wgkv[:, :, :], wgkv[:, :, :], 0.25, None, ALU.mult), P_("wgkv"))
        t1 = pool.put(lambda e: e.memset(w1T[:, :, 257:258], 0.0))
        tb = pool.put(lambda e: e.tensor_copy(w1T[:, :, 256:257], b1c.unsqueeze(2)), P_("b1c"))
        consts = pool_last()

        bank, over, gi = G.take()
        for j in range(12):
            for c in range(2):
                t1 = mm(bank[:, 16 * j:16 * j + 16], wada[:, c, 128 * j:128 * j + 128], condT[:, c, :], c == 0, c == 1,
                        P_("wada"), P_("cond"), mark=j == 11 and c == 1)
        for j in range(12):
            o, i = adaT[:, j, :], bank[:, 16 * j:16 * j + 16]
            if j in (2, 3, 8, 9):
                t2 = dve.put(ts(o, i, badaT[:, j:j + 1], 1.0, ALU.add, ALU.add), t1, P_("bada"))
            else:
                t2 = dve.put(ts(o, i, badaT[:, j:j + 1], None, ALU.add), t1, P_("bada"))
        G.give(gi, t2)
        bank, over, gi = G.take()
        wg2 = wada.rearrange("p c (s k n) -> p c s k n", s=2, k=3)[:, :, :, 2, :]
        for c in range(2):
            t1 = mm(bank[0:16, :].rearrange("p (s n) -> p s n", s=2), condT[:, c, :], wg2[:, c], c == 0, c == 1, over,
                    mark=c == 1)
        T["grow"] = dve.put(tt(grow[:, :], bank[0:16, :], brow[:, :], ALU.add), t1, P_("brow0"), P_("brow1"))
        wada_read = t1
        for r in range(8):
            load(f"B{r}", Bf[16 * r:16 * r + 16, :], A["Bc"], sp, wada_read)
        G.give(gi, T["grow"])

        for ic in range(2):
            for dst, w, n in ((W12, w2x, 256), (GG, w1T, 258)):
                bank, over, gi = G.take()
                for f in range(8):
                    t1 = mm(bank[:, 0:n], w1T[:, f, 128 * ic:128 * ic + 128], w[:, f, 0:n], f == 0, f == 7, over,
                            P_("w1T"), P_("w2"), consts, mark=f == 7)
                t2 = evac(dst[:, ic, :], bank[:, 0:n], t1)
                G.give(gi, t2)
                T["w12", ic, n] = t2
        bank, over, gi = G.take()
        for f in range(8):
            t1 = mm(bank[:, 0:256], b1c[:, f:f + 1].broadcast_to([128, 128]), w2x[:, f, :], f == 0, f == 7, over)
        for f in range(8):
            t1 = mm(bank[:, 256:258], b1c[:, f:f + 1].broadcast_to([128, 128]), w1T[:, f, 256:258], f == 0, f == 7,
                    mark=f == 7)
        T["b1w2"] = evac(b1w2[:, :], bank[:, 0:258], t1)
        G.give(gi, T["b1w2"])
        for g in range(2):
            t1 = pool.put(lambda e, g=g: e.tensor_tensor(gtmp[:, g], wat[:, :, 0:256],
                                                         gate[:, g, :].unsqueeze(1).broadcast_to([128, 2, 256]), ALU.mult),
                          P_("wat"), P_(f"gate{g}"))
            for c in range(2):
                T["wgate"] = dve.put(red(wat[:, c, 896 + 16 * g:912 + 16 * g],
                                         gtmp[:, g, c].rearrange("p (h d) -> p h d", d=16)), t1)
        t1 = dve.put(ts(ysT[:, :, :], condT[:, :, :], 1.0 / 16, None, ALU.mult), P_("cond"))
        yq = lp[:, 8, 0:32].rearrange("p (c b) -> p c b", c=2)
        t2 = dve.put(tt(yq, ysT[:, :, :], ysT[:, :, :], ALU.mult), t1)
        t3 = pool.put(lambda e: e.tensor_tensor(w2sq, w2c[:, :, :], w2c[:, :, :], ALU.mult), P_("w2c"))
        bank, over, gi = G.take()
        for oc in range(2):
            for c in range(2):
                t1 = mm(bank[:, 16 * oc:16 * oc + 16], w2sq[:, c, 128 * oc:128 * oc + 128], yq[:, c, :], c == 0, c == 1,
                        over, t2, t3, mark=True)
        dz, dy, da, db = (lp[:, i, 0:32] for i in (9, 0, 1, 2))
        for _ in chain(dve, [ts(dz, bank[:, 0:32], 1e-8, None, ALU.add)], t1, dve_last()):
            pass
        G.give(gi, dve_last())
        for _ in chain(dve, rsqrt(dz, dy, da, db), dve_last()):
            pass
        T["dT"] = dve.put(lambda e: e.tensor_copy(dT[:, :, :], dy.rearrange("p (c b) -> p c b", c=2)), dve_last())
        t1 = dve.put(lambda e: e.tensor_copy(Bh[:, :].bitcast(F32R), Bf[:, :]), [P_(f"B{r}") for r in range(8)], wada_read)
        t2 = dve.put(tt(Bf[:, :], Bf[:, :], Bh[:, :], ALU.subtract), t1)
        t3 = dve.put(ts(Bf[:, :], Bf[:, :], hsel[:, 1:2], None, ALU.mult), t2, P_("hsel"))
        T["Bst"] = dve.put(stt(Bst[:, :].bitcast(F32R), Bh[:, :], hsel[:, 0:1], Bf[:, :], ALU.mult, ALU.add), t3)

        setup_done = [dve_last(), act_last(), pool_last(), T["b1w2"], T["Bst"],
                      pe.put(lambda e: e.matmul(bank[0:2, 100:102], ident[:, 0:2], ident[:, 0:2], start=True, stop=True),
                             dve_last(), P_("ident"))]

        if taps is not None and taps.get("stop") == 0:
            return finish_up(nc, ctx, (pe, act, dve, pool, sp), loads, taps, dict(X1=X1, adaT=adaT, W12=W12, GG=GG, dT=dT, b1w2=b1w2, rX=rX), setup_done)
        frp[0], fap[0] = 0, 0
        QsT = [cut(FR, frp, 8, 256) for _ in range(2)]
        KsT = [cut(FR, frp, 8, 256) for _ in range(2)]
        PT = Ring([cut(FA, fap, 1024) for _ in range(4)])
        tT = cut(FA, fap, 2, 256)
        mTs = [cut(FA, fap, 2, 256), XR[0]]
        HL = RND[:, :].rearrange("p (g h a d) -> p g h a d", g=2, h=16, a=4)
        Vg = [cut(FA, fap, 2, 16, 32) for _ in range(2)]
        U = [cut(FA, fap, 768) for _ in range(2)] + [SQ[:, 1, :]]
        OT = cut(FA, fap, 4, 256)
        O = cut(FA, fap, 2, 256)
        xn = cut(FA, fap, 2, 256)
        JK = sb("JK", [128, 2, 256])
        Z = sb("Z", [128, 2, 256])
        UOs = [sb(f"UO{i}", [128, 2, 256]) for i in range(2)]
        sm = sb("sm", [128, 64, 2])
        hall = sb("hall", [128, 520])
        h_a, h_b0, h_y, h_s, h_b1 = (hall[:, 104 * i:104 * i + 104].rearrange("p (t n) -> p t n", t=2) for i in range(5))
        k_a, k_b, k_y, k_s, k_f = (sb(n, [128, 2, 16]) for n in ("k_a", "k_b", "k_y", "k_s", "k_f"))

        for v in range(2):
            a = pool.put(lambda e, m=Vg[v]: e.memset(m, 0.0), setup_done)
            T["vg", v] = pool.put(lambda e, m=Vg[v]: e.memset(m[:, :, :, 16:17], 1.0), a)
        ph1 = [setup_done, T["vg", 1], [P_(k) for k in ("wqkv", "bqkv", "wo", "bo")]]

        def s_mod(b, src, mean, r, sh, base, mT, so, lag, *after):
            for t in range(2):
                i = 2 * b + t
                tk = dve.put(ts(xn[:, t, :], src[:, i, :], mean[:, i:i + 1], r[:, i:i + 1], ALU.subtract, ALU.mult), *after, T.get(("xnT", base, b - 1)))
                yield
            bank, over, gi = yield from grab(G)
            for t in range(2):
                for c in range(2):
                    tp = tr(bank[:, 256 * c + 128 * t:256 * c + 128 * t + 128], xn[:, t, 128 * c:128 * c + 128], over, tk,
                            mark=t + c == 2)
            T["xnT", base, b] = tp
            yield
            for c in range(2):
                tk = act.put(lambda e, c=c, bank=bank: e.activation(mT[:, c, :], bank[:, 256 * c:256 * c + 256], ACT.Identity,
                                                         bias=adaT[:, sh + c, b:b + 1], scale=adaT[:, sh + 2 + c, b:b + 1]),
                             tp, T.get(("mTread", base, b - lag)))
                yield
            G.give(gi, tk)
            T["mT", base, b] = tk
            bank, over, gi = yield from grab(G)
            for t in range(2):
                for c in range(2):
                    tp = tr(bank[:, 256 * t + 128 * c:256 * t + 128 * c + 128], mT[:, c, 128 * t:128 * t + 128], over, tk,
                            mark=t + c == 2)
            for t in range(2):
                tk = act.put(lambda e, t=t, bank=bank: e.activation(JK[:, t, :], bank[:, 256 * t:256 * t + 256], ACT.Square,
                                                         accum_out=sm[:, so, t:t + 1]), tp, T.get(("sm0", base, b - lag)),
                             T.get(("jk",)))
                T["jk",] = tk
                yield
            T["mss", base, b] = tk
            T["mbank"] = (bank, gi, tk, tp)

        def s_norm(b):
            so = 32 * (b % 2)
            yield from need("Q", b - 2)
            yield from s_mod(b, X, mv[:, :, 0], rX, 0, 1, mTs[b % 2], so, 2, ph1)
            bank, gi, tk, tp = T["mbank"]
            G.give(gi, tk)
            z, y, a, c_ = (sm[:, so + i, :] for i in (1, 2, 3, 4))
            yield from chain(dve, [ts(z, sm[:, so, :], EPS * EPS, None, ALU.max)] + rsqrt(z, y, a, c_)
                             + [ts(y, y, CL, 1.0, ALU.mult, ALU.min)], T["mss", 1, b], T.get(("Uw", b - 2)))
            T["sm0", 1, b] = dve_last()

        def s_qkv(b):
            so, mT, s1 = 32 * (b % 2), mTs[b % 2], T["sm0", 1, b]
            h_b = (h_b0, h_b1)[b % 2]
            yield from need("K", b - 2)
            for t in range(2):
                while 2 * b + t >= 3 and ("Uread", 2 * b + t - 3) not in T:
                    yield
                war, u = T.get(("Uread", 2 * b + t - 3)), U[(2 * b + t) % 3]
                b0, o0, g0 = yield from grab(G)
                for c in range(2):
                    t0 = mm(b0[:, :], mT[:, c, 128 * t:128 * t + 128], wqkv[:, c, 0:512], c == 0, c == 1, o0,
                            T["mT", 1, b], mark=c == 1)
                yield
                b1, o1, g1 = yield from grab(G)
                for c in range(2):
                    t1 = mm(b1[:, 0:256], mT[:, c, 128 * t:128 * t + 128], wqkv[:, c, 512:768], c == 0, c == 1, o1,
                            mark=c == 1)
                yield
                tk = dve.put(stt(u[:, 0:512], b0[:, :], sm[:, so + 2, t:t + 1], bqkv[:, 0:512], ALU.mult, ALU.add), t0, s1, war)
                G.give(g0, tk)
                yield
                tk = dve.put(stt(u[:, 512:768], b1[:, 0:256], sm[:, so + 2, t:t + 1], bqkv[:, 512:768], ALU.mult, ALU.add),
                             t1, s1, war)
                G.give(g1, tk)
                T["Uw", b] = tk
                yield
                tk = act.put(lambda e, u=u: e.activation(SQ[:, 0, :], u, ACT.Square), tk, T.get(("sq",)))
                yield
                T["sq",] = T["hss", b, t] = dve.put(red(h_s[:, t, 0:48], SQ[:, 0, :].rearrange("p (h d) -> p h d", d=16)), tk,
                                         T.get(("hf", b - 1)))
                yield
            T["mTread", 1, b] = t1
            hf = [red(h_s[:, :, 48:51], h_s[:, :, 0:48].rearrange("p t (g h) -> p t g h", g=3)),
                  ts(h_s[:, :, 0:51], h_s[:, :, 0:51], EPS * EPS, None, ALU.max)]
            hf += rsqrt(h_s[:, :, 0:51], h_y[:, :, 0:51], h_a[:, :, 0:51], h_b[:, :, 0:51])
            hf += [ts(h_a[:, :, 48:51], h_y[:, :, 48:51], CL, 1.0, ALU.mult, ALU.min),
                   ts(h_a[:, :, 48:51], h_a[:, :, 48:51], RT, None, ALU.mult)]
            yield from chain(dve, hf, [T["hss", b, t] for t in range(2)], T.get(("hread", b - 2)), T.get(("hf", b - 1)))
            for t in range(2):
                tk = dve.put(stt(h_b[:, t, 0:48].rearrange("p (g h) -> p g h", g=3),
                                 h_y[:, t, 0:48].rearrange("p (g h) -> p g h", g=3), CL,
                                 bc(h_a[:, t, 48:51], 16), ALU.mult, ALU.min), dve_last())
            T["hf", b] = tk

        def s_heads(b):
            h_b, tk = (h_b0, h_b1)[b % 2], T["hf", b]
            vg = Vg[b % 2]
            yield from need("A", b - 2)
            for t in range(2):
                uv = U[(2 * b + t) % 3].rearrange("p (h d) -> p h d", d=16)
                tq = dve.put(tt(uv[:, 0:32], uv[:, 0:32], bc(h_b[:, t, 0:32], 16), ALU.mult), tk)
                yield
                for g in range(2):
                    ug = uv[:, 16 * g:16 * g + 16].unsqueeze(2).broadcast_to([128, 16, 2, 16])
                    hi, lo = hilo(HL[:, g], g)
                    th = act.put(lambda e, hi=hi, ug=ug: e.activation(hi, ug, ACT.Copy), tq, T.get(("hlread", g)))
                    yield
                    T["hl", g] = dve.put(tt(lo, ug, HL[:, g, :, 0, :].unsqueeze(2).broadcast_to([128, 16, 2, 16]),
                                            ALU.subtract), th, T.get(("hlread", g)))
                    yield
                    if g == 0:
                        tv = dve.put(tt(vg[:, t, :, 0:16], uv[:, 32:48], bc(h_b[:, t, 32:48], 16), ALU.mult), tk,
                                     T.get(("pv", b - 2)))
                        yield
                    yield from stack(HL[:, g], 8, (QsT, KsT)[g][b % 2], t, T["hl", g], T.get(("scores", b - 2)))
                    T["hlread", g] = T["stackT"]
                T["Uread", 2 * b + t] = T["hl", 1]
            T["st", b] = T["stdone"]
            T["Vg", b] = tv
            T["hread", b] = tq

        def hilo(v, kind):
            v = v.bitcast(F32R)
            return (v[:, :, 0:2, :], v[:, :, 2:4, :]) if kind == 0 else (v[:, :, 0:4:2, :], v[:, :, 1:4:2, :])

        def stack(hl, npair, dst, t, ready, war):
            flat_ = hl.rearrange("p h a d -> p (h a d)")
            for p4 in range(npair // 4):
                bank, over, gi = yield from grab(G)
                for j in range(4):
                    tp = mm(bank[:, 128 * j:128 * j + 128],
                            flat_[:, 512 * p4 + 128 * j:512 * p4 + 128 * j + 128].bitcast(F32R),
                            identr[:, :].bitcast(F32R), True, True, over, ready, mark=j == 3)
                tk = evac(dst[:, 4 * p4:4 * p4 + 4, 128 * t:128 * t + 128].bitcast(F32R),
                          bank[:, :].rearrange("p (a n) -> p a n", a=4), tp, war)
                G.give(gi, tk)
                yield
            T["stackT"] = tp
            T["stdone"] = [act_last(), dve_last()]

        def s_att(b):
            q_, k_, vg = QsT[b % 2], KsT[b % 2], Vg[b % 2]
            ready = T["st", b]
            pend = []
            for p in range(8):
                ps, over, si = yield from grab(S2)
                for j in range(2):
                    for kt in range(2):
                        tp = mm(ps[:, 512 * j + 256 * kt:512 * j + 256 * kt + 256],
                                k_[64 * j:64 * j + 64, p, 128 * kt:128 * kt + 128].bitcast(F32R),
                                q_[64 * j:64 * j + 64, p, :].bitcast(F32R), True, True, over, ready, mark=j + kt == 2)
                yield
                pt, over, pi = yield from grab(PT)
                tk = act.put(lambda e, pt=pt, ps=ps: e.activation(pt, ps[:, :], ACT.Exp, scale=0.25), tp, over)
                S2.give(si, tk)
                pend.append((pt, pi, tk))
                yield
                if p == 7:
                    T["scores", b] = tp
                if p % 2 == 1:
                    g = p // 2
                    if g % 2 == 0:
                        po, oover, oi = yield from grab(PO)
                    for kt in range(2):
                        for j in range(4):
                            pt, pi, tk = pend[j // 2]
                            h = 4 * g + j
                            tp = mm(po[32 * j:32 * j + 32, 256 * (g % 2):256 * (g % 2) + 256], vg[:, kt, h, :],
                                    pt[:, 512 * (j % 2) + 256 * kt:512 * (j % 2) + 256 * kt + 256], kt == 0, kt == 1,
                                    oover, tk, T["Vg", b], pend[1][2], mark=kt == 1 and j == 3)
                        yield
                    for pt, pi, tk in pend:
                        PT.give(pi, tp)
                    pend = []
                    T["pv", b] = tp
                    if g % 2 == 1:
                        yield from need("OTread", b - 1)
                        tk = evac(OT[:, g - 1:g + 1, :], po[:, :].rearrange("p (a n) -> p a n", a=2), tp,
                                  T.get(("OTread", b - 1)))
                        PO.give(oi, tk)
                        T["OT", b, g // 2] = tk
                        yield

        def s_out(b):
            ready = [T["OT", b, 0], T["OT", b, 1]]
            for t in range(2):
                bank, over, gi = yield from grab(G)
                for g in range(4):
                    tp = tr(bank[:, 128 * g:128 * g + 128], OT[:, g, 128 * t:128 * t + 128], over, ready, mark=g == 3)
                bv = bank[:, :].rearrange("p (h n) -> p h n", n=32)
                yield
                tk = dve.put(lambda e, t=t, bv=bv: e.reciprocal(k_f[:, t, :], bv[:, :, 16]), tp, T.get(("kf", b - 1)))
                ov = O[:, t, :].rearrange("p (h d) -> p h d", d=16)
                yield
                to = dve.put(tt(ov, bv[:, :, 0:16], bc(k_f[:, t, :], 16), ALU.mult), tk, T.get(("Oread", b - 1)))
                G.give(gi, to)
                yield
                tq = act.put(lambda e, t=t: e.activation(JK2[:, t, :], O[:, t, :], ACT.Square), to,
                             T.get(("ks", b - 1, t)))
                yield
                T["ks", b, t] = dve.put(red(k_s[:, t, :], JK2[:, t, :].rearrange("p (h d) -> p h d", d=16)), tq)
                yield
            T["OTread", b] = tp
            n1, z1, y1, a1, c1 = (sm[:, i, :] for i in (5, 6, 7, 8, 9))
            fns = [ts(k_s[:, :, :], k_s[:, :, :], EPS * EPS, None, ALU.max)]
            fns += rsqrt(k_s[:, :, :], k_y[:, :, :], k_a[:, :, :], k_b[:, :, :])
            fns += [ts(k_y[:, :, :], k_y[:, :, :], CL / RT, 1.0 / RT, ALU.mult, ALU.min),
                    tt(k_a[:, :, :], k_y[:, :, :], k_y[:, :, :], ALU.mult),
                    tt(k_a[:, :, :], k_a[:, :, :], k_s[:, :, :], ALU.mult),
                    red(z1, k_a[:, :, :]), ts(z1, z1, EPS * EPS, None, ALU.max)]
            fns += rsqrt(z1, y1, a1, c1) + [ts(y1, y1, CL, 1.0, ALU.mult, ALU.min)]
            yield from chain(dve, fns, T["ks", b, 0], T["ks", b, 1])
            tk = dve_last()
            for t in range(2):
                ov = O[:, t, :].rearrange("p (h d) -> p h d", d=16)
                tv = dve.put(tt(ov, ov, bc(k_y[:, t, :], 16), ALU.mult), tk)
                yield
            T["kf", b] = tv
            bank, over, gi = yield from grab(G)
            for t in range(2):
                for c in range(2):
                    tp = tr(bank[:, 256 * c + 128 * t:256 * c + 128 * t + 128], O[:, t, 128 * c:128 * c + 128], over, tv,
                            mark=t + c == 2)
            T["Oread", b] = tp
            yield
            te = evac(tT, bank[:, :].rearrange("p (c n) -> p c n", c=2), tp, T.get(("tTread", b - 1)))
            G.give(gi, te)
            yield
            bank, over, gi = yield from grab(G)
            for t in range(2):
                for c in range(2):
                    tp = mm(bank[:, 256 * t:256 * t + 256], tT[:, c, 128 * t:128 * t + 128], wo[:, c, :], c == 0, c == 1,
                            over, te, mark=t + c == 2)
            T["tTread", b] = tp
            yield
            yield from need("Y", b - 2)
            for t in range(2):
                tu = dve.put(stt(UOs[b % 2][:, t, :], bank[:, 256 * t:256 * t + 256], sm[:, 7, t:t + 1], bo[:, :], ALU.mult, ALU.add),
                             tp, tk, T.get(("UOread", b - 2)))
                yield
            G.give(gi, tu)
            T["UO", b] = tu

        def s_fin(b):
            yield from finish(b, 0, X, ssX, X1, UOs[b % 2], T["UO", b])
            for t in range(2):
                i = 2 * b + t
                t1 = dve.put(lambda e, i=i, t=t: e.bn_stats(bn[:, t, :], X1[:, i, :]), T["x1", b, t], T.get(("bn", t)))
                yield
                T["bn", t] = dve.put(lambda e, i=i, t=t: e.bn_aggr(mv2[:, i, :], bn[:, t, :]), t1)
                yield

        def finish(b, half, src, ssx, dst, UO, tu):
            bank, over, gi = yield from grab(G)
            tp = mm(bank[:, 0:256], ident[0:16, b:b + 1].broadcast_to([16, 128]), grow[:, 256 * half:256 * half + 256],
                    True, True, over, T["grow"], mark=True)
            yield
            for t in range(2):
                tz = dve.put(tt(Z[:, t, :], UO[:, t, :], bank[:, 0:256], ALU.mult), tp, tu, T.get(("Zread",)))
                yield
            G.give(gi, tz)
            r0 = 10 + 0
            s = lambda i: sm[:, r0 + i, :]
            for t in range(2):
                ta = act.put(lambda e, t=t: e.activation(JK[:, t, :], UO[:, t, :], ACT.Square,
                                                         accum_out=sm[:, r0, t:t + 1]), tu, T.get(("finsm",)),
                             T.get(("jk",)))
                yield
                ta = act.put(lambda e, t=t: e.activation(JK[:, t, :], Z[:, t, :], ACT.Square,
                                                         accum_out=sm[:, r0 + 1, t:t + 1]), tz, ta)
                T["jk",] = ta
                yield
                i = 2 * b + t
                tx = dve.put(lambda e, t=t, i=i, JD=JD: e.tensor_tensor_reduce(out=JD[:, :], in0=src[:, i, :], in1=Z[:, t, :],
                                                                        scale=1.0, scalar=0.0, op0=ALU.mult, op1=ALU.add,
                                                                        accum_out=sm[:, r0 + 2, t:t + 1]), tz, dve_last())
                yield
            T["UOread", b] = ta
            x2 = ssx[:, 2 * b:2 * b + 2]
            nn = sm[:, r0:r0 + 2, :]
            yy = sm[:, r0 + 3:r0 + 5, :]
            aa = sm[:, r0 + 5:r0 + 7, :]
            bb = sm[:, r0 + 7:r0 + 9, :]
            zz = sm[:, r0 + 9:r0 + 11, :]
            so, nz, th, psi = s(11), s(12), s(13), s(14)
            yield from chain(dve, [ts(zz, nn, 1e-30, None, ALU.max)] + rsqrt(zz, yy, aa, bb)
                             + [ts(so, s(3), CL, 1.0, ALU.mult, ALU.min), tt(nz, s(10), s(4), ALU.mult),
                                tt(nz, nz, so, ALU.mult), ts(nz, nz, EPS, None, ALU.max)], ta, tx)
            tw = act.put(lambda e: e.activation(th, nz, ACT.Tanh), dve_last())
            yield
            y2, xy, Aa, den, ca, cb = s(15), s(16), s(17), s(18), s(19), s(20)
            yield from chain(dve, [lambda e: e.reciprocal(psi, nz), tt(psi, psi, so, ALU.mult),
                                   tt(psi, psi, th, ALU.mult), tt(y2, psi, psi, ALU.mult), tt(y2, y2, s(1), ALU.mult),
                                   tt(xy, psi, s(2), ALU.mult), ts(xy, xy, 2.0, 1.0, ALU.mult, ALU.add),
                                   tt(Aa, xy, y2, ALU.add), tt(den, x2, y2, ALU.mult), tt(den, den, xy, ALU.add),
                                   ts(den, den, EPS, None, ALU.max), lambda e: e.reciprocal(cb, den),
                                   tt(ca, Aa, cb, ALU.mult), tt(cb, cb, psi, ALU.mult),
                                   ts(den, x2, -1.0, 1.0, ALU.mult, ALU.add), tt(cb, cb, den, ALU.mult)], tw, dve_last())
            tc = dve_last()
            for t in range(2):
                i = 2 * b + t
                o = dst[:, i, :]
                t1 = dve.put(ts(o, src[:, i, :], sm[:, r0 + 19, t:t + 1], None, ALU.mult), tc, T.get(("dstfree",)))
                yield
                T["x1", b, t] = dve.put(stt(o, Z[:, t, :], sm[:, r0 + 20, t:t + 1], o, ALU.mult, ALU.add), t1)
                yield
            T["Zread",] = T["finsm",] = T["x1", b, 1]

        JK2 = sb("JK2", [128, 2, 256])
        JD = XR[1][:, 0, :]
        mv2 = sb("mv2", [128, NT, 2])

        weave(thread(s_norm, "N", None), thread(s_qkv, "Q", "N"), thread(s_heads, "K", "Q"), thread(s_att, "A", "K"),
              thread(s_out, "O", "A"), thread(s_fin, "Y", "O"))

        for _ in ln_prep(mv2[:, 0:NN, 0], mv2[:, 0:NN, 1], ssX1[:, 0:NN], rX1[:, 0:NN], NN, dve_last()):
            pass
        pe_end = pe.put(lambda e: e.matmul(bank[0:2, 100:102], ident[:, 0:2], ident[:, 0:2], start=True, stop=True),
                        dve_last(), [f[0] for f in G.free if f[0]])
        ph2 = [pe_end, dve_last(), act_last(), pool_last()]
        G.free = [(flat([f[0], ph2]), f[1]) for f in G.free]
        if taps is not None and taps.get("stop") == 1:
            return finish_up(nc, ctx, (pe, act, dve, pool, sp), loads, taps, dict(X1=X1), ph2)

        fap[0], frp[0], fwp[0] = 0, 0, 0
        QsT = [cut(FR, frp, 8, 256) for _ in range(2)]
        KsT = [cut(FR, frp, 8, 256) for _ in range(2)]
        GQsT = GR[:, 0:1024].rearrange("p (a n) -> p a n", a=4)
        GKsT = GR[:, 1024:1536].rearrange("p (a n) -> p a n", a=4)
        NMT = sb("NMT", [128, 256])
        PT = Ring([cut(FA, fap, 1024) for _ in range(4)])
        PT.free = [(ph2, i) for i in range(4)]
        Vg = [cut(FA, fap, 2, 16, 32) for _ in range(2)]
        GV = [cut(FA, fap, 8, 32) for _ in range(2)]
        HLs = [HL[:, v] for v in range(2)]
        OT = cut(FA, fap, 4, 256)
        OTL = cut(FA, fap, 2, 256)
        OO = cut(FA, fap, 2, 256)
        xsT = cut(FA, fap, 2, 256)
        zT = cut(FA, fap, 2, 256)
        h0p = cut(FA, fap, 2, 128)
        UG = cut(FA, fap, 2, 258)
        RL = JK2[:, 0, :].rearrange("p (t n) -> p t n", t=2)
        rT = JK2[:, 1, :]
        xn = SQ[:, 0, 0:512].rearrange("p (t n) -> p t n", t=2)
        mT = SQ[:, 1, 0:512].rearrange("p (t n) -> p t n", t=2)
        R2 = [cut(FW, fwp, 1024) for _ in range(2)]
        rhoT = cut(FW, fwp, 256)
        h0T = cut(FW, fwp, 2, 256)
        JD = cut(FW, fwp, 256)
        nm = lp[:, 0:2, 0:24]
        nmhl = hall[:, 0:256].rearrange("p (t r n) -> p t r n", t=2, r=2)
        gt = [hall[:, 256 + 64 * i:320 + 64 * i].rearrange("p (t n) -> p t n", t=2) for i in range(2)]
        RW = SQ[:, 0, 512:768]
        LTW = sb("LTW", [128, 512])
        LT = LTW[:, 0:256]
        LW = LTW[:, 256:512].rearrange("p (t s a d) -> p t s a d", t=2, s=2, a=4)
        MO = [0, 320, 640, 768]

        for v in range(2):
            pool.put(lambda e, m=Vg[v]: e.memset(m, 0.0), ph2)
            a_ = pool.put(lambda e, v=v: e.memset(GV[v], 0.0), ph2)
        pool.put(lambda e: e.memset(h0p, 0.0), ph2)
        pool.put(lambda e: e.memset(nmhl, 0.0), ph2)
        for v in range(2):
            pool.put(lambda e, m=Vg[v]: e.memset(m[:, :, :, 16:17], 1.0), a_)
            pool.put(lambda e, v=v: e.memset(GV[v][:, :, 16:17], 1.0), a_)
        init2 = [ph2, pool_last(), [P_(k) for k in ("wr", "wout", "w2c", "wrt", "bg", "ltm", "wat", "wgkv", "b2")]]
        for k in [k for k in T if isinstance(k, tuple) and k[0] in ("x1", "xnT", "mTread", "sm0", "hlread", "Uread", "Zread",
                                                                   "UOread", "finsm", "scores", "pv", "OTread")]:
            T.pop(k)
        outs = []

        def maskmm(o, off, n, rep, over):
            rhs = maskb[:, off:off + n]
            if rep > 1:
                rhs = rhs.unsqueeze(1).broadcast_to([128, rep, n])
                o = o.rearrange("p (r n) -> p r n", r=rep)
            return mm(o, identb[:, :], rhs, True, False, over, init2)

        def f32r(a):
            return a.bitcast(F32R)

        def b_ffn(b):
            UO = UOs[b % 2]
            yield from s_mod(b, X, mv2[:, :, 0], rX1, 6, 2, mT, 0, 1, init2)
            mb, mgi, tk, tp = T["mbank"]
            for t in range(2):
                bank, over, gi = yield from grab(G)
                for c in range(2):
                    tp = mm(bank[:, 0:258], mT[:, c, 128 * t:128 * t + 128], GG[:, c, :], c == 0, c == 1, over,
                            T["mT", 2, b], mark=c == 1)
                tu = acopy(UG[:, t, :], bank[:, 0:258], tp, T.get(("UGread", b - 1)))
                G.give(gi, tu)
                yield
                tq = dve.put(lambda e, t=t, mb=mb: e.tensor_tensor_reduce(
                    out=JD[:, :], in0=mb[:, 256 * t:256 * t + 256], in1=UG[:, t, 0:256], scale=1.0, scalar=0.0,
                    op0=ALU.mult, op1=ALU.add, accum_out=sm[:, 1, t:t + 1]), tu, tk, dve_last())
                yield
            G.give(mgi, [tk, tq])
            z, y, a, c_, q, k = (sm[:, i, :] for i in (2, 3, 4, 5, 6, 7))
            yield from chain(dve, [ts(z, sm[:, 0, :], EPS * EPS, None, ALU.max)] + rsqrt(z, y, a, c_)
                             + [ts(y, y, CL, 1.0, ALU.mult, ALU.min), tt(q, sm[:, 1, :], y, ALU.mult),
                                stt(q, UG[:, :, 256], 2.0, q, ALU.mult, ALU.add), tt(q, q, y, ALU.mult),
                                ts(q, q, b1w2[:, 256:257], EPS * EPS, ALU.add, ALU.max)]
                             + rsqrt(q, z, a, c_)
                             + [ts(z, z, CL, 1.0, ALU.mult, ALU.min), tt(k, z, y, ALU.mult)], T["mss", 2, b], tq)
            ck = T["sm0", 2, b] = T["UGread", b] = dve_last()
            bank, over, gi = yield from grab(G)
            for t in range(2):
                for c in range(2):
                    tp = mm(bank[:, 256 * t:256 * t + 256], mT[:, c, 128 * t:128 * t + 128], W12[:, c, :], c == 0, c == 1,
                            over, mark=t + c == 2)
            T["mTread", 2, b] = tp
            yield
            for t in range(2):
                t1 = dve.put(stt(UO[:, t, :], b1w2[:, 0:256], sm[:, 2, t:t + 1], b2[:, :], ALU.mult, ALU.add), ck,
                             P_("b2"), T.get(("UOread", b - 2)))
                yield
                tu = dve.put(stt(UO[:, t, :], bank[:, 256 * t:256 * t + 256], sm[:, 7, t:t + 1], UO[:, t, :],
                                 ALU.mult, ALU.add), t1, tp)
                yield
            G.give(gi, tu)
            yield from finish(b, 1, X, ssX1, X, UO, tu)

        hlturn = [0]

        def split(src, n, kind, ready):
            v = hlturn[0] % 2
            hlturn[0] += 1
            hl = HLs[v][:, 0:n]
            hi, lo = hilo(hl, kind)
            sv = src.rearrange("p (h d) -> p h d", d=16).unsqueeze(2).broadcast_to([128, n, 2, 16])
            th = acopy(hi, sv, ready, T.get(("hlread", v)))
            yield
            tl = dve.put(tt(lo, sv, hl[:, :, 0, :].unsqueeze(2).broadcast_to([128, n, 2, 16]), ALU.subtract), th)
            yield
            return hl, v, tl

        def b_proj(b):
            hx = [X[:, 2 * b + t, :] for t in range(2)]
            bank, over, gi = yield from grab(G)
            for t in range(2):
                for c in range(2):
                    tp = tr(bank[:, 256 * c + 128 * t:256 * c + 128 * t + 128], hx[t][:, 128 * c:128 * c + 128], over,
                            T["x1", b, t], mark=t + c == 2)
            te = evac(h0T, bank[:, :].rearrange("p (c n) -> p c n", c=2), tp, T.get(("h0read", b - 1)))
            G.give(gi, te)
            yield
            for t in range(2):
                ba, over, ga = yield from grab(G)
                for c in range(2):
                    tp = mm(ba[:, :], h0T[:, c, 128 * t:128 * t + 128], wat[:, c, 0:512], c == 0, c == 1, over, te,
                            mark=c == 1)
                yield
                tl = None
                yield from need("L", b - 2)
                for g in range(2):
                    hl, v, tl = yield from split(ba[:, 256 * g:256 * g + 256], 16, g, [tp, tl])
                    if g == 1:
                        G.give(ga, tl)
                    yield from stack(hl, 8, (QsT, KsT)[g][b % 2], t, tl, T.get(("scores", b - 2)))
                    T["hlread", v] = T["stackT"]
            for t in range(2):
                bb, over, gb_ = yield from grab(G)
                for c in range(2):
                    tp = mm(bb[:, 0:416], h0T[:, c, 128 * t:128 * t + 128], wat[:, c, 512:928], c == 0, c == 1, over, te,
                            mark=c == 1)
                yield
                tv = dve.put(lambda e, t=t, bb=bb: e.tensor_copy(Vg[b % 2][:, t, :, 0:16],
                                                                 bb[:, 0:256].rearrange("p (h d) -> p h d", d=16)),
                             tp, T.get(("pv", b - 2)))
                yield
                yield from need("gtread", b - 2)
                tg2 = act.put(lambda e, t=t, bb=bb: e.activation(gt[b % 2][:, t, :], bb[:, 384:416], ACT.Exp, scale=-1.0),
                              tv, T.get(("gtread", b - 2)))
                yield
                hl, v, tl = yield from split(bb[:, 256:384], 8, 0, [tp, tv])
                G.give(gb_, [tl, tg2, tv])
                yield from need("lsc", b - 1)
                yield from stack(hl, 4, GQsT, t, tl, T.get(("lsc", b - 1)))
                T["hlread", v] = T["stackT"]
            for c in range(2):
                tp_ = dve.put(red(h0p[:, c, 0:64], h0T[:, c, :].rearrange("p (n k) -> p n k", k=4)), te, init2,
                              T.get(("h0read", b - 1)))
                yield
            bank, over, gi = yield from grab(G)
            for c in range(2):
                tp = mm(bank[:, 0:256], h0p[:, c, :], wgkv[:, c, :], c == 0, c == 1, over, tp_, mark=c == 1)
            yield
            yield from need("L", b - 2)
            tg = acopy(GV[b % 2][:, :, 0:16], bank[:, 128:256].rearrange("p (h d) -> p h d", d=16), tp,
                       T.get(("pvl", b - 2)))
            yield
            hl, v, tl = yield from split(bank[:, 0:128], 8, 1, tp)
            G.give(gi, [tl, tg])
            yield from need("lsc", b - 1)
            yield from stack(hl, 4, GKsT, 0, tl, T.get(("lsc", b - 1)))
            T["hlread", v] = T["stackT"]
            T["h0read", b] = tp
            T["proj", b] = [act_last(), dve_last()]
            g_ = gt[b % 2]
            yield from chain(dve, [ts(g_, g_, 1.0, None, ALU.add), lambda e: e.reciprocal(g_, g_)], tg2)
            T["gt", b] = dve_last()

        def sc(o, lk, lsl, rk, rsl, h, start, stop, *after, mark=False):
            r = 64 * (h % 2)
            return mm(o, f32r(lk[r:r + 64, h // 2, lsl]), f32r(rk[r:r + 64, h // 2, rsl]), start, stop, *after, mark=mark)

        def sub(o, h, qs, *after):
            r = 64 * (h % 2)
            return mm(o, f32r(zselr[r:r + 48, h:h + 1]).broadcast_to([48, 128]), f32r(NMT[r:r + 48, qs]), False, False,
                      *after)

        def b_max(b):
            q_, k_ = QsT[b % 2], KsT[b % 2]
            yield from need("E", b - 2)
            sem = ctx.enter_context(nc.semaphore(f"d_xr{b}"))
            T["xr", b] = sp.dma(lambda e: e.dma_start(XR[b % 2][:, :, :], xv[:, 2 * b:2 * b + 2, :]), sem, 16,
                                T.get(("out", b - 2)), ph2)
            ready = T["proj", b]

            war = T.get(("nmT", b - 1))
            jobs = [("a", 0), ("a", 8)] + [("b", 4 * i) for i in range(4)] + [("l", 0)]
            for kind, h0 in jobs:
                ps, over, si = yield from grab(S2)
                for i in range(2):
                    pb = ps[:, 512 * i:512 * i + 512]
                    if kind == "a":
                        maskmm(pb, MO[0], 128, 4, over)
                        for j in range(4):
                            tp = sc(pb[:, 128 * j:128 * j + 128], q_, slice(0, 128), k_, slice(0, 128), h0 + i + 2 * j,
                                    False, True, ready, mark=j == 3)
                        o, i_ = nm[:, 0, h0 + i:h0 + 8:2], pb.rearrange("p (h n) -> p h n", h=4)
                    elif kind == "b":
                        maskmm(pb[:, 0:384], MO[0] + 128, 192, 2, over)
                        for j in range(2):
                            tp = sc(pb[:, 192 * j:192 * j + 192], q_, slice(128, 256), k_, slice(64, 256),
                                    h0 + i + 2 * j, False, True, ready, mark=j == 1)
                        o, i_ = nm[:, 1, h0 + i:h0 + 4:2], pb[:, 0:384].rearrange("p (h n) -> p h n", h=2)
                    else:
                        maskmm(pb, MO[2], 128, 4, over)
                        for j in range(4):
                            for t in range(2):
                                tp = sc(pb[:, 128 * j + 64 * t:128 * j + 64 * t + 64], GQsT,
                                        slice(128 * t, 128 * t + 128), GKsT, slice(0, 64), i + 2 * j, False, True, ready,
                                        mark=j + t == 4)
                        o = nm[:, :, 16 + i:24:2].rearrange("p t h -> p h t")
                        i_ = pb.rearrange("p (h t n) -> p h t n", h=4, t=2)
                    yield
                    tk = dve.put(red(o, i_, ALU.max, negate=True), tp, T.get(("nmhl", b - 1)))
                    yield
                S2.give(si, tk)
            n2 = nm.unsqueeze(2).broadcast_to([128, 2, 2, 24])
            th = dve.put(lambda e: e.tensor_copy(f32r(nmhl[:, :, :, 0:24]), n2), tk, war, init2)
            yield
            tl = dve.put(tt(f32r(nmhl[:, :, :, 24:48]), n2, nmhl[:, :, :, 0:24], ALU.subtract), th)
            T["nmhl", b] = tl
            bank, over, gi = yield from grab(G)
            for t in range(2):
                tp = tr(bank[:, 128 * t:128 * t + 128], nmhl[:, t].rearrange("p r n -> p (r n)"), over, tl, mark=t == 1)
            T["nmT", b] = tp
            yield from need("L", b - 1)
            tn = dve.put(lambda e, bank=bank: e.tensor_copy(f32r(NMT[:, :]), bank[:, 0:256]), tp,
                         T.get(("sTdone", b - 1)))
            G.give(gi, tn)
            yield

            T["tn", b] = tn

        def b_loc(b):
            q_, k_, vg, gv, tn = QsT[b % 2], KsT[b % 2], Vg[b % 2], GV[b % 2], T["tn", b]
            po, oover, oi = yield from grab(PO)
            for g in range(2):
                ps, over, si = yield from grab(S2)
                for i in range(2):
                    maskmm(ps[:, 512 * i:512 * i + 512], MO[3], 256, 2, over)
                    for j in range(2):
                        h = 4 * g + i + 2 * j
                        o = ps[:, 512 * i + 256 * j:512 * i + 256 * j + 256]
                        sub(o, 16 + h, slice(0, 256), tn)
                        tp = sc(o, GKsT, slice(0, 128), GQsT, slice(0, 256), h, False, True, mark=i + j == 2)
                    yield
                pt, over, pi = yield from grab(PT)
                tk = act.put(lambda e, pt=pt, ps=ps: e.activation(pt, ps[:, :], ACT.Exp, scale=0.25), tp, over)
                S2.give(si, tk)
                yield
                if g == 1:
                    T["lsc", b] = tp
                for j in range(4):
                    tp = mm(po[32 * j:32 * j + 32, 256 * g:256 * g + 256], gv[:, 4 * g + j, :],
                            pt[:, 512 * (j % 2) + 256 * (j // 2):512 * (j % 2) + 256 * (j // 2) + 256], True,
                            True, oover, tk, mark=j == 3)
                PT.give(pi, tp)
                T["pvl", b] = tp
                yield
            yield from need("OTread", b - 1)
            tk = evac(OTL, po[:, :].rearrange("p (a n) -> p a n", a=2), tp, T.get(("OTread", b - 1)))
            PO.give(oi, tk)
            pend = []
            for p in range(8):
                ps, over, si = yield from grab(S2)
                for j in range(2):
                    h = 2 * p + j
                    pb = ps[:, 512 * j:512 * j + 320]
                    maskmm(pb, MO[1], 320, 1, over)
                    for o, ks, qs in ((pb[:, 0:192], slice(0, 128), slice(0, 192)),
                                      (pb[:, 192:320], slice(128, 256), slice(128, 256))):
                        sub(o, h, qs, tn)
                        tp = sc(o, k_, ks, q_, qs, h, False, True, mark=j == 1 and ks.start == 128)
                    yield
                if p == 7:
                    T["scores", b] = T["sTdone", b] = tp
                pt, over, pi = yield from grab(PT)
                tk = act.put(lambda e, pt=pt, ps=ps: e.activation(
                    pt[:, 0:640].rearrange("p (h n) -> p h n", h=2),
                    ps[:, :].rearrange("p (h n) -> p h n", h=2)[:, :, 0:320], ACT.Exp, scale=0.25), tp, over)
                S2.give(si, tk)
                pend.append((pt, pi, tk))
                yield
                if p % 2 == 1:
                    g = p // 2
                    if g % 2 == 0:
                        po, oover, oi = yield from grab(PO)
                    base = 256 * (g % 2)
                    for kt in range(2):
                        for j in range(4):
                            pt, pi, tk = pend[j // 2]
                            off = 320 * (j % 2)
                            o = po[32 * j:32 * j + 32, base:base + 192] if kt == 0 else po[32 * j:32 * j + 32, base + 128:base + 256]
                            r = pt[:, off:off + 192] if kt == 0 else pt[:, off + 192:off + 320]
                            tp = mm(o, vg[:, kt, 4 * g + j, :], r, kt == 0, kt == 1, oover, pend[1][2],
                                    mark=kt == 1 and j == 3)
                        yield
                    for pt, pi, tk in pend:
                        PT.give(pi, tp)
                    pend = []
                    T["pv", b] = tp
                    if g % 2 == 1:
                        yield from need("OTread", b - 1)
                        tk = evac(OT[:, g - 1:g + 1, :], po[:, :].rearrange("p (a n) -> p a n", a=2), tp,
                                  T.get(("OTread", b - 1)))
                        PO.give(oi, tk)
                        yield
            T["OT2", b] = [act_last(), dve_last()]
            yield

        def b_mix(b):
            ready = T["OT2", b]
            xr = XR[b % 2]
            gl, gr = gt[b % 2][:, :, 0:16], gt[b % 2][:, :, 16:32]
            for t in range(2):
                bank, over, gi = yield from grab(G)
                for g in range(2):
                    tp = tr(bank[:, 128 * g:128 * g + 128], OTL[:, g, 128 * t:128 * t + 128], over, ready, mark=g == 1)
                bv = bank[:, 0:256].rearrange("p (h n) -> p h n", n=32)
                yield
                tk = dve.put(lambda e, t=t, bv=bv: e.reciprocal(k_a[:, t, 0:8], bv[:, :, 16]), tp)
                yield
                tr_ = dve.put(tt(RL[:, t, :].rearrange("p (h d) -> p h d", d=16), bv[:, :, 0:16], bc(k_a[:, t, 0:8], 16),
                                 ALU.mult), tk, T.get(("RLread",)))
                G.give(gi, tr_)
                yield
                bank, over, gi = yield from grab(G)
                for g in range(4):
                    tp = tr(bank[:, 128 * g:128 * g + 128], OT[:, g, 128 * t:128 * t + 128], over, ready, mark=g == 3)
                bv = bank[:, :].rearrange("p (h n) -> p h n", n=32)
                yield
                tk = dve.put(lambda e, t=t, bv=bv: e.reciprocal(k_b[:, t, :], bv[:, :, 16]), tp)
                yield
                tk = dve.put(tt(k_b[:, t, :], k_b[:, t, :], gl[:, t, :], ALU.mult), tk, T["gt", b])
                yield
                to = dve.put(tt(OO[:, t, :].rearrange("p (h d) -> p h d", d=16), bv[:, :, 0:16], bc(k_b[:, t, :], 16),
                                ALU.mult), tk, T.get(("OOread",)))
                G.give(gi, to)
                yield
            T["OTread", b] = tp
            bank, over, gi = yield from grab(G)
            for t in range(2):
                tp = tr(bank[:, 128 * t:128 * t + 128], RL[:, t, :], over, tr_, mark=t == 1)
            T["RLread",] = tp
            te = evac(rT, bank[:, 0:256], tp, T.get(("rTread",)))
            G.give(gi, te)
            yield
            bank, over, gi = yield from grab(G)
            for t in range(2):
                tp = mm(bank[:, 256 * t:256 * t + 256], rT[:, 128 * t:128 * t + 128], wr[:, :], True, True, over, te,
                        mark=t == 1)
            T["rTread",] = tp
            yield
            for t in range(2):
                bv = bank[:, 256 * t:256 * t + 256].rearrange("p (h d) -> p h d", d=16)
                t1 = dve.put(tt(JK2[:, t, :].rearrange("p (h d) -> p h d", d=16), bv, bc(gr[:, t, :], 16), ALU.mult), tp)
                yield
                to = dve.put(tt(OO[:, t, :], OO[:, t, :], JK2[:, t, :], ALU.add), t1)
                yield
            T["gtread", b] = T["RLread",] = T["rTread",] = to
            G.give(gi, to)
            bank, over, gi = yield from grab(G)
            for t in range(2):
                for c in range(2):
                    tp = tr(bank[:, 256 * c + 128 * t:256 * c + 128 * t + 128], OO[:, t, 128 * c:128 * c + 128], over, to,
                            mark=t + c == 2)
            te = evac(OO, bank[:, :].rearrange("p (c n) -> p c n", c=2), tp, to)
            G.give(gi, te)
            yield
            bank, over, gi = yield from grab(G)
            for t in range(2):
                for c in range(2):
                    tp = mm(bank[:, 256 * t:256 * t + 256], OO[:, c, 128 * t:128 * t + 128], wout[:, c, :], c == 0,
                            c == 1, over, te, mark=t + c == 2)
            T["OOread",] = tp
            yield
            tx = dve.put(tt(xr[:, :, :], xr[:, :, :], bank[:, :].rearrange("p (t n) -> p t n", t=2), ALU.add), tp,
                         T["xr", b])
            G.give(gi, tx)
            T["tx", b] = tx
            yield

        def b_moe(b):
            xr, tx, tp = XR[b % 2], T["tx", b], T.get(("xsread",))
            bank, over, gi = yield from grab(G)
            for t in range(2):
                for c in range(2):
                    tq = tr(bank[:, 256 * c + 128 * t:256 * c + 128 * t + 128], xr[:, t, 128 * c:128 * c + 128], over, tx,
                            mark=t + c == 2)
            yield
            for c in range(2):
                te = act.put(lambda e, c=c, bank=bank: e.activation(xsT[:, c, :], bank[:, 256 * c:256 * c + 256], ACT.Copy,
                                                                    scale=ysT[:, c, b:b + 1]), tq, tp)
                yield
            G.give(gi, te)
            bank, over, gi = yield from grab(G)
            for oc in range(2):
                for c in range(2):
                    tp = mm(bank[:, 256 * oc:256 * oc + 256], w2c[:, c, 128 * oc:128 * oc + 128], xsT[:, c, :], c == 0,
                            c == 1, over, te, mark=oc + c == 2)
            T["xsread",] = tp
            yield
            for oc in range(2):
                te = act.put(lambda e, oc=oc, bank=bank: e.activation(zT[:, oc, :], bank[:, 256 * oc:256 * oc + 256],
                                                                      ACT.Copy, scale=dT[:, oc, b:b + 1]), tp,
                             T.get(("zread",)))
                yield
            G.give(gi, te)
            bank, over, gi = yield from grab(G)
            for t in range(2):
                for c in range(2):
                    tp = mm(bank[:, 20 * t:20 * t + 20], zT[:, c, 128 * t:128 * t + 128], wrt[:, c, :], c == 0, c == 1,
                            over, te, mark=t + c == 2)
            yield
            rv = bank[:, 0:40].rearrange("p (t n) -> p t n", t=2)

            def w(i, *shape):
                a = RW[:, i:i + int(np.prod(shape))]
                if len(shape) == 1:
                    return a
                names = "abc"[:len(shape)]
                return a.rearrange(f"p ({' '.join(names)}) -> p {' '.join(names)}",
                                   **{names[i]: shape[i] for i in range(1, len(shape))})

            lg, mx, pr, cm, eq = w(0, 2, 4), w(8, 2), w(10, 2, 4), w(18, 2, 4, 4), w(50, 2, 4, 4)
            rk, oh, w12, lf = w(82, 2, 4), w(90, 2, 2, 4), w(106, 2, 2), w(110, 2, 2, 16)
            rho, sm_, tmp = w(174, 2), w(176, 2), w(178, 2, 2, 4)
            yield from chain(dve, [tt(lg, rv[:, :, 0:4], bg[:, :].unsqueeze(1).broadcast_to([128, 2, 4]), ALU.add),
                                   red(mx, lg, ALU.max, negate=True), tt(lg, lg, bc(mx, 4), ALU.add)], tp,
                             T.get(("rwread",)))
            ta = act.put(lambda e: e.activation(pr, lg, ACT.Exp), dve_last())
            yield
            pj = pr.unsqueeze(2).broadcast_to([128, 2, 4, 4])
            lt4 = ltm[:, :].rearrange("p (i j) -> p i j", j=4)
            fns = [red(sm_, pr), lambda e: e.reciprocal(sm_, sm_), tt(pr, pr, bc(sm_, 4), ALU.mult),
                   tt(cm, pj, bc(pr, 4), ALU.is_gt), tt(eq, pj, bc(pr, 4), ALU.is_equal)]
            fns += [tt(eq[:, t], eq[:, t], lt4, ALU.mult) for t in range(2)]
            fns += [tt(cm, cm, eq, ALU.add), red(rk, cm), ts(oh[:, :, 0, :], rk, 0.0, None, ALU.is_equal),
                    ts(oh[:, :, 1, :], rk, 1.0, None, ALU.is_equal),
                    tt(tmp, oh, pr.unsqueeze(2).broadcast_to([128, 2, 2, 4]), ALU.mult), red(w12, tmp),
                    lambda e: e.reciprocal(rho, w12[:, :, 0]), tt(rho, rho, w12[:, :, 1], ALU.mult),
                    tt(oh[:, :, 0, :], oh[:, :, 0, :], oh[:, :, 1, :], ALU.subtract)]
            lw4 = lf.rearrange("p t s (e r) -> p t s e r", r=4)
            lo4 = rv[:, :, 4:20].rearrange("p t (e r) -> p t e r", r=4)
            for t in range(2):
                fns += [tt(lw4[:, t, s_], lo4[:, t], bc(oh[:, t, 1 - s_, :], 4), ALU.mult) for s_ in range(2)]
            yield from chain(dve, fns, ta)
            G.give(gi, dve_last())
            hi, lo = LW[:, :, :, 0:2, :].rearrange("p t s a d -> p (t s) a d"), \
                LW[:, :, :, 2:4, :].rearrange("p t s a d -> p (t s) a d")
            lfb = lf.rearrange("p t s d -> p (t s) d").unsqueeze(2).broadcast_to([128, 4, 2, 16])
            yield from chain(dve, [lambda e: e.tensor_copy(f32r(hi), lfb), tt(f32r(lo), lfb, hi, ALU.subtract)],
                             dve_last(), T.get(("LWread",)))
            tl = dve_last()
            bank, over, gi = yield from grab(G)
            for t in range(2):
                tp = mm(bank[:, 128 * t:128 * t + 128], f32r(LW[:, t].rearrange("p s a d -> p (s a d)")),
                        f32r(identr[:, :]), True, True, over, tl, mark=True)
                tr_ = mm(bank[:, 256 + 128 * t:384 + 128 * t], rho[:, t:t + 1].broadcast_to([128, 128]), ident[:, :],
                         True, True, mark=t == 1)
            T["LWread",] = tp
            yield
            te = acopy(f32r(LT[:, :]), bank[:, 0:256], [tp, tr_], T.get(("LTread",)))
            yield
            tb = acopy(rhoT[:, :], bank[:, 256:512], tr_, T.get(("LTread",)))
            G.give(gi, tb)
            yield
            ob, oover, og = yield from grab(G)
            for hf in range(2):
                R = R2[hf]
                ps, over, si = yield from grab(S2)
                for j in range(4):
                    f0 = 512 * hf + 128 * j
                    o = ps[:, 256 * j:256 * j + 256]
                    for c in range(2):
                        mm(o, WiT[:, c, f0:f0 + 128], zT[:, c, :], c == 0 and j % 2 == 0, False, over, P_("WiT"))
                    tp = mm(o, f32r(Bst[0:64, f0:f0 + 128]), f32r(LT[0:64, :]), False, True, te, mark=j == 3)
                    if j % 2 == 1:
                        yield
                ta = act.put(lambda e, R=R, ps=ps: e.activation(R, ps[:, :], ACT.Relu), tp, T.get(("Hread", hf)))
                yield
                for j in range(4):
                    f0 = 512 * hf + 128 * j
                    tp = mm(ps[:, 256 * j:256 * j + 256], f32r(Bst[64:128, f0:f0 + 128]), f32r(LT[64:128, :]), False,
                            True, ta, mark=j == 3)
                yield
                R4 = R.rearrange("p (j n) -> p j n", j=4)
                t2 = dve.put(tt(R4, R4, rhoT[:, :].unsqueeze(1).broadcast_to([128, 4, 256]), ALU.mult), ta, tb)
                yield
                th = dve.put(stt(R, ps[:, :], 0.0, R, ALU.max, ALU.add), tp, t2)
                S2.give(si, th)
                yield
                for t in range(2):
                    for j in range(4):
                        tp = mm(ob[:, 256 * t:256 * t + 256], R[:, 256 * j + 128 * t:256 * j + 128 * t + 128],
                                WoT[:, 4 * hf + j, :], hf + j + t == 0, hf == 1 and j == 3, oover, th, P_("WoT"),
                                mark=j == 3)
                    yield
                T["Hread", hf] = tp
            T["LTread",] = th
            for t in range(2):
                tx = dve.put(stt(xr[:, t, :], ob[:, 256 * t:256 * t + 256], w12[:, t, 0:1], xr[:, t, :], ALU.mult, ALU.add),
                             tp, tx, tq)
                yield
            G.give(og, tx)
            T["zread",] = tp
            T["rwread",] = tx
            sem = ctx.enter_context(nc.semaphore(f"d_out{b}"))
            T["out", b] = sp.dma(lambda e, xr=xr: e.dma_start(
                out[b].rearrange("(t p) d -> p t d", p=128), xr[:, :, :]), sem, 16, tx)
            outs.append(T["out", b])
            yield

        weave(thread(b_ffn, "F", None), thread(b_proj, "P", "F"), thread(b_max, "M", "P"), thread(b_loc, "L", "M"),
              thread(b_mix, "X", "L"), thread(b_moe, "E", "X"))
        sp.ops.append((lambda e: e.nop(), flat(outs), None))
        run_lanes(nc, ctx, (pe, act, dve, pool, sp))


def finish_up(nc, ctx, lanes, loads, taps, bufs, done):
    pe, act, dve, pool, sp = lanes
    n = 0
    for name, ap in taps["out"]:
        sem = ctx.enter_context(nc.semaphore(f"d_tap{name}"))
        src = bufs[name]
        n += 1
        tok = sp.dma(lambda e, ap=ap, src=src: e.dma_start(ap, src[:]), sem, 16, done)
        sp.ops.append((lambda e: e.nop(), flat(tok), None))
    run_lanes(nc, ctx, lanes)


def run_lanes(nc, ctx, lanes):
    pe, act, dve, pool, sp = lanes
    block = ctx.enter_context(nc.Block())

    @block.tensor
    def _(e):
        pe.play(e)

    @block.scalar
    def _(e):
        act.play(e)

    @block.vector
    def _(e):
        dve.play(e)

    @block.gpsimd
    def _(e):
        pool.play(e)

    @block.sync
    def _(e):
        sp.play(e)


def _inputs(inp):
    f = lambda k: np.asarray(inp[k])
    T_ = lambda a: np.ascontiguousarray(a.T)
    cat = lambda *a: np.ascontiguousarray(np.concatenate(a, axis=-1))
    q = np.arange(128)
    neg = np.float32(-1e30)

    def allow(m):
        return np.where(m, np.float32(0), neg).astype(np.float32)

    k0 = np.arange(128)
    m_t0 = allow((k0[None] <= q[:, None]) & (k0[None] > q[:, None] - 64))
    k1 = 64 + np.arange(192)
    m_t1 = allow((k1[None] <= 128 + q[:, None]) & (k1[None] > 128 + q[:, None] - 64))
    qa = np.arange(192)
    m_k0 = allow((qa[None] >= q[:, None]) & (qa[None] < q[:, None] + 64))
    qb = np.arange(128)
    m_k1 = allow((qb[None] >= q[:, None]) & (qb[None] < q[:, None] + 64))
    lat = np.arange(64)
    m_l = [allow(lat[None] <= (128 * t + q[:, None]) // 4) for t in range(2)]
    ql = np.arange(256)
    m_lt = allow((q[:, None] <= ql[None] // 4) & (q[:, None] < 64))
    masks = cat(m_t0, m_t1, m_k0, m_k1, m_l[0], m_l[1], m_lt)
    zsel = np.zeros((128, 24), np.float32)
    for r in (0, 24, 64, 88):
        zsel[r + np.arange(24), np.arange(24)] = 1
    hs = np.zeros((128, 2), np.float32)
    hs[:, 0] = (np.arange(128) // 16) % 2 == 0
    hs[:, 1] = 1 - hs[:, 0]
    ltm = np.array([[1.0 if j < i else 0.0 for j in range(4)] for i in range(4)], np.float32).reshape(16)
    c = "L0_cond_"
    a = "L0_attn_"
    w = "L0_ffn_"
    return {
        "x": f("x"), "condT": T_(f("cond_1024")), "ident": np.eye(128, dtype=np.float32), "masks": masks,
        "zsel": zsel, "hsel": hs, "ltm": ltm,
        "w_ada": f(c + "w_ada"), "b_ada": f(c + "b_ada"), "badaT": T_(f(c + "b_ada").reshape(12, 128)),
        "wqkv": cat(f(c + "w_q"), f(c + "w_k"), f(c + "w_v")), "bqkv": cat(f(c + "b_q"), f(c + "b_k"), f(c + "b_v")),
        "w_o": f(c + "w_o"), "b_o": f(c + "b_o"), "w1T": T_(f(c + "w_f1")), "b1c": T_(f(c + "b_f1").reshape(8, 128)),
        "w2": f(c + "w_f2"), "b_f2": f(c + "b_f2"),
        "wat": cat(f(a + "wq"), f(a + "wk"), f(a + "wv"), f(a + "wgq")), "wgkv": cat(f(a + "wgk"), f(a + "wgv")),
        "gl": f(a + "gate_local_w").reshape(256), "gr": f(a + "gate_remote_w").reshape(256),
        "r_out_w": f(a + "r_out_w"), "w_out": f(a + "w_out"), "weight": f("L0_cond2_weight"),
        "wrt": cat(T_(f(w + "Wg")), T_(f(w + "A").reshape(16, 256))), "bg": f(w + "bg"),
        "WiT": T_(f(w + "Wi")), "WoT": T_(f(w + "Wo")),
        "Bc": np.ascontiguousarray(np.transpose(f(w + "B"), (0, 2, 1)).reshape(16, 1024)),
    }


_OUT = (NB, S, D)


def kernel(**inputs):
    import concourse.bacc as _bacc
    from concourse.bass_utils import run_bass_kernel_spmd as _run

    nc = _bacc.Bacc("TRN2", target_bir_lowering=False, num_devices=1)
    arrays, args = {}, {}
    for name, a in _inputs(inputs).items():
        arrays[f"in_{name}"] = a
        args[name] = nc.dram_tensor(f"in_{name}", a.shape, F32, kind="ExternalInput").ap()
    o = nc.dram_tensor("out_0", _OUT, F32, kind="ExternalOutput").ap()
    program(nc, args, o)
    r = _run(nc, [arrays], core_ids=[0])
    return r.results[0]["out_0"]
```

```python
import math
from contextlib import ExitStack

import numpy as np

import concourse.bass as bass
from concourse import mybir

F32 = mybir.dt.float32
F32R = mybir.dt.float32r
BF16 = mybir.dt.bfloat16
I32 = mybir.dt.int32
ALU = mybir.AluOpType
ACT = mybir.ActivationFunctionType
AX = mybir.AxisListType

NB, S, D, FF = 16, 256, 256, 1024
NT = 2 * NB
EPS = 1e-7
TMAX = float(np.float32(1.0 - 1e-5))
CL = math.atanh(TMAX)


def _beta(a, b):
    return math.exp(math.lgamma(a) + math.lgamma(b) - math.lgamma(a + b))


RT = _beta(8, 0.5) / _beta(128, 0.5)


class Meter:

    def __init__(self, fixed, each):
        self.fixed, self.each = fixed, each

    def time(self, ap, more=0):
        return self.fixed + more + self.each * int(np.prod(ap.shape[1:]))

    def activation(self, o, i, func, bias=0.0, scale=1.0, accum_out=None):
        return self.time(o, 90 * (not isinstance(scale, float)) + 135 * (accum_out is not None))

    def tensor_scalar(self, o, *a):
        return self.time(o)

    def tensor_tensor(self, o, *a):
        return self.time(o)

    def tensor_copy(self, o, i):
        return self.time(o)

    def memset(self, o, v):
        return self.time(o)

    def reciprocal(self, o, i):
        return self.time(o)

    def scalar_tensor_tensor(self, out, **k):
        return self.time(out)

    def tensor_tensor_reduce(self, out, **k):
        return self.time(out)

    def tensor_reduce(self, o, i, *a, **k):
        return self.time(i)

    def bn_stats(self, o, i):
        return self.time(i)

    def bn_aggr(self, o, i):
        return self.time(i)


class Lane:

    done, latest = {}, 0

    def __init__(self, nc, ctx, name, usual=100, limit=16000):
        self.free, self.usual = 0, usual
        self.nc, self.ctx, self.name, self.limit = nc, ctx, name, limit
        self.ops, self.count, self.turn = [], limit, 0

    def put(self, fn, *after, mark=True, cost=None):
        after = flat(after)
        start = max([self.free] + [Lane.done.get((s.name, v), 0) + self.notice(s) for s, v in after])
        if cost is None:
            cost = self.usual if isinstance(self.usual, int) else fn(self.usual)
        self.free = start + cost
        Lane.latest = max(Lane.latest, self.free)
        token = None
        if mark:
            if self.count >= self.limit:
                self.sem = self.ctx.enter_context(self.nc.semaphore(f"s_{self.name}{self.turn}"))
                self.turn += 1
                self.count = 0
            self.count += 1
            token = (self.sem, self.count)
            Lane.done[self.sem.name, self.count] = self.free
        self.ops.append((fn, after, token))
        return token

    def notice(self, sem):
        src = sem.name.split("_")[1][:3]
        if src.startswith("pe"):
            return 197
        if self.name == "pe":
            return 240
        return 34 if src == "act" == self.name else 152 if src == "act" else 128

    def dma(self, fn, sem, value, *after):
        self.ops.append((fn, flat(after), (sem, 16)))
        return (sem, value)

    def play(self, eng):
        seen = {}
        for fn, after, token in self.ops:
            for sem, value in after:
                if seen.get(sem.name, 0) < value:
                    seen[sem.name] = value
                    eng.wait_ge(sem, value)
            ins = fn(eng)
            if token is not None:
                ins.then_inc(token[0], 16 if token[1] == 16 and "d_" in token[0].name else 1)


def flat(x):
    if x is None:
        return []
    if isinstance(x, tuple) and len(x) == 2 and isinstance(x[1], int) and not isinstance(x[0], (tuple, list)):
        return [x]
    return [t for y in x for t in flat(y)]


class Ring:

    def __init__(self, tiles):
        self.tiles, self.free = tiles, [(None, i) for i in range(len(tiles))]

    def take(self):
        assert self.free, "no tile is free"
        self.free.sort(key=lambda f: max([Lane.done.get((t[0].name, t[1]), 0) for t in flat(f[0])] + [0]))
        over, i = self.free.pop(0)
        return self.tiles[i], over, i

    def give(self, i, *over):
        self.free.append((flat(over), i))


def grab(ring):
    while not ring.free:
        yield None
    when = min(max([Lane.done.get((t[0].name, t[1]), 0) for t in flat(f[0])] + [0]) for f in ring.free)
    yield when - 100
    while not ring.free:
        yield None
    return ring.take()


def weave(*threads):
    start = max([0] + [Lane.latest])
    live = [[start, i, g, False] for i, g in enumerate(threads)]
    idle = 0
    while live:
        live.sort(key=lambda x: x[:2])
        s = live[0]
        Lane.latest = 0
        try:
            hint = next(s[2])
        except StopIteration:
            live.pop(0)
            idle = 0
            continue
        if Lane.latest:
            s[0], s[3], idle = Lane.latest, False, 0
        elif isinstance(hint, (int, float)) and hint > s[0]:
            s[0], s[3] = hint, False
        elif isinstance(hint, (int, float)):
            idle = 0
        else:
            idle += 1
            assert idle < 50 * len(live), "the stages wait for each other"
            s[3] = True
            s[0] = max(s[0], min([x[0] for x in live if not x[3]] or [s[0]])) + 1


def program(nc, A, out, nb=NB):
    ctx = ExitStack()
    with ctx:
        def sb(name, shape, dt=F32):
            return ctx.enter_context(nc.sbuf_tensor(name, shape, dt))

        pe, act, dve, pool, sp = (
            Lane(nc, ctx, *n) for n in (("pe", 107), ("act", Meter(53, 0.83)),
                                      ("dve", Meter(60, 1.04)), ("pool", Meter(100, 2.4)), ("sp", 0)))
        Lane.done, Lane.latest = {}, 0
        loads = {}

        def load(name, dst, src, lane=sp, *after):
            sem = ctx.enter_context(nc.semaphore(f"d_{name}"))
            loads[name] = lane.dma(lambda e: e.dma_start(dst, src), sem, 16, *after)
            return loads[name]

        G = Ring([ctx.enter_context(nc.psum_tensor(f"pG{i}", [128, 512], F32)) for i in range(8)])

        X = sb("X", [128, NT, D])
        X1 = X
        GR = sb("GR", [128, 1536])
        XR = [sb(f"XR{i}", [128, 2, D]) for i in range(2)]
        ident = sb("ident", [128, 128])
        identb = sb("identb", [128, 128], BF16)
        identr = sb("identr", [128, 128])
        maskb = sb("maskb", [128, 320 + 320 + 128 + 256], BF16)
        zsel = sb("zsel", [128, 24])
        zselr = sb("zselr", [128, 24])
        hsel = sb("hsel", [128, 2])
        condT = sb("condT", [128, 2, 16])
        adaT = sb("adaT", [128, 12, 16])
        badaT = sb("badaT", [128, 12])
        grow = sb("grow", [16, 512])
        b2 = sb("b2", [128, D])
        b1w2 = sb("b1w2", [128, 258])
        W12 = sb("W12", [128, 2, 256])
        GG = sb("GG", [128, 2, 258])
        wat = sb("wat", [128, 2, 928])
        wgkv = sb("wgkv", [128, 2, 256])
        wr = sb("wr", [128, D])
        wout = sb("wout", [128, 2, D])
        w2c = sb("w2c", [128, 2, D])
        dT = sb("dT", [128, 2, 16])
        ysT = sb("ysT", [128, 2, 16])
        WiT = sb("WiT", [128, 2, FF])
        WoT = sb("WoT", [128, 8, D])
        wrt = sb("wrt", [128, 2, 20])
        bg = sb("bg", [128, 4])
        ltm = sb("ltm", [128, 16])
        Bst = sb("Bst", [128, FF])
        mv = sb("mv", [128, NT, 2])
        bn = sb("bn", [128, 4, 6])
        rX, ssX, rX1, ssX1 = (sb(n, [128, NT]) for n in ("rX", "ssX", "rX1", "ssX1"))
        lp = sb("lp", [128, 10, NT])
        FR = sb("FR", [128, 8192])
        FA = sb("FA", [128, 10752])
        RND = sb("RND", [128, 2048])

        frp, fap = [0], [0]

        FW = sb("FW", [128, 3072])
        SQ = sb("SQ", [128, 2, 768])
        fwp = [0]

        def cut(arena, ptr, *shape):
            n = int(np.prod(shape))
            a = arena[:, ptr[0]:ptr[0] + n]
            ptr[0] += n
            assert ptr[0] <= arena.shape[1], (ptr, arena.shape)
            names = "abcdef"[:len(shape)]
            if len(shape) == 1:
                return a
            kw = {names[i]: shape[i] for i in range(1, len(shape))}
            return a.rearrange(f"p ({' '.join(names)}) -> p {' '.join(names)}", **kw)

        def bc(ap, n):
            shape = list(ap.shape)
            return ap.unsqueeze(len(shape)).broadcast_to(shape + [n])

        def chain(lane, fns, *after):
            tok = after
            for fn in fns:
                tok = lane.put(fn, tok)
                yield

        def size(ap):
            return int(np.prod(ap.shape[1:]))

        def thread(fn, name, before, *free):
            for b in range(nb):
                if before:
                    yield from need(before, b)
                for kind, lag in free:
                    yield from need(kind, b - lag)
                yield from fn(b)
                T[name, b] = True

        def need(kind, b):
            while b >= 0 and (kind, b) not in T:
                yield

        def ts(o, i, s1, s2, op0, op1=None):
            if op1 is None:
                return lambda e: e.tensor_scalar(o, i, s1, None, op0)
            return lambda e: e.tensor_scalar(o, i, s1, s2, op0, op1)

        def tt(o, a, b, op):
            return lambda e: e.tensor_tensor(o, a, b, op)

        def stt(o, a, s, b, op0, op1):
            return lambda e: e.scalar_tensor_tensor(out=o, in0=a, scalar=s, in1=b, op0=op0, op1=op1)

        def red(o, i, op=ALU.add, negate=False):
            return lambda e: e.tensor_reduce(o, i, AX.X, op, negate=negate)

        def rsqrt(x, y, a, b):
            fns = [ts(a.bitcast(I32), x.bitcast(I32), 1, None, ALU.logical_shift_right),
                   ts(y.bitcast(I32), a.bitcast(I32), -1.0, float(0x5F3759DF), ALU.mult, ALU.add)]
            for _ in range(3):
                fns += [tt(a, y, y, ALU.mult), stt(b, a, -0.5, x, ALU.mult, ALU.mult),
                        stt(y, b, 1.5, y, ALU.add, ALU.mult)]
            return fns

        def mm(o, lhsT, rhs, start, stop, *after, mark=False):
            passes = 4 if rhs.dtype == F32 else 1
            cost = max(passes * size(rhs), 128 * passes) / 2.4 / (4 if lhsT.shape[-1] == 32 else 1)
            return pe.put(lambda e: e.matmul(o, lhsT, rhs, start=start, stop=stop, skip_group_check=True),
                          *after, mark=mark, cost=cost)

        def tr(o, i, *after, mark=False):
            return pe.put(lambda e: e.transpose(o, i, ident[:, :]), *after, mark=mark)

        def acopy(o, i, *after):
            return act.put(lambda e: e.activation(o, i, ACT.Copy), *after)

        def evac(o, i, *after):
            return acopy(o, i, *after)

        wqkv, bqkv, wo, bo = (cut(FW, fwp, *n) for n in ((2, 768), (768,), (2, D), (D,)))

        xv = A["x"].rearrange("b (t p) d -> p (b t) d", p=128)
        load("cond", condT[:, :, :], A["condT"].rearrange("(c p) b -> p c b", p=128))
        load("ident", ident[:, :], A["ident"])
        wada = cut(FA, [0], 2, 1536)
        w1T = cut(FA, [3584], 8, 258)
        w2x = cut(FA, [3584 + 2064], 8, 256)
        b1c = cut(FA, [3584 + 2048 + 2064], 8)
        brow = SQ[0:16, 0, 0:512]
        early = [WiT.rearrange("p c n -> p (c n)"), WoT.rearrange("p c n -> p (c n)")]
        mf, Bf, Bh = early[0][:, 0:1024], early[0][:, 1024:2048], early[0][:, 0:1024]
        gate = cut(early[1], [0], 2, 256)
        gtmp = cut(early[1], [512], 2, 2, 256)
        w2sq = cut(early[1], [1536], 2, 256)

        def load_x(q, lane):
            load(f"x{q}", X[:, 8 * q:8 * q + 8, :], xv[:, 8 * q:8 * q + 8, :], lane)

        load_x(0, act)
        load("wada", wada, A["w_ada"].rearrange("(c p) n -> p c n", p=128))
        load("bada", badaT[:, :], A["badaT"])
        load("b1c", b1c, A["b1c"], act)
        load("w1T", w1T[:, :, 0:256], A["w1T"].rearrange("(c p) n -> p c n", p=128))
        load("w2", w2x, A["w2"].rearrange("(c p) n -> p c n", p=128), act)
        load("brow0", brow[:, 0:256], A["b_ada"][512:768].partition_broadcast(16))
        load("brow1", brow[:, 256:512], A["b_ada"][1280:1536].partition_broadcast(16))
        load("wqkv", wqkv, A["wqkv"].rearrange("(c p) n -> p c n", p=128))
        load("bqkv", bqkv[:, :], A["bqkv"].partition_broadcast(128), act)
        load("wo", wo, A["w_o"].rearrange("(c p) n -> p c n", p=128))
        load("bo", bo[:, :], A["b_o"].partition_broadcast(128), act)
        load_x(1, sp)
        load_x(2, act)
        load_x(3, sp)
        load("mf", mf, A["masks"], act)
        load("wat", wat[:, :, 0:896], A["wat"].rearrange("(c p) n -> p c n", p=128))
        load("zsel", zsel[:, :], A["zsel"])
        load("hsel", hsel[:, :], A["hsel"])
        load("gate0", gate[:, 0, :], A["gl"].partition_broadcast(128))
        load("gate1", gate[:, 1, :], A["gr"].partition_broadcast(128))
        load("w2c", w2c[:, :, :], A["weight"].rearrange("(c p) n -> p c n", p=128))
        for r in range(8):
            load(f"B{r}", Bf[16 * r:16 * r + 16, :], A["Bc"])
        load("wgkv", wgkv[:, :, :], A["wgkv"].rearrange("(c p) n -> p c n", p=128))
        load("ltm", ltm[:, :], A["ltm"].partition_broadcast(128))
        load("b2", b2[:, :], A["b_f2"].partition_broadcast(128))
        load("wr", wr[:, :], A["r_out_w"])
        load("wout", wout[:, :, :], A["w_out"].rearrange("(c p) n -> p c n", p=128))
        load("wrt", wrt[:, :, :], A["wrt"].rearrange("(c p) n -> p c n", p=128))
        load("bg", bg[:, :], A["bg"].partition_broadcast(128))

        def ln_prep(mean, var, ss, r, n, *after):
            a, b, y, t, z, p, q, m = (lp[:, i, 0:n] for i in range(8))
            yield from chain(dve, [
                tt(a, mean, mean, ALU.mult), tt(a, a, var, ALU.add),
                ts(ss, a, 256.0, 0.0, ALU.mult, ALU.add), ts(z, ss, EPS * EPS, None, ALU.max)], *after)
            yield from chain(dve, rsqrt(z, y, a, b), dve_last())
            yield from chain(dve, [tt(t, z, y, ALU.mult), ts(t, t, TMAX, None, ALU.min),
                                   ts(q, t, -1.0, 1.0, ALU.mult, ALU.add)], dve_last())
            yield from chain(dve, [lambda e: e.reciprocal(b, q), stt(q, t, 1.0, b, ALU.add, ALU.mult)], dve_last())
            tok = act.put(lambda e: e.activation(p, q, ACT.Ln), dve_last())
            yield from chain(dve, [
                tt(z, t, t, ALU.mult), ts(a, z, 1.0 / 11, None, ALU.mult),
                stt(a, a, 1.0 / 9, z, ALU.add, ALU.mult), stt(a, a, 1.0 / 7, z, ALU.add, ALU.mult),
                stt(a, a, 1.0 / 5, z, ALU.add, ALU.mult), stt(a, a, 1.0 / 3, z, ALU.add, ALU.mult),
                stt(a, a, 1.0, t, ALU.add, ALU.mult), ts(m, t, 0.25, None, ALU.is_lt),
                stt(a, p, -0.5, a, ALU.mult, ALU.add), tt(a, a, m, ALU.mult),
                stt(a, p, 0.5, a, ALU.mult, ALU.add), tt(q, a, y, ALU.mult),
                tt(a, q, q, ALU.mult), tt(a, a, var, ALU.mult), ts(z, a, 1e-6, None, ALU.add)], dve_last(), tok)
            yield from chain(dve, rsqrt(z, y, a, b), dve_last())
            yield from chain(dve, [tt(r, q, y, ALU.mult)], dve_last())

        def dve_last():
            return (dve.sem, dve.count)

        def act_last():
            return (act.sem, act.count)

        def pool_last():
            return (pool.sem, pool.count)

        T = {}
        NN = 2 * nb

        def prep(i0, i1, mv_, ss, r, *after):
            yield from ln_prep(mv_[:, i0:i1, 0], mv_[:, i0:i1, 1], ss[:, i0:i1], r[:, i0:i1], i1 - i0, *after)

        def stats(i0, i1):
            for i in range(i0, i1):
                k = i % 4
                t1 = dve.put(lambda e, i=i, k=k: e.bn_stats(bn[:, k, :], X[:, i, :]), loads[f"x{i // 8}"], T.get(("bn", k)))
                T["bn", k] = dve.put(lambda e, i=i, k=k: e.bn_aggr(mv[:, i, :], bn[:, k, :]), t1)
                yield
            yield from prep(i0, i1, mv, ssX, rX, T["bn", (i1 - 1) % 4])

        FIRST = min(8, NN)
        for _ in stats(0, FIRST):
            pass

        def P_(t):
            return loads[t]

        tb = pool.put(lambda e: e.tensor_copy(identb[:, :], ident[:, :]), P_("ident"))
        pool.put(lambda e: e.tensor_copy(identr[:, :].bitcast(F32R), ident[:, :]), P_("ident"))
        t1 = pool.put(lambda e: e.memset(w1T[:, :, 257:258], 0.0))
        tb = pool.put(lambda e: e.tensor_copy(w1T[:, :, 256:257], b1c.unsqueeze(2)), P_("b1c"))
        consts = pool_last()

        bank, over, gi = G.take()
        for j in range(12):
            for c in range(2):
                t1 = mm(bank[:, 16 * j:16 * j + 16], wada[:, c, 128 * j:128 * j + 128], condT[:, c, :], c == 0, c == 1,
                        P_("wada"), P_("cond"), mark=j == 11 and c == 1)
        for j in range(12):
            o, i = adaT[:, j, :], bank[:, 16 * j:16 * j + 16]
            if j in (2, 3, 8, 9):
                t2 = dve.put(ts(o, i, badaT[:, j:j + 1], 1.0, ALU.add, ALU.add), t1, P_("bada"))
            else:
                t2 = dve.put(ts(o, i, badaT[:, j:j + 1], None, ALU.add), t1, P_("bada"))
        G.give(gi, t2)
        bank, over, gi = G.take()
        wg2 = wada.rearrange("p c (s k n) -> p c s k n", s=2, k=3)[:, :, :, 2, :]
        for c in range(2):
            t1 = mm(bank[0:16, :].rearrange("p (s n) -> p s n", s=2), condT[:, c, :], wg2[:, c], c == 0, c == 1, over,
                    mark=c == 1)
        T["grow"] = dve.put(tt(grow[:, :], bank[0:16, :], brow[:, :], ALU.add), t1, P_("brow0"), P_("brow1"))
        wada_read = t1
        G.give(gi, T["grow"])

        for ic in range(2):
            for dst, w, n in ((W12, w2x, 256), (GG, w1T, 258)):
                bank, over, gi = G.take()
                for f in range(8):
                    t1 = mm(bank[:, 0:n], w1T[:, f, 128 * ic:128 * ic + 128], w[:, f, 0:n], f == 0, f == 7, over,
                            P_("w1T"), P_("w2"), consts, mark=f == 7)
                t2 = evac(dst[:, ic, :], bank[:, 0:n], t1)
                G.give(gi, t2)
                T["w12", ic, n] = t2
        bank, over, gi = G.take()
        for f in range(8):
            t1 = mm(bank[:, 0:256], b1c[:, f:f + 1].broadcast_to([128, 128]), w2x[:, f, :], f == 0, f == 7, over)
        for f in range(8):
            t1 = mm(bank[:, 256:258], b1c[:, f:f + 1].broadcast_to([128, 128]), w1T[:, f, 256:258], f == 0, f == 7,
                    mark=f == 7)
        T["b1w2"] = evac(b1w2[:, :], bank[:, 0:258], t1)
        G.give(gi, T["b1w2"])
        setup_done = [dve_last(), act_last(), pool_last(), T["b1w2"],
                      pe.put(lambda e: e.matmul(bank[0:2, 100:102], ident[:, 0:2], ident[:, 0:2], start=True, stop=True),
                             dve_last(), T["b1w2"], P_("ident"))]

        frp[0], fap[0] = 0, 0
        QsT = [cut(FR, frp, 8, 256) for _ in range(2)]
        KsT = [cut(FR, frp, 8, 256) for _ in range(2)]
        PT = Ring([cut(FA, fap, 512) for _ in range(8)])
        tT = cut(FA, fap, 2, 256)
        mTs = [cut(FA, fap, 2, 256), XR[0]]
        HL = RND[:, :].rearrange("p (g h a d) -> p g h a d", g=2, h=16, a=4)
        Vg = [cut(FA, fap, 2, 16, 32) for _ in range(2)]
        U = [cut(FA, fap, 768) for _ in range(2)] + [SQ[:, 1, :]]
        OT = cut(FA, fap, 4, 256)
        O = cut(FA, fap, 2, 256)
        xn = cut(FA, fap, 2, 256)
        JK = sb("JK", [128, 2, 256])
        Z = sb("Z", [128, 2, 256])
        UOs = [sb(f"UO{i}", [128, 2, 256]) for i in range(2)]
        sm = sb("sm", [128, 64, 2])
        hall = sb("hall", [128, 520])
        h_a, h_b0, h_y, h_s, h_b1 = (hall[:, 104 * i:104 * i + 104].rearrange("p (t n) -> p t n", t=2) for i in range(5))
        k_a, k_b, k_y, k_s, k_f = (sb(n, [128, 2, 16]) for n in ("k_a", "k_b", "k_y", "k_s", "k_f"))

        for v in range(2):
            a = pool.put(lambda e, m=Vg[v]: e.memset(m, 0.0), setup_done)
            T["vg", v] = pool.put(lambda e, m=Vg[v]: e.memset(m[:, :, :, 16:17], 1.0), a)
        ph1 = [setup_done, T["vg", 1], [P_(k) for k in ("wqkv", "bqkv", "wo", "bo")]]

        def s_mod(b, src, mean, r, sh, base, mT, so, lag, *after):
            for t in range(2):
                i = 2 * b + t
                tk = pool.put(ts(xn[:, t, :], src[:, i, :], mean[:, i:i + 1], r[:, i:i + 1], ALU.subtract, ALU.mult), *after, T.get(("xnT", base, b - 1)))
                yield
            bank, over, gi = yield from grab(G)
            for t in range(2):
                for c in range(2):
                    tp = tr(bank[:, 256 * c + 128 * t:256 * c + 128 * t + 128], xn[:, t, 128 * c:128 * c + 128], over, tk,
                            mark=t + c == 2)
            T["xnT", base, b] = tp
            yield
            for c in range(2):
                tk = act.put(lambda e, c=c, bank=bank: e.activation(mT[:, c, :], bank[:, 256 * c:256 * c + 256], ACT.Identity,
                                                         bias=adaT[:, sh + c, b:b + 1], scale=adaT[:, sh + 2 + c, b:b + 1]),
                             tp, T.get(("mTread", base, b - lag)))
                yield
            G.give(gi, tk)
            T["mT", base, b] = tk
            bank, over, gi = yield from grab(G)
            for t in range(2):
                for c in range(2):
                    tp = tr(bank[:, 256 * t + 128 * c:256 * t + 128 * c + 128], mT[:, c, 128 * t:128 * t + 128], over, tk,
                            mark=t + c == 2)
            for t in range(2):
                tk = act.put(lambda e, t=t, bank=bank: e.activation(JK[:, t, :], bank[:, 256 * t:256 * t + 256], ACT.Square,
                                                         accum_out=sm[:, so, t:t + 1]), tp, T.get(("sm0", base, b - lag)),
                             T.get(("jk",)))
                T["jk",] = tk
                yield
            T["mss", base, b] = tk
            T["mbank"] = (bank, gi, tk, tp)

        def s_norm(b):
            so = 32 * (b % 2)
            yield from need("Q", b - 2)
            while b > 3 and ("prep",) not in T:
                yield
            yield from s_mod(b, X, mv[:, :, 0], rX, 0, 1, mTs[b % 2], so, 2, ph1, T["prep",] if b > 3 else None)
            bank, gi, tk, tp = T["mbank"]
            G.give(gi, tk)
            z, y, a, c_ = (sm[:, so + i, :] for i in (1, 2, 3, 4))
            yield from chain(dve, [ts(z, sm[:, so, :], EPS * EPS, None, ALU.max)] + rsqrt(z, y, a, c_)
                             + [ts(y, y, CL, 1.0, ALU.mult, ALU.min)], T["mss", 1, b], T.get(("Uw", b - 2)))
            T["sm0", 1, b] = dve_last()

        def s_qkv(b):
            so, mT, s1 = 32 * (b % 2), mTs[b % 2], T["sm0", 1, b]
            h_b = (h_b0, h_b1)[b % 2]
            yield from need("K", b - 2)
            for t in range(2):
                while 2 * b + t >= 3 and ("Uread", 2 * b + t - 3) not in T:
                    yield
                war, u = T.get(("Uread", 2 * b + t - 3)), U[(2 * b + t) % 3]
                b0, o0, g0 = yield from grab(G)
                for c in range(2):
                    t0 = mm(b0[:, :], mT[:, c, 128 * t:128 * t + 128], wqkv[:, c, 0:512], c == 0, c == 1, o0,
                            T["mT", 1, b], mark=c == 1)
                yield
                b1, o1, g1 = yield from grab(G)
                for c in range(2):
                    t1 = mm(b1[:, 0:256], mT[:, c, 128 * t:128 * t + 128], wqkv[:, c, 512:768], c == 0, c == 1, o1,
                            mark=c == 1)
                yield
                tk = dve.put(stt(u[:, 0:512], b0[:, :], sm[:, so + 2, t:t + 1], bqkv[:, 0:512], ALU.mult, ALU.add), t0, s1, war)
                G.give(g0, tk)
                yield
                tk = dve.put(stt(u[:, 512:768], b1[:, 0:256], sm[:, so + 2, t:t + 1], bqkv[:, 512:768], ALU.mult, ALU.add),
                             t1, s1, war)
                G.give(g1, tk)
                T["Uw", b] = tk
                yield
                tk = act.put(lambda e, u=u: e.activation(SQ[:, 0, :], u, ACT.Square), tk, T.get(("sq",)))
                yield
                T["sq",] = T["hss", b, t] = dve.put(red(h_s[:, t, 0:48], SQ[:, 0, :].rearrange("p (h d) -> p h d", d=16)), tk,
                                         T.get(("hf", b - 1)))
                yield
            T["mTread", 1, b] = t1
            hf = [red(h_s[:, :, 48:51], h_s[:, :, 0:48].rearrange("p t (g h) -> p t g h", g=3)),
                  ts(h_s[:, :, 0:51], h_s[:, :, 0:51], EPS * EPS, None, ALU.max)]
            hf += rsqrt(h_s[:, :, 0:51], h_y[:, :, 0:51], h_a[:, :, 0:51], h_b[:, :, 0:51])
            hf += [ts(h_a[:, :, 48:51], h_y[:, :, 48:51], CL, 1.0, ALU.mult, ALU.min),
                   ts(h_a[:, :, 48:51], h_a[:, :, 48:51], RT, None, ALU.mult)]
            yield from chain(dve, hf, [T["hss", b, t] for t in range(2)], T.get(("hread", b - 2)), T.get(("hf", b - 1)))
            for t in range(2):
                tk = dve.put(stt(h_b[:, t, 0:48].rearrange("p (g h) -> p g h", g=3),
                                 h_y[:, t, 0:48].rearrange("p (g h) -> p g h", g=3), CL,
                                 bc(h_a[:, t, 48:51], 16), ALU.mult, ALU.min), dve_last())
            T["hf", b] = tk

        def s_heads(b):
            h_b, tk = (h_b0, h_b1)[b % 2], T["hf", b]
            vg = Vg[b % 2]
            yield from need("A0", b - 2)
            yield from need("A1", b - 2)
            for t in range(2):
                uv = U[(2 * b + t) % 3].rearrange("p (h d) -> p h d", d=16)
                tq = dve.put(tt(uv[:, 0:32], uv[:, 0:32], bc(h_b[:, t, 0:32], 16), ALU.mult), tk)
                yield
                for g in range(2):
                    ug = uv[:, 16 * g:16 * g + 16].unsqueeze(2).broadcast_to([128, 16, 2, 16])
                    hi, lo = hilo(HL[:, g], g)
                    th = act.put(lambda e, hi=hi, ug=ug: e.activation(hi, ug, ACT.Copy), tq, T.get(("hlread", g)))
                    yield
                    T["hl", g] = dve.put(tt(lo, ug, HL[:, g, :, 0, :].unsqueeze(2).broadcast_to([128, 16, 2, 16]),
                                            ALU.subtract), th, T.get(("hlread", g)))
                    yield
                    if g == 0:
                        tv = dve.put(tt(vg[:, t, :, 0:16], uv[:, 32:48], bc(h_b[:, t, 32:48], 16), ALU.mult), tk,
                                     T.get(("pv", b - 2)))
                        yield
                    yield from stack(HL[:, g], 8, (QsT, KsT)[g][b % 2], t, T["hl", g], T.get(("scores", b - 2)))
                    T["hlread", g] = T["stackT"]
                T["Uread", 2 * b + t] = [T["hl", 1], tv]
            T["st", b] = T["stdone"]
            T["Vg", b] = tv
            T["hread", b] = [tq, tv]

        def hilo(v, kind):
            v = v.bitcast(F32R)
            return (v[:, :, 0:2, :], v[:, :, 2:4, :]) if kind == 0 else (v[:, :, 0:4:2, :], v[:, :, 1:4:2, :])

        def stack(hl, npair, dst, t, ready, war):
            flat_ = hl.rearrange("p h a d -> p (h a d)")
            for p4 in range(npair // 4):
                bank, over, gi = yield from grab(G)
                for j in range(4):
                    tp = mm(bank[:, 128 * j:128 * j + 128],
                            flat_[:, 512 * p4 + 128 * j:512 * p4 + 128 * j + 128].bitcast(F32R),
                            identr[:, :].bitcast(F32R), True, True, over, ready, mark=j == 3)
                tk = evac(dst[:, 4 * p4:4 * p4 + 4, 128 * t:128 * t + 128].bitcast(F32R),
                          bank[:, :].rearrange("p (a n) -> p a n", a=4), tp, war)
                G.give(gi, tk)
                yield
            T["stackT"] = tp
            T["stdone"] = [act_last(), dve_last()]

        def s_att(b, half):
            q_, k_, vg = QsT[b % 2], KsT[b % 2], Vg[b % 2]
            ready = T["st", b]
            pend = []
            for h in range(8 * half, 8 * half + 8):
                ps, over, si = yield from grab(G)
                r = 64 * (h % 2)
                for kt in range(2):
                    tp = mm(ps[:, 256 * kt:256 * kt + 256], k_[r:r + 64, h // 2, 128 * kt:128 * kt + 128].bitcast(F32R),
                            q_[r:r + 64, h // 2, :].bitcast(F32R), True, True, over, ready, mark=kt == 1)
                yield
                pt, over, pi = yield from grab(PT)
                tk = act.put(lambda e, pt=pt, ps=ps: e.activation(pt, ps[:, :], ACT.Exp, scale=0.25), tp, over)
                G.give(si, tk)
                pend.append((pt, pi, tk))
                yield
                if h == 8 * half + 7:
                    T["scores", b] = tp
                if h % 4 == 3:
                    g = h // 4
                    if g % 2 == 0:
                        po, oover, oi = yield from grab(G)
                    for kt in range(2):
                        for j in range(4):
                            pt, pi, tk = pend[j]
                            tp = mm(po[32 * j:32 * j + 32, 256 * (g % 2):256 * (g % 2) + 256], vg[:, kt, 4 * g + j, :],
                                    pt[:, 256 * kt:256 * kt + 256], kt == 0, kt == 1,
                                    oover, T["Vg", b], pend[3][2], mark=kt == 1 and j == 3)
                        yield
                    for pt, pi, tk in pend:
                        PT.give(pi, tp)
                    pend = []
                    T["pv", b] = tp
                    if g % 2 == 1:
                        yield from need("OTread", b - 1)
                        tk = evac(OT[:, g - 1:g + 1, :], po[:, :].rearrange("p (a n) -> p a n", a=2), tp,
                                  T.get(("OTread", b - 1)))
                        G.give(oi, tk)
                        T["OT", b, g // 2] = tk
                        yield

        def s_out(b):
            yield from need("A1", b)
            ready = [T["OT", b, 0], T["OT", b, 1]]
            for t in range(2):
                bank, over, gi = yield from grab(G)
                for g in range(4):
                    tp = tr(bank[:, 128 * g:128 * g + 128], OT[:, g, 128 * t:128 * t + 128], over, ready, mark=g == 3)
                bv = bank[:, :].rearrange("p (h n) -> p h n", n=32)
                yield
                tk = dve.put(lambda e, t=t, bv=bv: e.reciprocal(k_f[:, t, :], bv[:, :, 16]), tp, T.get(("kf", b - 1)))
                ov = O[:, t, :].rearrange("p (h d) -> p h d", d=16)
                yield
                to = dve.put(tt(ov, bv[:, :, 0:16], bc(k_f[:, t, :], 16), ALU.mult), tk, T.get(("Oread", b - 1)))
                G.give(gi, to)
                yield
                tq = act.put(lambda e, t=t: e.activation(JK2[:, t, :], O[:, t, :], ACT.Square), to,
                             T.get(("ks", b - 1, t)))
                yield
                T["ks", b, t] = dve.put(red(k_s[:, t, :], JK2[:, t, :].rearrange("p (h d) -> p h d", d=16)), tq)
                yield
            T["OTread", b] = tp
            n1, z1, y1, a1, c1 = (sm[:, i, :] for i in (5, 6, 7, 8, 9))
            fns = [ts(k_s[:, :, :], k_s[:, :, :], EPS * EPS, None, ALU.max)]
            fns += rsqrt(k_s[:, :, :], k_y[:, :, :], k_a[:, :, :], k_b[:, :, :])
            fns += [ts(k_y[:, :, :], k_y[:, :, :], CL / RT, 1.0 / RT, ALU.mult, ALU.min),
                    tt(k_a[:, :, :], k_y[:, :, :], k_y[:, :, :], ALU.mult),
                    tt(k_a[:, :, :], k_a[:, :, :], k_s[:, :, :], ALU.mult),
                    red(z1, k_a[:, :, :]), ts(z1, z1, EPS * EPS, None, ALU.max)]
            fns += rsqrt(z1, y1, a1, c1) + [ts(y1, y1, CL, 1.0, ALU.mult, ALU.min)]
            yield from chain(dve, fns, T["ks", b, 0], T["ks", b, 1])
            tk = dve_last()
            for t in range(2):
                ov = O[:, t, :].rearrange("p (h d) -> p h d", d=16)
                tv = dve.put(tt(ov, ov, bc(k_y[:, t, :], 16), ALU.mult), tk)
                yield
            T["kf", b] = tv
            bank, over, gi = yield from grab(G)
            for t in range(2):
                for c in range(2):
                    tp = tr(bank[:, 256 * c + 128 * t:256 * c + 128 * t + 128], O[:, t, 128 * c:128 * c + 128], over, tv,
                            mark=t + c == 2)
            T["Oread", b] = tp
            yield
            te = evac(tT, bank[:, :].rearrange("p (c n) -> p c n", c=2), tp, T.get(("tTread", b - 1)))
            G.give(gi, te)
            yield
            bank, over, gi = yield from grab(G)
            for t in range(2):
                for c in range(2):
                    tp = mm(bank[:, 256 * t:256 * t + 256], tT[:, c, 128 * t:128 * t + 128], wo[:, c, :], c == 0, c == 1,
                            over, te, mark=t + c == 2)
            T["tTread", b] = tp
            yield
            yield from need("Y", b - 2)
            for t in range(2):
                tu = dve.put(stt(UOs[b % 2][:, t, :], bank[:, 256 * t:256 * t + 256], sm[:, 7, t:t + 1], bo[:, :], ALU.mult, ALU.add),
                             tp, tk, T.get(("UOread", b - 2)))
                yield
            G.give(gi, tu)
            T["UO", b] = tu

        def s_fin(b):
            yield from finish(b, 0, X, ssX, X1, UOs[b % 2], T["UO", b])
            for t in range(2):
                i = 2 * b + t
                t1 = dve.put(lambda e, i=i, t=t: e.bn_stats(bn[:, t, :], X1[:, i, :]), T["x1", b, t], T.get(("bn", t)))
                yield
                T["bn", t] = dve.put(lambda e, i=i, t=t: e.bn_aggr(mv2[:, i, :], bn[:, t, :]), t1)
                yield

        def finish(b, half, src, ssx, dst, UO, tu):
            bank, over, gi = yield from grab(G)
            tp = mm(bank[:, 0:256], ident[0:16, b:b + 1].broadcast_to([16, 128]), grow[:, 256 * half:256 * half + 256],
                    True, True, over, T["grow"], mark=True)
            yield
            for t in range(2):
                tz = dve.put(tt(Z[:, t, :], UO[:, t, :], bank[:, 0:256], ALU.mult), tp, tu, T.get(("Zread",)))
                yield
            G.give(gi, tz)
            r0 = 10 + 0
            s = lambda i: sm[:, r0 + i, :]
            for t in range(2):
                ta = act.put(lambda e, t=t: e.activation(JK[:, t, :], UO[:, t, :], ACT.Square,
                                                         accum_out=sm[:, r0, t:t + 1]), tu, T.get(("finsm",)),
                             T.get(("jk",)))
                T["jk",] = ta
                yield
                ta = act.put(lambda e, t=t: e.activation(JK[:, t, :], Z[:, t, :], ACT.Square,
                                                         accum_out=sm[:, r0 + 1, t:t + 1]), tz, T["jk",])
                T["jk",] = ta
                yield
                i = 2 * b + t
                tx = dve.put(lambda e, t=t, i=i, JD=JD: e.tensor_tensor_reduce(out=JD[:, :], in0=src[:, i, :], in1=Z[:, t, :],
                                                                        scale=1.0, scalar=0.0, op0=ALU.mult, op1=ALU.add,
                                                                        accum_out=sm[:, r0 + 2, t:t + 1]), tz, dve_last())
                yield
            T["UOread", b] = ta
            x2 = ssx[:, 2 * b:2 * b + 2]
            nn = sm[:, r0:r0 + 2, :]
            yy = sm[:, r0 + 3:r0 + 5, :]
            aa = sm[:, r0 + 5:r0 + 7, :]
            bb = sm[:, r0 + 7:r0 + 9, :]
            zz = sm[:, r0 + 9:r0 + 11, :]
            so, nz, th, psi = s(11), s(12), s(13), s(14)
            yield from chain(dve, [ts(zz, nn, 1e-30, None, ALU.max)] + rsqrt(zz, yy, aa, bb)
                             + [ts(so, s(3), CL, 1.0, ALU.mult, ALU.min), tt(nz, s(10), s(4), ALU.mult),
                                tt(nz, nz, so, ALU.mult), ts(nz, nz, EPS, None, ALU.max)], ta, tx)
            tw = act.put(lambda e: e.activation(th, nz, ACT.Tanh), dve_last())
            yield
            y2, xy, Aa, den, ca, cb = s(15), s(16), s(17), s(18), s(19), s(20)
            yield from chain(dve, [lambda e: e.reciprocal(psi, nz), tt(psi, psi, so, ALU.mult),
                                   tt(psi, psi, th, ALU.mult), tt(y2, psi, psi, ALU.mult), tt(y2, y2, s(1), ALU.mult),
                                   tt(xy, psi, s(2), ALU.mult), ts(xy, xy, 2.0, 1.0, ALU.mult, ALU.add),
                                   tt(Aa, xy, y2, ALU.add), tt(den, x2, y2, ALU.mult), tt(den, den, xy, ALU.add),
                                   ts(den, den, EPS, None, ALU.max), lambda e: e.reciprocal(cb, den),
                                   tt(ca, Aa, cb, ALU.mult), tt(cb, cb, psi, ALU.mult),
                                   ts(den, x2, -1.0, 1.0, ALU.mult, ALU.add), tt(cb, cb, den, ALU.mult)], tw, dve_last())
            tc = dve_last()
            for t in range(2):
                i = 2 * b + t
                o = dst[:, i, :]
                t1 = dve.put(ts(o, src[:, i, :], sm[:, r0 + 19, t:t + 1], None, ALU.mult), tc)
                yield
                T["x1", b, t] = dve.put(stt(o, Z[:, t, :], sm[:, r0 + 20, t:t + 1], o, ALU.mult, ALU.add), t1)
                yield
            T["Zread",] = T["finsm",] = T["x1", b, 1]

        def s_late():
            yield from need("Q", 0)
            if NN > FIRST:
                yield from stats(FIRST, NN)
            T["prep",] = dve_last()
            yield from need("Q", min(3, nb - 1))
            T["maskb"] = pool.put(lambda e: e.tensor_copy(maskb[:, :], mf), P_("mf"))
            pool.put(lambda e: e.tensor_copy(zselr[:, :].bitcast(F32R), zsel[:, :]), P_("zsel"))
            pool.put(lambda e: e.tensor_scalar(wgkv[:, :, :], wgkv[:, :, :], 0.25, None, ALU.mult), P_("wgkv"))
            yield
            for g in range(2):
                t1 = pool.put(lambda e, g=g: e.tensor_tensor(gtmp[:, g], wat[:, :, 0:256],
                                                             gate[:, g, :].unsqueeze(1).broadcast_to([128, 2, 256]), ALU.mult),
                              P_("wat"), P_(f"gate{g}"))
                for c in range(2):
                    T["wgate"] = dve.put(red(wat[:, c, 896 + 16 * g:912 + 16 * g],
                                             gtmp[:, g, c].rearrange("p (h d) -> p h d", d=16)), t1)
            t1 = dve.put(ts(ysT[:, :, :], condT[:, :, :], 1.0 / 16, None, ALU.mult), P_("cond"))
            yq = lp[:, 8, 0:32].rearrange("p (c b) -> p c b", c=2)
            t2 = dve.put(tt(yq, ysT[:, :, :], ysT[:, :, :], ALU.mult), t1)
            t3 = pool.put(lambda e: e.tensor_tensor(w2sq, w2c[:, :, :], w2c[:, :, :], ALU.mult), P_("w2c"))
            bank, over, gi = yield from grab(G)
            for oc in range(2):
                for c in range(2):
                    t1 = mm(bank[:, 16 * oc:16 * oc + 16], w2sq[:, c, 128 * oc:128 * oc + 128], yq[:, c, :], c == 0, c == 1,
                            over, t2, t3, mark=True)
            T["w2sq"] = t1
            dz, dy, da, db = (lp[:, i, 0:32] for i in (9, 0, 1, 2))
            yield from chain(dve, [ts(dz, bank[:, 0:32], 1e-8, None, ALU.add)], t1, dve_last())
            G.give(gi, dve_last())
            yield from chain(dve, rsqrt(dz, dy, da, db), dve_last())
            T["dT"] = dve.put(lambda e: e.tensor_copy(dT[:, :, :], dy.rearrange("p (c b) -> p c b", c=2)), dve_last())
            t1 = dve.put(lambda e: e.tensor_copy(Bh[:, :].bitcast(F32R), Bf[:, :]), [P_(f"B{r}") for r in range(8)], T["maskb"])
            t2 = dve.put(tt(Bf[:, :], Bf[:, :], Bh[:, :], ALU.subtract), t1)
            t3 = dve.put(ts(Bf[:, :], Bf[:, :], hsel[:, 1:2], None, ALU.mult), t2, P_("hsel"))
            T["Bst"] = dve.put(stt(Bst[:, :].bitcast(F32R), Bh[:, :], hsel[:, 0:1], Bf[:, :], ALU.mult, ALU.add), t3)
            yield
            used = [dve_last(), pool_last(), T["w2sq"]]
            load("WiT", WiT[:, :, :], A["WiT"].rearrange("(c p) n -> p c n", p=128), sp, used)
            load("WoT", WoT[:, :, :], A["WoT"].rearrange("(c p) n -> p c n", p=128), sp, used)
            if nb > 10:
                yield from need("Y", 9)
                yield from prep(0, 20, mv2, ssX1, rX1, dve_last())

        JK2 = sb("JK2", [128, 2, 256])
        JD = XR[1][:, 0, :]
        mv2 = sb("mv2", [128, NT, 2])

        weave(thread(s_norm, "N", None), thread(s_qkv, "Q", "N"), thread(s_heads, "K", "Q"), thread(lambda b: s_att(b, 0), "A0", "K"),
              thread(lambda b: s_att(b, 1), "A1", "K"),
              thread(s_out, "O", "A0"), thread(s_fin, "Y", "O"), s_late())

        HALF = 20 if nb > 10 else 0
        if not HALF:
            for _ in prep(0, NN, mv2, ssX1, rX1, dve_last()):
                pass
        pe_end = pe.put(lambda e: e.matmul(bank[0:2, 100:102], ident[:, 0:2], ident[:, 0:2], start=True, stop=True),
                        dve_last(), [f[0] for f in G.free if f[0]])
        ph2 = [pe_end, dve_last(), act_last(), pool_last()]
        G.free = [(flat([f[0], ph2]), f[1]) for f in G.free]

        fap[0], frp[0], fwp[0] = 0, 0, 0
        QsT = [cut(FR, frp, 8, 256) for _ in range(2)]
        KsT = [cut(FR, frp, 8, 256) for _ in range(2)]
        GQsT = GR[:, 0:1024].rearrange("p (a n) -> p a n", a=4)
        GKsT = GR[:, 1024:1536].rearrange("p (a n) -> p a n", a=4)
        NMT = sb("NMT", [128, 256])
        PT = Ring([cut(FA, fap, 512) for _ in range(8)])
        PT.free = [(ph2, i) for i in range(8)]
        Vg = [cut(FA, fap, 2, 16, 32) for _ in range(2)]
        GV = [cut(FA, fap, 8, 32) for _ in range(2)]
        HLs = [HL[:, v] for v in range(2)]
        OT = cut(FA, fap, 4, 256)
        OTL = cut(FA, fap, 2, 256)
        OO = cut(FA, fap, 2, 256)
        xsT = cut(FA, fap, 2, 256)
        zT = cut(FA, fap, 2, 256)
        h0p = cut(FA, fap, 2, 128)
        UG = cut(FA, fap, 2, 258)
        RL = JK2[:, 0, :].rearrange("p (t n) -> p t n", t=2)
        rT = JK2[:, 1, :]
        xn = SQ[:, 0, 0:512].rearrange("p (t n) -> p t n", t=2)
        mT = SQ[:, 1, 0:512].rearrange("p (t n) -> p t n", t=2)
        R2 = cut(FW, fwp, 4, 512)
        rhoT = cut(FW, fwp, 256)
        h0T = cut(FW, fwp, 2, 256)
        JD = cut(FW, fwp, 256)
        nm = SQ[:, 1, 512:560].rearrange("p (t n) -> p t n", t=2)
        nmhl = hall[:, 0:256].rearrange("p (t r n) -> p t r n", t=2, r=2)
        gt = [hall[:, 256 + 64 * i:320 + 64 * i].rearrange("p (t n) -> p t n", t=2) for i in range(2)]
        RW = SQ[:, 0, 512:768]
        LTW = sb("LTW", [128, 512])
        LT = LTW[:, 0:256]
        LW = LTW[:, 256:512].rearrange("p (t s a d) -> p t s a d", t=2, s=2, a=4)
        MO = [0, 320, 640, 768]

        for v in range(2):
            pool.put(lambda e, m=Vg[v]: e.memset(m, 0.0), ph2)
            a_ = pool.put(lambda e, v=v: e.memset(GV[v], 0.0), ph2)
        pool.put(lambda e: e.memset(h0p, 0.0), ph2)
        pool.put(lambda e: e.memset(nmhl, 0.0), ph2)
        for v in range(2):
            pool.put(lambda e, m=Vg[v]: e.memset(m[:, :, :, 16:17], 1.0), a_)
            pool.put(lambda e, v=v: e.memset(GV[v][:, :, 16:17], 1.0), a_)
        init2 = [ph2, pool_last(), [P_(k) for k in ("wr", "wout", "w2c", "wrt", "bg", "ltm", "wat", "wgkv", "b2")]]
        for k in [k for k in T if isinstance(k, tuple) and k[0] in ("x1", "xnT", "mTread", "sm0", "hlread", "Uread", "Zread",
                                                                   "UOread", "finsm", "scores", "pv", "OTread")]:
            T.pop(k)
        outs = []

        def maskmm(o, off, n, rep, over):
            rhs = maskb[:, off:off + n]
            if rep > 1:
                rhs = rhs.unsqueeze(1).broadcast_to([128, rep, n])
                o = o.rearrange("p (r n) -> p r n", r=rep)
            return mm(o, identb[:, :], rhs, True, False, over, init2)

        def f32r(a):
            return a.bitcast(F32R)

        def b_ffn(b):
            UO = UOs[b % 2]
            if HALF and 2 * b >= HALF:
                while ("prep2",) not in T:
                    yield
            yield from s_mod(b, X, mv2[:, :, 0], rX1, 6, 2, mT, 0, 1, init2, T.get(("prep2",)))
            mb, mgi, tk, tp = T["mbank"]
            for t in range(2):
                bank, over, gi = yield from grab(G)
                for c in range(2):
                    tp = mm(bank[:, 0:258], mT[:, c, 128 * t:128 * t + 128], GG[:, c, :], c == 0, c == 1, over,
                            T["mT", 2, b], mark=c == 1)
                tu = acopy(UG[:, t, :], bank[:, 0:258], tp, T.get(("UGread", b - 1)))
                G.give(gi, tu)
                yield
                tq = dve.put(lambda e, t=t, mb=mb: e.tensor_tensor_reduce(
                    out=JD[:, :], in0=mb[:, 256 * t:256 * t + 256], in1=UG[:, t, 0:256], scale=1.0, scalar=0.0,
                    op0=ALU.mult, op1=ALU.add, accum_out=sm[:, 1, t:t + 1]), tu, tk, dve_last())
                yield
            G.give(mgi, [tk, tq])
            z, y, a, c_, q, k = (sm[:, i, :] for i in (2, 3, 4, 5, 6, 7))
            yield from chain(dve, [ts(z, sm[:, 0, :], EPS * EPS, None, ALU.max)] + rsqrt(z, y, a, c_)
                             + [ts(y, y, CL, 1.0, ALU.mult, ALU.min), tt(q, sm[:, 1, :], y, ALU.mult),
                                stt(q, UG[:, :, 256], 2.0, q, ALU.mult, ALU.add), tt(q, q, y, ALU.mult),
                                ts(q, q, b1w2[:, 256:257], EPS * EPS, ALU.add, ALU.max)]
                             + rsqrt(q, z, a, c_)
                             + [ts(z, z, CL, 1.0, ALU.mult, ALU.min), tt(k, z, y, ALU.mult)], T["mss", 2, b], tq)
            ck = T["sm0", 2, b] = T["UGread", b] = dve_last()
            bank, over, gi = yield from grab(G)
            for t in range(2):
                for c in range(2):
                    tp = mm(bank[:, 256 * t:256 * t + 256], mT[:, c, 128 * t:128 * t + 128], W12[:, c, :], c == 0, c == 1,
                            over, mark=t + c == 2)
            T["mTread", 2, b] = tp
            yield
            yield from need("I", b - 2)
            for t in range(2):
                t1 = dve.put(stt(UO[:, t, :], b1w2[:, 0:256], sm[:, 2, t:t + 1], b2[:, :], ALU.mult, ALU.add), ck,
                             P_("b2"), T.get(("UOread", b - 2)))
                yield
                tu = dve.put(stt(UO[:, t, :], bank[:, 256 * t:256 * t + 256], sm[:, 7, t:t + 1], UO[:, t, :],
                                 ALU.mult, ALU.add), t1, tp)
                yield
            G.give(gi, tu)
            T["UO2", b] = tu

        def b_fin(b):
            yield from finish(b, 1, X, ssX1, X, UOs[b % 2], T["UO2", b])

        hlturn = [0]

        def split(src, n, kind, ready):
            v = hlturn[0] % 2
            hlturn[0] += 1
            hl = HLs[v][:, 0:n]
            hi, lo = hilo(hl, kind)
            sv = src.rearrange("p (h d) -> p h d", d=16).unsqueeze(2).broadcast_to([128, n, 2, 16])
            th = acopy(hi, sv, ready, T.get(("hlread", v)))
            yield
            tl = dve.put(tt(lo, sv, hl[:, :, 0, :].unsqueeze(2).broadcast_to([128, n, 2, 16]), ALU.subtract), th)
            yield
            return hl, v, tl

        def b_proj(b):
            hx = [X[:, 2 * b + t, :] for t in range(2)]
            bank, over, gi = yield from grab(G)
            for t in range(2):
                for c in range(2):
                    tp = tr(bank[:, 256 * c + 128 * t:256 * c + 128 * t + 128], hx[t][:, 128 * c:128 * c + 128], over,
                            T["x1", b, t], mark=t + c == 2)
            te = evac(h0T, bank[:, :].rearrange("p (c n) -> p c n", c=2), tp, T.get(("h0read", b - 1)))
            G.give(gi, te)
            yield
            for t in range(2):
                ba, over, ga = yield from grab(G)
                for c in range(2):
                    tp = mm(ba[:, :], h0T[:, c, 128 * t:128 * t + 128], wat[:, c, 0:512], c == 0, c == 1, over, te,
                            mark=c == 1)
                yield
                tl = None
                yield from need("L0", b - 2)
                yield from need("L1", b - 2)
                for g in range(2):
                    hl, v, tl = yield from split(ba[:, 256 * g:256 * g + 256], 16, g, [tp, tl])
                    if g == 1:
                        G.give(ga, tl)
                    yield from stack(hl, 8, (QsT, KsT)[g][b % 2], t, tl, T.get(("scores", b - 2)))
                    T["hlread", v] = T["stackT"]
            for t in range(2):
                bb, over, gb_ = yield from grab(G)
                for c in range(2):
                    tp = mm(bb[:, 0:416], h0T[:, c, 128 * t:128 * t + 128], wat[:, c, 512:928], c == 0, c == 1, over, te,
                            mark=c == 1)
                yield
                tv = dve.put(lambda e, t=t, bb=bb: e.tensor_copy(Vg[b % 2][:, t, :, 0:16],
                           bb[:, 0:256].rearrange("p (h d) -> p h d", d=16)), tp,
                           T.get(("pv", b - 2)))
                yield
                yield from need("gtread", b - 2)
                tg2 = act.put(lambda e, t=t, bb=bb: e.activation(gt[b % 2][:, t, :], bb[:, 384:416], ACT.Exp, scale=-1.0),
                              tv, T.get(("gtread", b - 2)))
                yield
                hl, v, tl = yield from split(bb[:, 256:384], 8, 0, [tp, tv])
                G.give(gb_, [tl, tg2, tv])
                yield from need("lsc", b - 1)
                yield from stack(hl, 4, GQsT, t, tl, T.get(("lsc", b - 1)))
                T["hlread", v] = T["stackT"]
            for c in range(2):
                tp_ = dve.put(red(h0p[:, c, 0:64], h0T[:, c, :].rearrange("p (n k) -> p n k", k=4)), te, init2,
                              T.get(("h0read", b - 1)))
                yield
            bank, over, gi = yield from grab(G)
            for c in range(2):
                tp = mm(bank[:, 0:256], h0p[:, c, :], wgkv[:, c, :], c == 0, c == 1, over, tp_, mark=c == 1)
            yield
            yield from need("L0", b - 2)
            yield from need("L1", b - 2)
            tg = acopy(GV[b % 2][:, :, 0:16], bank[:, 128:256].rearrange("p (h d) -> p h d", d=16), tp,
                       T.get(("pvl", b - 2)))
            yield
            hl, v, tl = yield from split(bank[:, 0:128], 8, 1, tp)
            G.give(gi, [tl, tg])
            yield from need("lsc", b - 1)
            yield from stack(hl, 4, GKsT, 0, tl, T.get(("lsc", b - 1)))
            T["hlread", v] = T["stackT"]
            T["h0read", b] = tp
            T["proj", b] = [act_last(), dve_last()]
            g_ = gt[b % 2]
            yield from chain(dve, [ts(g_, g_, 1.0, None, ALU.add), lambda e: e.reciprocal(g_, g_)], tg2)
            T["gt", b] = dve_last()

        def sc(o, lk, lsl, rk, rsl, h, start, stop, *after, mark=False):
            r = 64 * (h % 2)
            return mm(o, f32r(lk[r:r + 64, h // 2, lsl]), f32r(rk[r:r + 64, h // 2, rsl]), start, stop, *after, mark=mark)

        def sub(o, h, qs, *after):
            r = 64 * (h % 2)
            return mm(o, f32r(zselr[r:r + 48, h:h + 1]).broadcast_to([48, 128]), f32r(NMT[r:r + 48, qs]), False, False,
                      *after)

        def b_max(b):
            q_, k_ = QsT[b % 2], KsT[b % 2]
            ready = T["proj", b]

            war = T.get(("nmT", b - 1))
            jobs = [("a", 0), ("a", 8)] + [("b", 4 * i) for i in range(4)] + [("l", 0)]
            for kind, h0 in jobs:
                for i in range(2):
                    pb, over, si = yield from grab(G)
                    if kind == "a":
                        maskmm(pb[:, :], MO[0], 128, 4, over)
                        for j in range(4):
                            tp = sc(pb[:, 128 * j:128 * j + 128], q_, slice(0, 128), k_, slice(0, 128), h0 + i + 2 * j,
                                    False, True, ready, mark=j == 3)
                        o, i_ = nm[:, 0, h0 + i:h0 + 8:2], pb[:, :].rearrange("p (h n) -> p h n", h=4)
                    elif kind == "b":
                        maskmm(pb[:, 0:384], MO[0] + 128, 192, 2, over)
                        for j in range(2):
                            tp = sc(pb[:, 192 * j:192 * j + 192], q_, slice(128, 256), k_, slice(64, 256),
                                    h0 + i + 2 * j, False, True, ready, mark=j == 1)
                        o, i_ = nm[:, 1, h0 + i:h0 + 4:2], pb[:, 0:384].rearrange("p (h n) -> p h n", h=2)
                    else:
                        maskmm(pb[:, :], MO[2], 128, 4, over)
                        for j in range(4):
                            for t in range(2):
                                tp = sc(pb[:, 128 * j + 64 * t:128 * j + 64 * t + 64], GQsT,
                                        slice(128 * t, 128 * t + 128), GKsT, slice(0, 64), i + 2 * j, False, True, ready,
                                        mark=j + t == 4)
                        o = nm[:, :, 16 + i:24:2].rearrange("p t h -> p h t")
                        i_ = pb[:, :].rearrange("p (h t n) -> p h t n", h=4, t=2)
                    yield
                    tk = dve.put(red(o, i_, ALU.max, negate=True), tp, T.get(("nmhl", b - 1)))
                    G.give(si, tk)
                    yield
            n2 = nm.unsqueeze(2).broadcast_to([128, 2, 2, 24])
            th = dve.put(lambda e: e.tensor_copy(f32r(nmhl[:, :, :, 0:24]), n2), tk, war, init2)
            yield
            tl = dve.put(tt(f32r(nmhl[:, :, :, 24:48]), n2, nmhl[:, :, :, 0:24], ALU.subtract), th)
            T["nmhl", b] = tl
            yield from need("L0", b - 1)
            yield from need("L1", b - 1)
            bank, over, gi = yield from grab(G)
            for t in range(2):
                tp = tr(bank[:, 128 * t:128 * t + 128], nmhl[:, t].rearrange("p r n -> p (r n)"), over, tl, mark=t == 1)
            T["nmT", b] = tp
            tn = dve.put(lambda e, bank=bank: e.tensor_copy(f32r(NMT[:, :]), bank[:, 0:256]), tp,
                         T.get(("sTdone", b - 1)))
            G.give(gi, tn)
            yield

            T["tn", b] = tn

        def latent_heads(b):
            gv, tn = GV[b % 2], T["tn", b]
            po, oover, oi = yield from grab(G)
            for g in range(2):
                pend = []
                for i in range(2):
                    ps, over, si = yield from grab(G)
                    maskmm(ps[:, :], MO[3], 256, 2, over)
                    for j in range(2):
                        h = 4 * g + i + 2 * j
                        sub(ps[:, 256 * j:256 * j + 256], 16 + h, slice(0, 256), tn)
                        tp = sc(ps[:, 256 * j:256 * j + 256], GKsT, slice(0, 128), GQsT, slice(0, 256), h, False, True,
                                mark=j == 1)
                    yield
                    pt, over, pi = yield from grab(PT)
                    tk = act.put(lambda e, pt=pt, ps=ps: e.activation(pt, ps[:, :], ACT.Exp, scale=0.25), tp, over)
                    G.give(si, tk)
                    pend.append((pt, pi, tk))
                    yield
                if g == 1:
                    T["lsc", b] = tp
                for j in range(4):
                    pt = pend[j % 2][0]
                    tp = mm(po[32 * j:32 * j + 32, 256 * g:256 * g + 256], gv[:, 4 * g + j, :],
                            pt[:, 256 * (j // 2):256 * (j // 2) + 256], True, True, oover, pend[1][2], mark=j == 3)
                for pt, pi, tk in pend:
                    PT.give(pi, tp)
                T["pvl", b] = tp
                yield
            yield from need("OTread", b - 1)
            tk = evac(OTL, po[:, :].rearrange("p (a n) -> p a n", a=2), tp, T.get(("OTread", b - 1)))
            G.give(oi, tk)

        def b_loc(b, half):
            q_, k_, vg, gv, tn = QsT[b % 2], KsT[b % 2], Vg[b % 2], GV[b % 2], T["tn", b]
            if half == 0:
                yield from latent_heads(b)
            pend = []
            for h in range(8 * half, 8 * half + 8):
                ps, over, si = yield from grab(G)
                maskmm(ps[:, 0:320], MO[1], 320, 1, over)
                for o, ks, qs in ((ps[:, 0:192], slice(0, 128), slice(0, 192)),
                                  (ps[:, 192:320], slice(128, 256), slice(128, 256))):
                    sub(o, h, qs, tn)
                    tp = sc(o, k_, ks, q_, qs, h, False, True, mark=ks.start == 128)
                yield
                if h == 8 * half + 7:
                    T["scores", b] = T["sTdone", b] = tp
                pt, over, pi = yield from grab(PT)
                tk = act.put(lambda e, pt=pt, ps=ps: e.activation(pt[:, 0:320], ps[:, 0:320], ACT.Exp, scale=0.25), tp,
                             over)
                G.give(si, tk)
                pend.append((pt, pi, tk))
                yield
                if h % 4 == 3:
                    g = h // 4
                    if g % 2 == 0:
                        po, oover, oi = yield from grab(G)
                    base = 256 * (g % 2)
                    for kt in range(2):
                        for j in range(4):
                            pt = pend[j][0]
                            o = po[32 * j:32 * j + 32, base:base + 192] if kt == 0 else po[32 * j:32 * j + 32, base + 128:base + 256]
                            r = pt[:, 0:192] if kt == 0 else pt[:, 192:320]
                            tp = mm(o, vg[:, kt, 4 * g + j, :], r, kt == 0, kt == 1, oover, pend[3][2],
                                    mark=kt == 1 and j == 3)
                        yield
                    for pt, pi, tk in pend:
                        PT.give(pi, tp)
                    pend = []
                    T["pv", b] = tp
                    if g % 2 == 1:
                        yield from need("OTread", b - 1)
                        tk = evac(OT[:, g - 1:g + 1, :], po[:, :].rearrange("p (a n) -> p a n", a=2), tp,
                                  T.get(("OTread", b - 1)))
                        G.give(oi, tk)
                        yield
            T["OT2", b, half] = [act_last(), dve_last()]
            yield

        def b_mix(b):
            yield from need("L1", b)
            ready = [T["OT2", b, 0], T["OT2", b, 1]]
            xr = XR[b % 2]
            yield from need("E", b - 2)
            sem = ctx.enter_context(nc.semaphore(f"d_xr{b}"))
            T["xr", b] = sp.dma(lambda e: e.dma_start(XR[b % 2][:, :, :], xv[:, 2 * b:2 * b + 2, :]), sem, 16,
                                T.get(("out", b - 2)), ph2)
            gl, gr = gt[b % 2][:, :, 0:16], gt[b % 2][:, :, 16:32]
            for t in range(2):
                bank, over, gi = yield from grab(G)
                for g in range(2):
                    tp = tr(bank[:, 128 * g:128 * g + 128], OTL[:, g, 128 * t:128 * t + 128], over, ready, mark=g == 1)
                bv = bank[:, 0:256].rearrange("p (h n) -> p h n", n=32)
                yield
                tk = dve.put(lambda e, t=t, bv=bv: e.reciprocal(k_a[:, t, 0:8], bv[:, :, 16]), tp)
                yield
                tr_ = dve.put(tt(RL[:, t, :].rearrange("p (h d) -> p h d", d=16), bv[:, :, 0:16], bc(k_a[:, t, 0:8], 16),
                                 ALU.mult), tk, T.get(("RLread",)))
                G.give(gi, tr_)
                yield
                bank, over, gi = yield from grab(G)
                for g in range(4):
                    tp = tr(bank[:, 128 * g:128 * g + 128], OT[:, g, 128 * t:128 * t + 128], over, ready, mark=g == 3)
                bv = bank[:, :].rearrange("p (h n) -> p h n", n=32)
                yield
                tk = dve.put(lambda e, t=t, bv=bv: e.reciprocal(k_b[:, t, :], bv[:, :, 16]), tp)
                yield
                tk = dve.put(tt(k_b[:, t, :], k_b[:, t, :], gl[:, t, :], ALU.mult), tk, T["gt", b])
                yield
                to = dve.put(tt(OO[:, t, :].rearrange("p (h d) -> p h d", d=16), bv[:, :, 0:16], bc(k_b[:, t, :], 16),
                                ALU.mult), tk, T.get(("OOread",)))
                G.give(gi, to)
                yield
            T["OTread", b] = tp
            bank, over, gi = yield from grab(G)
            for t in range(2):
                tp = tr(bank[:, 128 * t:128 * t + 128], RL[:, t, :], over, tr_, mark=t == 1)
            T["RLread",] = tp
            te = evac(rT, bank[:, 0:256], tp, T.get(("rTread",)))
            G.give(gi, te)
            yield
            bank, over, gi = yield from grab(G)
            for t in range(2):
                tp = mm(bank[:, 256 * t:256 * t + 256], rT[:, 128 * t:128 * t + 128], wr[:, :], True, True, over, te,
                        mark=t == 1)
            T["rTread",] = tp
            yield
            for t in range(2):
                bv = bank[:, 256 * t:256 * t + 256].rearrange("p (h d) -> p h d", d=16)
                t1 = dve.put(tt(JK2[:, t, :].rearrange("p (h d) -> p h d", d=16), bv, bc(gr[:, t, :], 16), ALU.mult), tp)
                yield
                to = dve.put(tt(OO[:, t, :], OO[:, t, :], JK2[:, t, :], ALU.add), t1)
                yield
            T["gtread", b] = T["RLread",] = T["rTread",] = to
            G.give(gi, to)
            bank, over, gi = yield from grab(G)
            for t in range(2):
                for c in range(2):
                    tp = tr(bank[:, 256 * c + 128 * t:256 * c + 128 * t + 128], OO[:, t, 128 * c:128 * c + 128], over, to,
                            mark=t + c == 2)
            te = evac(OO, bank[:, :].rearrange("p (c n) -> p c n", c=2), tp, to)
            G.give(gi, te)
            yield
            bank, over, gi = yield from grab(G)
            for t in range(2):
                for c in range(2):
                    tp = mm(bank[:, 256 * t:256 * t + 256], OO[:, c, 128 * t:128 * t + 128], wout[:, c, :], c == 0,
                            c == 1, over, te, mark=t + c == 2)
            T["OOread",] = tp
            yield
            tx = dve.put(tt(xr[:, :, :], xr[:, :, :], bank[:, :].rearrange("p (t n) -> p t n", t=2), ALU.add), tp,
                         T["xr", b])
            G.give(gi, tx)
            T["tx", b] = tx
            yield

        def b_moe(b):
            xr, tx, tp = XR[b % 2], T["tx", b], T.get(("xsread",))
            bank, over, gi = yield from grab(G)
            for t in range(2):
                for c in range(2):
                    tq = tr(bank[:, 256 * c + 128 * t:256 * c + 128 * t + 128], xr[:, t, 128 * c:128 * c + 128], over, tx,
                            mark=t + c == 2)
            yield
            for c in range(2):
                te = act.put(lambda e, c=c, bank=bank: e.activation(xsT[:, c, :], bank[:, 256 * c:256 * c + 256], ACT.Copy,
                                                                    scale=ysT[:, c, b:b + 1]), tq, tp)
                yield
            G.give(gi, te)
            bank, over, gi = yield from grab(G)
            for oc in range(2):
                for c in range(2):
                    tp = mm(bank[:, 256 * oc:256 * oc + 256], w2c[:, c, 128 * oc:128 * oc + 128], xsT[:, c, :], c == 0,
                            c == 1, over, te, mark=oc + c == 2)
            T["xsread",] = tp
            yield
            for oc in range(2):
                te = act.put(lambda e, oc=oc, bank=bank: e.activation(zT[:, oc, :], bank[:, 256 * oc:256 * oc + 256],
                                                                      ACT.Copy, scale=dT[:, oc, b:b + 1]), tp,
                             T.get(("zread",)))
                yield
            G.give(gi, te)
            bank, over, gi = yield from grab(G)
            for t in range(2):
                for c in range(2):
                    tp = mm(bank[:, 20 * t:20 * t + 20], zT[:, c, 128 * t:128 * t + 128], wrt[:, c, :], c == 0, c == 1,
                            over, te, mark=t + c == 2)
            yield
            rv = bank[:, 0:40].rearrange("p (t n) -> p t n", t=2)

            def w(i, *shape):
                a = RW[:, i:i + int(np.prod(shape))]
                if len(shape) == 1:
                    return a
                names = "abc"[:len(shape)]
                return a.rearrange(f"p ({' '.join(names)}) -> p {' '.join(names)}",
                                   **{names[i]: shape[i] for i in range(1, len(shape))})

            lg, mx, pr, cm, eq = w(0, 2, 4), w(8, 2), w(10, 2, 4), w(18, 2, 4, 4), w(50, 2, 4, 4)
            rk, oh, w12, lf = w(82, 2, 4), w(90, 2, 2, 4), w(106, 2, 2), w(110, 2, 2, 16)
            rho, sm_, tmp = w(174, 2), w(176, 2), w(178, 2, 2, 4)
            yield from chain(dve, [tt(lg, rv[:, :, 0:4], bg[:, :].unsqueeze(1).broadcast_to([128, 2, 4]), ALU.add),
                                   red(mx, lg, ALU.max, negate=True), tt(lg, lg, bc(mx, 4), ALU.add)], tp,
                             T.get(("rwread",)))
            ta = act.put(lambda e: e.activation(pr, lg, ACT.Exp), dve_last())
            yield
            pj = pr.unsqueeze(2).broadcast_to([128, 2, 4, 4])
            lt4 = ltm[:, :].rearrange("p (i j) -> p i j", j=4)
            fns = [red(sm_, pr), lambda e: e.reciprocal(sm_, sm_), tt(pr, pr, bc(sm_, 4), ALU.mult),
                   tt(cm, pj, bc(pr, 4), ALU.is_gt), tt(eq, pj, bc(pr, 4), ALU.is_equal)]
            fns += [tt(eq[:, t], eq[:, t], lt4, ALU.mult) for t in range(2)]
            fns += [tt(cm, cm, eq, ALU.add), red(rk, cm), ts(oh[:, :, 0, :], rk, 0.0, None, ALU.is_equal),
                    ts(oh[:, :, 1, :], rk, 1.0, None, ALU.is_equal),
                    tt(tmp, oh, pr.unsqueeze(2).broadcast_to([128, 2, 2, 4]), ALU.mult), red(w12, tmp),
                    lambda e: e.reciprocal(rho, w12[:, :, 0]), tt(rho, rho, w12[:, :, 1], ALU.mult),
                    tt(oh[:, :, 0, :], oh[:, :, 0, :], oh[:, :, 1, :], ALU.subtract)]
            lw4 = lf.rearrange("p t s (e r) -> p t s e r", r=4)
            lo4 = rv[:, :, 4:20].rearrange("p t (e r) -> p t e r", r=4)
            for t in range(2):
                fns += [tt(lw4[:, t, s_], lo4[:, t], bc(oh[:, t, 1 - s_, :], 4), ALU.mult) for s_ in range(2)]
            yield from chain(dve, fns, ta)
            G.give(gi, dve_last())
            hi, lo = LW[:, :, :, 0:2, :].rearrange("p t s a d -> p (t s) a d"), \
                LW[:, :, :, 2:4, :].rearrange("p t s a d -> p (t s) a d")
            lfb = lf.rearrange("p t s d -> p (t s) d").unsqueeze(2).broadcast_to([128, 4, 2, 16])
            yield from chain(dve, [lambda e: e.tensor_copy(f32r(hi), lfb), tt(f32r(lo), lfb, hi, ALU.subtract)],
                             dve_last(), T.get(("LWread",)))
            tl = dve_last()
            bank, over, gi = yield from grab(G)
            for t in range(2):
                tp = mm(bank[:, 128 * t:128 * t + 128], f32r(LW[:, t].rearrange("p s a d -> p (s a d)")),
                        f32r(identr[:, :]), True, True, over, tl, mark=True)
                tr_ = mm(bank[:, 256 + 128 * t:384 + 128 * t], rho[:, t:t + 1].broadcast_to([128, 128]), ident[:, :],
                         True, True, mark=t == 1)
            T["LWread",] = tp
            yield
            te = acopy(f32r(LT[:, :]), bank[:, 0:256], [tp, tr_], T.get(("LTread",)))
            yield
            tb = acopy(rhoT[:, :], bank[:, 256:512], tr_, T.get(("LTread",)))
            G.give(gi, tb)
            yield
            for hf in range(4):
                R = R2[:, hf, :]
                ps, over, si = yield from grab(G)
                for j in range(2):
                    f0 = 256 * hf + 128 * j
                    o = ps[:, 256 * j:256 * j + 256]
                    for c in range(2):
                        mm(o, WiT[:, c, f0:f0 + 128], zT[:, c, :], c == 0 and j == 0, False, over, P_("WiT"))
                    tp = mm(o, f32r(Bst[0:64, f0:f0 + 128]), f32r(LT[0:64, :]), False, True, te, mark=j == 1)
                yield
                ta = act.put(lambda e, R=R, ps=ps: e.activation(R, ps[:, :], ACT.Relu), tp, T.get(("Hread", hf)))
                yield
                for j in range(2):
                    f0 = 256 * hf + 128 * j
                    tp = mm(ps[:, 256 * j:256 * j + 256], f32r(Bst[64:128, f0:f0 + 128]), f32r(LT[64:128, :]), False,
                            True, ta, mark=j == 1)
                yield
                R4 = R.rearrange("p (j n) -> p j n", j=2)
                t2 = pool.put(tt(R4, R4, rhoT[:, :].unsqueeze(1).broadcast_to([128, 2, 256]), ALU.mult), ta, tb)
                yield
                th = dve.put(stt(R, ps[:, :], 0.0, R, ALU.max, ALU.add), tp, t2)
                G.give(si, th)
                yield
                T["th", hf] = th
            T["LTread",] = th
            ob, oover, og = yield from grab(G)
            for hf in range(4):
                for t in range(2):
                    for j in range(2):
                        tp = mm(ob[:, 256 * t:256 * t + 256], R2[:, hf, 256 * j + 128 * t:256 * j + 128 * t + 128],
                                WoT[:, 2 * hf + j, :], hf + j + t == 0, hf == 3 and j == 1, oover, T["th", hf],
                                P_("WoT"), mark=j == 1)
                yield
                T["Hread", hf] = tp
            for t in range(2):
                tx = dve.put(stt(xr[:, t, :], ob[:, 256 * t:256 * t + 256], w12[:, t, 0:1], xr[:, t, :], ALU.mult, ALU.add),
                             tp, tx, tq)
                yield
            G.give(og, tx)
            T["zread",] = tp
            T["rwread",] = tx
            sem = ctx.enter_context(nc.semaphore(f"d_out{b}"))
            T["out", b] = sp.dma(lambda e, xr=xr: e.dma_start(
                out[b].rearrange("(t p) d -> p t d", p=128), xr[:, :, :]), sem, 16, tx)
            outs.append(T["out", b])
            yield

        def b_prep():
            yield from need("F", 1)
            if HALF:
                yield from prep(HALF, NN, mv2, ssX1, rX1, ph2, dve_last())
            T["prep2",] = dve_last()

        weave(thread(b_ffn, "F", None, ("P", 4)), thread(b_fin, "I", "F"), thread(b_proj, "P", "I"), thread(b_max, "M", "P"), thread(lambda b: b_loc(b, 0), "L0", "M"),
              thread(lambda b: b_loc(b, 1), "L1", "M"),
              thread(b_mix, "X", "L0"), thread(b_moe, "E", "X"), b_prep())
        sp.ops.append((lambda e: e.nop(), flat(outs), None))
        run_lanes(nc, ctx, (pe, act, dve, pool, sp))


def run_lanes(nc, ctx, lanes):
    pe, act, dve, pool, sp = lanes
    block = ctx.enter_context(nc.Block())

    @block.tensor
    def _(e):
        pe.play(e)

    @block.scalar
    def _(e):
        act.play(e)

    @block.vector
    def _(e):
        dve.play(e)

    @block.gpsimd
    def _(e):
        pool.play(e)

    @block.sync
    def _(e):
        sp.play(e)


def _inputs(inp):
    f = lambda k: np.asarray(inp[k])
    T_ = lambda a: np.ascontiguousarray(a.T)
    cat = lambda *a: np.ascontiguousarray(np.concatenate(a, axis=-1))
    q = np.arange(128)
    neg = np.float32(-1e30)

    def allow(m):
        return np.where(m, np.float32(0), neg).astype(np.float32)

    k0 = np.arange(128)
    m_t0 = allow((k0[None] <= q[:, None]) & (k0[None] > q[:, None] - 64))
    k1 = 64 + np.arange(192)
    m_t1 = allow((k1[None] <= 128 + q[:, None]) & (k1[None] > 128 + q[:, None] - 64))
    qa = np.arange(192)
    m_k0 = allow((qa[None] >= q[:, None]) & (qa[None] < q[:, None] + 64))
    qb = np.arange(128)
    m_k1 = allow((qb[None] >= q[:, None]) & (qb[None] < q[:, None] + 64))
    lat = np.arange(64)
    m_l = [allow(lat[None] <= (128 * t + q[:, None]) // 4) for t in range(2)]
    ql = np.arange(256)
    m_lt = allow((q[:, None] <= ql[None] // 4) & (q[:, None] < 64))
    masks = cat(m_t0, m_t1, m_k0, m_k1, m_l[0], m_l[1], m_lt)
    zsel = np.zeros((128, 24), np.float32)
    for r in (0, 24, 64, 88):
        zsel[r + np.arange(24), np.arange(24)] = 1
    hs = np.zeros((128, 2), np.float32)
    hs[:, 0] = (np.arange(128) // 16) % 2 == 0
    hs[:, 1] = 1 - hs[:, 0]
    ltm = np.array([[1.0 if j < i else 0.0 for j in range(4)] for i in range(4)], np.float32).reshape(16)
    c = "L0_cond_"
    a = "L0_attn_"
    w = "L0_ffn_"
    return {
        "x": f("x"), "condT": T_(f("cond_1024")), "ident": np.eye(128, dtype=np.float32), "masks": masks,
        "zsel": zsel, "hsel": hs, "ltm": ltm,
        "w_ada": f(c + "w_ada"), "b_ada": f(c + "b_ada"), "badaT": T_(f(c + "b_ada").reshape(12, 128)),
        "wqkv": cat(f(c + "w_q"), f(c + "w_k"), f(c + "w_v")), "bqkv": cat(f(c + "b_q"), f(c + "b_k"), f(c + "b_v")),
        "w_o": f(c + "w_o"), "b_o": f(c + "b_o"), "w1T": T_(f(c + "w_f1")), "b1c": T_(f(c + "b_f1").reshape(8, 128)),
        "w2": f(c + "w_f2"), "b_f2": f(c + "b_f2"),
        "wat": cat(f(a + "wq"), f(a + "wk"), f(a + "wv"), f(a + "wgq")), "wgkv": cat(f(a + "wgk"), f(a + "wgv")),
        "gl": f(a + "gate_local_w").reshape(256), "gr": f(a + "gate_remote_w").reshape(256),
        "r_out_w": f(a + "r_out_w"), "w_out": f(a + "w_out"), "weight": f("L0_cond2_weight"),
        "wrt": cat(T_(f(w + "Wg")), T_(f(w + "A").reshape(16, 256))), "bg": f(w + "bg"),
        "WiT": T_(f(w + "Wi")), "WoT": T_(f(w + "Wo")),
        "Bc": np.ascontiguousarray(np.transpose(f(w + "B"), (0, 2, 1)).reshape(16, 1024)),
    }


_OUT = (NB, S, D)


def kernel(**inputs):
    import concourse.bacc as _bacc
    from concourse.bass_utils import run_bass_kernel_spmd as _run

    nc = _bacc.Bacc("TRN2", target_bir_lowering=False, num_devices=1)
    arrays, args = {}, {}
    for name, a in _inputs(inputs).items():
        arrays[f"in_{name}"] = a
        args[name] = nc.dram_tensor(f"in_{name}", a.shape, F32, kind="ExternalInput").ap()
    o = nc.dram_tensor("out_0", _OUT, F32, kind="ExternalOutput").ap()
    program(nc, args, o)
    r = _run(nc, [arrays], core_ids=[0])
    return r.results[0]["out_0"]
```
